# Optimizing a Trainium2 kernel written in Bass

```python
import numpy as np
import jax
import jax.numpy as jnp

def _softmax(x, axis=-1):
    return jax.nn.softmax(x, axis=axis)

def _gelu(x):
    return jax.nn.gelu(x, approximate=True)

def _silu(x):
    return jax.nn.silu(x)

def _sigmoid(x):
    return jax.nn.sigmoid(x)

def _layernorm(x, axis=-1, eps=1e-05):
    m = jnp.mean(x, axis=axis, keepdims=True)
    v = jnp.var(x, axis=axis, keepdims=True)
    return (x - m) / jnp.sqrt(v + eps)

def _scatter_add(tgt, idx, src, axis=0):
    return tgt.at[idx].add(src)

def _segment_sum(src, seg, n):
    return jax.ops.segment_sum(src, seg, n)
kernel_name = 'mk_decoder_postln_d4_seqx_r8_efa6a5'

def setup_inputs(seed: int=0):
    np.random.seed(seed)
    _w = jnp.asarray

    def _rec_inputs():
        import jax
        import jax.numpy as jnp
        _rk = jax.random.key(seed)
        x = -0.0002928 + 1 * jax.random.normal(jax.random.fold_in(_rk, 1), (8, 256, 128), jnp.float32)
        _lenS = 256 - jax.random.randint(jax.random.fold_in(_rk, 7), (8,), 0, max(1, 256 // 4) + 1, jnp.int32)
        _lenS2 = 64 - jax.random.randint(jax.random.fold_in(_rk, 8), (8,), 0, max(1, 64 // 4) + 1, jnp.int32)
        _ctx_1024P = jax.random.normal(jax.random.fold_in(_rk, 11), (8, 16, 128), jnp.float32)
        _ctx_1024c = jax.random.dirichlet(jax.random.fold_in(_rk, 511), 0.3 * jnp.ones((16,), jnp.float32), (8, 64))
        _ctx_1024t = jnp.einsum('bsk,bkd->bsd', _ctx_1024c, _ctx_1024P)
        _ctx_1024t = _ctx_1024t * jax.lax.rsqrt(jnp.mean(jnp.square(_ctx_1024t)) + 1e-12) * 0.953939
        ctx_1024 = 4.13588e-05 + 0.999923 * (_ctx_1024t + 0.3 * jax.random.normal(jax.random.fold_in(_rk, 611), (8, 64, 128), jnp.float32))
        _validS = jnp.arange(256)[None, :] < _lenS[:, None]
        _validS2 = jnp.arange(64)[None, :] < _lenS2[:, None]
        _causal = jnp.tril(jnp.ones((256, 256), dtype=bool))
        mask_BxS2_ik0 = jnp.where(jnp.broadcast_to(_validS2[:, :], (8, 64)), 0, 1).astype(jnp.int32)
        mask_BxS2_bf1 = jnp.ones((8, 64), dtype=bool)
        return (x, ctx_1024, mask_BxS2_ik0, mask_BxS2_bf1)
    x, ctx_1024, mask_BxS2_ik0, mask_BxS2_bf1 = _rec_inputs()

    def _L0_attn_setup():
        import jax, jax.numpy as jnp
        import numpy as np
        B, S, D, H = (2, 256, 128, 8)
        DH = D // H
        EPS = 1e-06

        def _retention(X, Wq, Wk, Wv):
            b, s, d = X.shape
            gammas = 1.0 - jnp.exp2(-5.0 - jnp.arange(H, dtype=jnp.float32))
            q = (X @ Wq).reshape(b, s, H, DH).transpose(0, 2, 1, 3)
            k = (X @ Wk).reshape(b, s, H, DH).transpose(0, 2, 1, 3)
            v = (X @ Wv).reshape(b, s, H, DH).transpose(0, 2, 1, 3)
            scores = jnp.einsum('bhnd,bhmd->bhnm', q, k) / np.sqrt(DH)
            idx = jnp.arange(s, dtype=jnp.float32)
            diff = idx[:, None] - idx[None, :]
            log_g = jnp.log(gammas)[:, None, None]
            decay = jnp.where(diff >= 0, jnp.exp(log_g * diff), 0.0)
            ret = jnp.einsum('bhnm,bhmd->bhnd', scores * decay[None], v)
            mean = ret.mean(axis=-1, keepdims=True)
            var = ret.var(axis=-1, keepdims=True)
            ret = (ret - mean) * jax.lax.rsqrt(var + EPS)
            return ret.transpose(0, 2, 1, 3).reshape(b, s, d)
        key = jax.random.key(seed)
        ks = jax.random.split(key, 6)
        scale = 1.0 / np.sqrt(D)
        return {'X': jax.random.normal(ks[0], (B, S, D), jnp.float32), 'Wq': jax.random.normal(ks[1], (D, D), jnp.float32) * scale, 'Wk': jax.random.normal(ks[2], (D, D), jnp.float32) * scale, 'Wv': jax.random.normal(ks[3], (D, D), jnp.float32) * scale, 'W_G': jax.random.normal(ks[4], (D, D), jnp.float32) * scale, 'W_O': jax.random.normal(ks[5], (D, D), jnp.float32) * scale}
    _L0_attn_all = _L0_attn_setup()
    _L0_attn_in = {k: v for k, v in _L0_attn_all.items() if k in ('Wq', 'Wk', 'Wv', 'W_G', 'W_O')}
    del _L0_attn_all

    def _L0_xattn_setup():
        import jax, jax.numpy as jnp
        import numpy as np
        import math
        D_MODEL = 128
        N_HEADS = 16
        D_K = D_MODEL // N_HEADS
        key = jax.random.key(seed)
        ks = jax.random.split(key, 12)
        B, SQ, SK = (4, 128, 256)
        s = 1.0 / math.sqrt(D_MODEL)
        inp = {'query': jax.random.normal(ks[0], (B, SQ, D_MODEL), jnp.float32), 'key_value': jax.random.normal(ks[1], (B, SK, D_MODEL), jnp.float32), 'mask': jax.random.randint(ks[2], (B, SK), 0, 2, jnp.int32), 'Wq': jax.random.normal(ks[3], (D_MODEL, D_MODEL), jnp.float32) * s, 'bq': jnp.zeros((D_MODEL,), jnp.float32), 'Wk': jax.random.normal(ks[4], (D_MODEL, D_MODEL), jnp.float32) * s, 'bk': jnp.zeros((D_MODEL,), jnp.float32), 'Wv': jax.random.normal(ks[5], (D_MODEL, D_MODEL), jnp.float32) * s, 'bv': jnp.zeros((D_MODEL,), jnp.float32), 'Wo': jax.random.normal(ks[6], (D_MODEL, D_MODEL), jnp.float32) * s, 'bo': jnp.zeros((D_MODEL,), jnp.float32)}
        return inp
    _L0_xattn_all = _L0_xattn_setup()
    _L0_xattn_in = {k: v for k, v in _L0_xattn_all.items() if k in ('Wq', 'bq', 'Wk', 'bk', 'Wv', 'bv', 'Wo', 'bo')}
    del _L0_xattn_all

    def _L0_ffn_setup():
        import jax, jax.numpy as jnp
        import numpy as np
        TOP_K = 2

        def _moe(x, Wr, br, W1, b1, W2, b2):
            B, S, D = x.shape
            E = Wr.shape[1]
            xt = x.reshape(-1, D)
            logits = xt @ Wr + br
            top_vals, top_idx = jax.lax.top_k(logits, TOP_K)
            mask = jnp.zeros_like(logits, dtype=bool).at[jnp.arange(xt.shape[0])[:, None], top_idx].set(True)
            sparse_logits = jnp.where(mask, logits, -jnp.inf)
            gate = jax.nn.softmax(sparse_logits, axis=-1)
            h = jax.nn.relu(jnp.einsum('td,edh->teh', xt, W1) + b1)
            y = jnp.einsum('teh,ehd->ted', h, W2) + b2
            out = jnp.einsum('ted,te->td', y, gate)
            return out.reshape(B, S, D)
        key = jax.random.key(seed)
        ks = jax.random.split(key, 5)
        B, S, D, E, H = (2, 256, 128, 8, 512)
        scale = 1.0 / np.sqrt(D)
        return {'x': jax.random.normal(ks[0], (B, S, D), dtype=jnp.float32), 'Wr': jax.random.normal(ks[1], (D, E), dtype=jnp.float32) * scale, 'br': jnp.zeros((E,), dtype=jnp.float32), 'W1': jax.random.normal(ks[2], (E, D, H), dtype=jnp.float32) * scale, 'b1': jnp.zeros((E, H), dtype=jnp.float32), 'W2': jax.random.normal(ks[3], (E, H, D), dtype=jnp.float32) * (1.0 / np.sqrt(H)), 'b2': jnp.zeros((E, D), dtype=jnp.float32)}
    _L0_ffn_all = _L0_ffn_setup()
    _L0_ffn_in = {k: v for k, v in _L0_ffn_all.items() if k in ('Wr', 'br', 'W1', 'b1', 'W2', 'b2')}
    del _L0_ffn_all

    def _L1_attn_setup():
        import jax, jax.numpy as jnp
        import numpy as np
        B, S, D, H = (4, 256, 128, 512)
        EPS = 1e-12

        def _linear(x, W, b):
            return x @ W.T + b
        key = jax.random.key(seed)
        ks = jax.random.split(key, 14)
        s = lambda d: 1.0 / np.sqrt(d)
        return {'x': jax.random.normal(ks[0], (B, S, D), dtype=jnp.float32), 'Wq': jax.random.normal(ks[1], (D, D), dtype=jnp.float32) * s(D), 'bq': jax.random.normal(ks[2], (D,), dtype=jnp.float32) * 0.01, 'Wk': jax.random.normal(ks[3], (D, D), dtype=jnp.float32) * s(D), 'bk': jax.random.normal(ks[4], (D,), dtype=jnp.float32) * 0.01, 'Wv': jax.random.normal(ks[5], (D, D), dtype=jnp.float32) * s(D), 'bv': jax.random.normal(ks[6], (D,), dtype=jnp.float32) * 0.01, 'W1': jax.random.normal(ks[7], (D, D), dtype=jnp.float32) * s(D), 'b1': jax.random.normal(ks[8], (D,), dtype=jnp.float32) * 0.01, 'W2': jax.random.normal(ks[9], (H, D), dtype=jnp.float32) * s(D), 'b2': jax.random.normal(ks[10], (H,), dtype=jnp.float32) * 0.01, 'W3': jax.random.normal(ks[11], (D, H), dtype=jnp.float32) * s(H), 'b3': jax.random.normal(ks[12], (D,), dtype=jnp.float32) * 0.01}
    _L1_attn_all = _L1_attn_setup()
    _L1_attn_in = {k: v for k, v in _L1_attn_all.items() if k in ('Wq', 'bq', 'Wk', 'bk', 'Wv', 'bv', 'W1', 'b1', 'W2', 'b2', 'W3', 'b3')}
    del _L1_attn_all

    def _L1_xattn_setup():
        import jax, jax.numpy as jnp
        import numpy as np
        from math import sqrt
        QUERY_DIM = 128
        KEY_DIM = 128
        VALUE_DIM = 128
        key = jax.random.key(seed)
        k1, k2, k3, k4 = jax.random.split(key, 4)
        B, Q, S = (8, 256, 256)
        query = jax.random.normal(k1, (B, Q, QUERY_DIM), dtype=jnp.float32)
        inputs = jax.random.normal(k2, (B, S, KEY_DIM), dtype=jnp.float32)
        std_k = sqrt(2.0 / (KEY_DIM + QUERY_DIM))
        std_v = sqrt(2.0 / (KEY_DIM + VALUE_DIM))
        key_matrix = jax.random.normal(k3, (KEY_DIM, QUERY_DIM), dtype=jnp.float32) * std_k
        value_matrix = jax.random.normal(k4, (KEY_DIM, VALUE_DIM), dtype=jnp.float32) * std_v
        return {'query': query, 'inputs': inputs, 'key_matrix': key_matrix, 'value_matrix': value_matrix}
    _L1_xattn_all = _L1_xattn_setup()
    _L1_xattn_in = {k: v for k, v in _L1_xattn_all.items() if k in ('key_matrix', 'value_matrix')}
    del _L1_xattn_all

    def _L1_ffn_setup():
        import jax, jax.numpy as jnp
        import numpy as np
        B, S, D, H, E = (4, 256, 128, 256, 8)
        key = jax.random.key(seed)
        ks = jax.random.split(key, 8)
        scale = 0.02
        return {'x': jax.random.normal(ks[0], (B, S, D), dtype=jnp.float32), 'Wr': jax.random.normal(ks[1], (D, E), dtype=jnp.float32) * scale, 'br': jnp.zeros((E,), dtype=jnp.float32), 'W1': jax.random.normal(ks[2], (E, D, H), dtype=jnp.float32) * scale, 'b1': jnp.zeros((E, H), dtype=jnp.float32), 'W2': jax.random.normal(ks[3], (E, H, D), dtype=jnp.float32) * scale, 'b2': jnp.zeros((E, D), dtype=jnp.float32)}
    _L1_ffn_all = _L1_ffn_setup()
    _L1_ffn_in = {k: v for k, v in _L1_ffn_all.items() if k in ('Wr', 'br', 'W1', 'b1', 'W2', 'b2')}
    del _L1_ffn_all

    def _L2_attn_setup():
        import jax, jax.numpy as jnp
        import numpy as np
        HIDDEN = 128
        BETA = 1.0
        SPARSITY_THRESHOLD = 1.0

        def _sparsemax(x):
            n = x.shape[-1]
            z = x - jnp.max(x, axis=-1, keepdims=True)
            sum_z = jnp.sum(z, axis=-1, keepdims=True)
            step = (sum_z - 1.0) / n
            sorted_z = -jnp.sort(-z, axis=-1)
            cumsum_z = jnp.cumsum(sorted_z, axis=-1)
            is_gt = sorted_z > step
            rng = jnp.arange(1, n + 1, dtype=jnp.int32)
            k = jnp.max(rng * is_gt, axis=-1, keepdims=True).astype(x.dtype)
            tau = (cumsum_z - 1.0 - step * k) / k
            return jnp.clip(z - tau, 0.0)
        key = jax.random.key(seed)
        kx, kq, kk, kv = jax.random.split(key, 4)
        B, S, D = (4, 256, 128)
        x = jax.random.normal(kx, (B, S, D), dtype=jnp.float32)
        scale = 1.0 / np.sqrt(D)
        Wq = jax.random.normal(kq, (HIDDEN, D), dtype=jnp.float32) * scale
        Wk = jax.random.normal(kk, (HIDDEN, D), dtype=jnp.float32) * scale
        Wv = jax.random.normal(kv, (HIDDEN, D), dtype=jnp.float32) * scale
        return {'x': x, 'Wq': Wq, 'Wk': Wk, 'Wv': Wv}
    _L2_attn_all = _L2_attn_setup()
    _L2_attn_in = {k: v for k, v in _L2_attn_all.items() if k in ('Wq', 'Wk', 'Wv')}
    del _L2_attn_all

    def _L2_xattn_setup():
        import jax, jax.numpy as jnp
        import numpy as np
        D_MODEL = 128
        NUM_HEADS = 16
        HEAD_DIM = D_MODEL // NUM_HEADS
        key = jax.random.key(seed)
        ks = jax.random.split(key, 10)
        B, SQ, SK = (2, 256, 256)
        scale = 1.0 / np.sqrt(D_MODEL)
        inp = {'x1': jax.random.normal(ks[0], (B, SQ, D_MODEL), jnp.float32), 'x2': jax.random.normal(ks[1], (B, SK, D_MODEL), jnp.float32), 'Wq': jax.random.normal(ks[2], (D_MODEL, D_MODEL), jnp.float32) * scale, 'bq': jnp.zeros((D_MODEL,), jnp.float32), 'Wk': jax.random.normal(ks[3], (D_MODEL, D_MODEL), jnp.float32) * scale, 'bk': jnp.zeros((D_MODEL,), jnp.float32), 'Wv': jax.random.normal(ks[4], (D_MODEL, D_MODEL), jnp.float32) * scale, 'bv': jnp.zeros((D_MODEL,), jnp.float32), 'Wo': jax.random.normal(ks[5], (D_MODEL, D_MODEL), jnp.float32) * scale, 'bo': jnp.zeros((D_MODEL,), jnp.float32)}
        return inp
    _L2_xattn_all = _L2_xattn_setup()
    _L2_xattn_in = {k: v for k, v in _L2_xattn_all.items() if k in ('Wq', 'bq', 'Wk', 'bk', 'Wv', 'bv', 'Wo', 'bo')}
    del _L2_xattn_all

    def _L2_ffn_setup():
        import jax, jax.numpy as jnp
        import numpy as np
        D_MODEL = 128
        D_OUT = 128
        RANK = 16
        NUM_TRUE = 8
        NUM_NULL = 2
        TOP_K = 2
        SCALING = 32.0 / 16.0
        key = jax.random.key(seed)
        ks = jax.random.split(key, 6)
        x = jax.random.normal(ks[0], (4, 512, D_MODEL), dtype=jnp.float32)
        base_w = jax.random.normal(ks[1], (D_OUT, D_MODEL), dtype=jnp.float32) / np.sqrt(D_MODEL)
        base_b = jax.random.normal(ks[2], (D_OUT,), dtype=jnp.float32) * 0.01
        gate_w = jax.random.normal(ks[3], (NUM_TRUE + NUM_NULL, D_MODEL), dtype=jnp.float32) / np.sqrt(D_MODEL)
        lora_A = jax.random.normal(ks[4], (NUM_TRUE, RANK, D_MODEL), dtype=jnp.float32) / np.sqrt(D_MODEL)
        lora_B = jax.random.normal(ks[5], (NUM_TRUE, D_OUT, RANK), dtype=jnp.float32) * 0.01
        return {'x': x, 'base_w': base_w, 'base_b': base_b, 'gate_w': gate_w, 'lora_A': lora_A, 'lora_B': lora_B}
    _L2_ffn_all = _L2_ffn_setup()
    _L2_ffn_in = {k: v for k, v in _L2_ffn_all.items() if k in ('base_w', 'base_b', 'gate_w', 'lora_A', 'lora_B')}
    del _L2_ffn_all

    def _L3_attn_setup():
        import jax, jax.numpy as jnp
        import numpy as np
        HEADS = 32
        DIM_HEAD = 32
        EPS = 1e-06
        key = jax.random.key(seed)
        k1, k2, k3 = jax.random.split(key, 3)
        b, n, dim = (2, 256, 128)
        x = jax.random.normal(k1, (b, n, dim), dtype=jnp.float32)
        w_qkv = jax.random.normal(k2, (dim, 3 * HEADS * DIM_HEAD), dtype=jnp.float32) * dim ** (-0.5)
        w_out = jax.random.normal(k3, (HEADS * DIM_HEAD, dim), dtype=jnp.float32) * dim ** (-0.5)
        b_out = jnp.zeros((dim,), dtype=jnp.float32)
        ln_gamma = jnp.ones((dim,), dtype=jnp.float32)
        ln_beta = jnp.zeros((dim,), dtype=jnp.float32)
        return {'x': x, 'w_qkv': w_qkv, 'w_out': w_out, 'b_out': b_out, 'ln_gamma': ln_gamma, 'ln_beta': ln_beta}
    _L3_attn_all = _L3_attn_setup()
    _L3_attn_in = {k: v for k, v in _L3_attn_all.items() if k in ('w_qkv', 'w_out', 'b_out', 'ln_gamma', 'ln_beta')}
    del _L3_attn_all

    def _L3_xattn_setup():
        import jax, jax.numpy as jnp
        import numpy as np
        N_HEADS = 16
        D_MODEL = 128
        HEAD_DIM = D_MODEL // N_HEADS
        MASK_FILL = -100000000.0

        def _split_heads(x):
            B, S, _ = x.shape
            return x.reshape(B, S, N_HEADS, HEAD_DIM).transpose(0, 2, 1, 3)
        key = jax.random.key(seed)
        ks = jax.random.split(key, 12)
        B, L, P = (2, 256, 256)
        s = 1.0 / np.sqrt(D_MODEL).astype(np.float32)
        inp = {'q': jax.random.normal(ks[0], (B, L, D_MODEL), dtype=jnp.float32), 'k': jax.random.normal(ks[1], (B, P, D_MODEL), dtype=jnp.float32), 'v': jax.random.normal(ks[2], (B, P, D_MODEL), dtype=jnp.float32), 'attention_mask': jnp.ones((B, P), dtype=bool), 'Wq': jax.random.normal(ks[3], (D_MODEL, D_MODEL), dtype=jnp.float32) * s, 'bq': jnp.zeros((D_MODEL,), dtype=jnp.float32), 'Wk': jax.random.normal(ks[4], (D_MODEL, D_MODEL), dtype=jnp.float32) * s, 'bk': jnp.zeros((D_MODEL,), dtype=jnp.float32), 'Wv': jax.random.normal(ks[5], (D_MODEL, D_MODEL), dtype=jnp.float32) * s, 'bv': jnp.zeros((D_MODEL,), dtype=jnp.float32), 'Wo': jax.random.normal(ks[6], (D_MODEL, D_MODEL), dtype=jnp.float32) * s, 'bo': jnp.zeros((D_MODEL,), dtype=jnp.float32)}
        return inp
    _L3_xattn_all = _L3_xattn_setup()
    _L3_xattn_in = {k: v for k, v in _L3_xattn_all.items() if k in ('Wq', 'bq', 'Wk', 'bk', 'Wv', 'bv', 'Wo', 'bo')}
    del _L3_xattn_all

    def _L3_ffn_setup():
        import jax, jax.numpy as jnp
        import numpy as np
        EPS = 1e-05
        THRESHOLD = 0.7
        QMAX = 127.0

        def _fake_quant_act(x):
            scale = jnp.maximum(jnp.max(jnp.abs(x)), 1e-08) / QMAX
            q = jnp.round(jnp.clip(x / scale, -QMAX, QMAX)) * scale
            return x + jax.lax.stop_gradient(q - x)

        def _ternary_quant_weight(w):
            absw = jnp.abs(w)
            delta = THRESHOLD * jnp.mean(absw)
            mask = (absw > delta).astype(w.dtype)
            alpha = jnp.sum(absw * mask) / jnp.maximum(jnp.sum(mask), 1.0)
            wq = alpha * jnp.sign(w) * mask
            return w + jax.lax.stop_gradient(wq - w)
        key = jax.random.key(seed)
        k1, k2 = jax.random.split(key)
        B, S, D_IN, D_OUT = (4, 1024, 128, 128)
        x = jax.random.normal(k1, (B, S, D_IN), dtype=jnp.float32)
        weight = jax.random.normal(k2, (D_OUT, D_IN), dtype=jnp.float32) * np.sqrt(2.0 / D_IN)
        gamma = jnp.ones((D_IN,), dtype=jnp.float32)
        beta = jnp.zeros((D_IN,), dtype=jnp.float32)
        return {'x': x, 'weight': weight, 'gamma': gamma, 'beta': beta}
    _L3_ffn_all = _L3_ffn_setup()
    _L3_ffn_in = {k: v for k, v in _L3_ffn_all.items() if k in ('weight', 'gamma', 'beta')}
    del _L3_ffn_all
    return {'x': x, 'ctx_1024': ctx_1024, 'mask_BxS2_ik0': mask_BxS2_ik0, 'mask_BxS2_bf1': mask_BxS2_bf1, 'L0_attn_Wq': _L0_attn_in['Wq'], 'L0_attn_Wk': _L0_attn_in['Wk'], 'L0_attn_Wv': _L0_attn_in['Wv'], 'L0_attn_W_G': _L0_attn_in['W_G'], 'L0_attn_W_O': _L0_attn_in['W_O'], 'L0_xattn_Wq': _L0_xattn_in['Wq'], 'L0_xattn_bq': _L0_xattn_in['bq'], 'L0_xattn_Wk': _L0_xattn_in['Wk'], 'L0_xattn_bk': _L0_xattn_in['bk'], 'L0_xattn_Wv': _L0_xattn_in['Wv'], 'L0_xattn_bv': _L0_xattn_in['bv'], 'L0_xattn_Wo': _L0_xattn_in['Wo'], 'L0_xattn_bo': _L0_xattn_in['bo'], 'L0_ffn_Wr': _L0_ffn_in['Wr'], 'L0_ffn_br': _L0_ffn_in['br'], 'L0_ffn_W1': _L0_ffn_in['W1'], 'L0_ffn_b1': _L0_ffn_in['b1'], 'L0_ffn_W2': _L0_ffn_in['W2'], 'L0_ffn_b2': _L0_ffn_in['b2'], 'L1_attn_Wq': _L1_attn_in['Wq'], 'L1_attn_bq': _L1_attn_in['bq'], 'L1_attn_Wk': _L1_attn_in['Wk'], 'L1_attn_bk': _L1_attn_in['bk'], 'L1_attn_Wv': _L1_attn_in['Wv'], 'L1_attn_bv': _L1_attn_in['bv'], 'L1_attn_W1': _L1_attn_in['W1'], 'L1_attn_b1': _L1_attn_in['b1'], 'L1_attn_W2': _L1_attn_in['W2'], 'L1_attn_b2': _L1_attn_in['b2'], 'L1_attn_W3': _L1_attn_in['W3'], 'L1_attn_b3': _L1_attn_in['b3'], 'L1_xattn_key_matrix': _L1_xattn_in['key_matrix'], 'L1_xattn_value_matrix': _L1_xattn_in['value_matrix'], 'L1_ffn_Wr': _L1_ffn_in['Wr'], 'L1_ffn_br': _L1_ffn_in['br'], 'L1_ffn_W1': _L1_ffn_in['W1'], 'L1_ffn_b1': _L1_ffn_in['b1'], 'L1_ffn_W2': _L1_ffn_in['W2'], 'L1_ffn_b2': _L1_ffn_in['b2'], 'L2_attn_Wq': _L2_attn_in['Wq'], 'L2_attn_Wk': _L2_attn_in['Wk'], 'L2_attn_Wv': _L2_attn_in['Wv'], 'L2_xattn_Wq': _L2_xattn_in['Wq'], 'L2_xattn_bq': _L2_xattn_in['bq'], 'L2_xattn_Wk': _L2_xattn_in['Wk'], 'L2_xattn_bk': _L2_xattn_in['bk'], 'L2_xattn_Wv': _L2_xattn_in['Wv'], 'L2_xattn_bv': _L2_xattn_in['bv'], 'L2_xattn_Wo': _L2_xattn_in['Wo'], 'L2_xattn_bo': _L2_xattn_in['bo'], 'L2_ffn_base_w': _L2_ffn_in['base_w'], 'L2_ffn_base_b': _L2_ffn_in['base_b'], 'L2_ffn_gate_w': _L2_ffn_in['gate_w'], 'L2_ffn_lora_A': _L2_ffn_in['lora_A'], 'L2_ffn_lora_B': _L2_ffn_in['lora_B'], 'L3_attn_w_qkv': _L3_attn_in['w_qkv'], 'L3_attn_w_out': _L3_attn_in['w_out'], 'L3_attn_b_out': _L3_attn_in['b_out'], 'L3_attn_ln_gamma': _L3_attn_in['ln_gamma'], 'L3_attn_ln_beta': _L3_attn_in['ln_beta'], 'L3_xattn_Wq': _L3_xattn_in['Wq'], 'L3_xattn_bq': _L3_xattn_in['bq'], 'L3_xattn_Wk': _L3_xattn_in['Wk'], 'L3_xattn_bk': _L3_xattn_in['bk'], 'L3_xattn_Wv': _L3_xattn_in['Wv'], 'L3_xattn_bv': _L3_xattn_in['bv'], 'L3_xattn_Wo': _L3_xattn_in['Wo'], 'L3_xattn_bo': _L3_xattn_in['bo'], 'L3_ffn_weight': _L3_ffn_in['weight'], 'L3_ffn_gamma': _L3_ffn_in['gamma'], 'L3_ffn_beta': _L3_ffn_in['beta']}

def reference(x, ctx_1024, mask_BxS2_ik0, mask_BxS2_bf1, L0_attn_Wq, L0_attn_Wk, L0_attn_Wv, L0_attn_W_G, L0_attn_W_O, L0_xattn_Wq, L0_xattn_bq, L0_xattn_Wk, L0_xattn_bk, L0_xattn_Wv, L0_xattn_bv, L0_xattn_Wo, L0_xattn_bo, L0_ffn_Wr, L0_ffn_br, L0_ffn_W1, L0_ffn_b1, L0_ffn_W2, L0_ffn_b2, L1_attn_Wq, L1_attn_bq, L1_attn_Wk, L1_attn_bk, L1_attn_Wv, L1_attn_bv, L1_attn_W1, L1_attn_b1, L1_attn_W2, L1_attn_b2, L1_attn_W3, L1_attn_b3, L1_xattn_key_matrix, L1_xattn_value_matrix, L1_ffn_Wr, L1_ffn_br, L1_ffn_W1, L1_ffn_b1, L1_ffn_W2, L1_ffn_b2, L2_attn_Wq, L2_attn_Wk, L2_attn_Wv, L2_xattn_Wq, L2_xattn_bq, L2_xattn_Wk, L2_xattn_bk, L2_xattn_Wv, L2_xattn_bv, L2_xattn_Wo, L2_xattn_bo, L2_ffn_base_w, L2_ffn_base_b, L2_ffn_gate_w, L2_ffn_lora_A, L2_ffn_lora_B, L3_attn_w_qkv, L3_attn_w_out, L3_attn_b_out, L3_attn_ln_gamma, L3_attn_ln_beta, L3_xattn_Wq, L3_xattn_bq, L3_xattn_Wk, L3_xattn_bk, L3_xattn_Wv, L3_xattn_bv, L3_xattn_Wo, L3_xattn_bo, L3_ffn_weight, L3_ffn_gamma, L3_ffn_beta):
    import jax
    import jax.numpy as jnp

    def _L0_attn_ref(X, Wq, Wk, Wv, W_G, W_O):
        import jax, jax.numpy as jnp
        import numpy as np
        B, S, D, H = (2, 256, 128, 8)
        DH = D // H
        EPS = 1e-06

        def _retention(X, Wq, Wk, Wv):
            b, s, d = X.shape
            gammas = 1.0 - jnp.exp2(-5.0 - jnp.arange(H, dtype=jnp.float32))
            q = (X @ Wq).reshape(b, s, H, DH).transpose(0, 2, 1, 3)
            k = (X @ Wk).reshape(b, s, H, DH).transpose(0, 2, 1, 3)
            v = (X @ Wv).reshape(b, s, H, DH).transpose(0, 2, 1, 3)
            scores = jnp.einsum('bhnd,bhmd->bhnm', q, k) / np.sqrt(DH)
            idx = jnp.arange(s, dtype=jnp.float32)
            diff = idx[:, None] - idx[None, :]
            log_g = jnp.log(gammas)[:, None, None]
            decay = jnp.where(diff >= 0, jnp.exp(log_g * diff), 0.0)
            ret = jnp.einsum('bhnm,bhmd->bhnd', scores * decay[None], v)
            mean = ret.mean(axis=-1, keepdims=True)
            var = ret.var(axis=-1, keepdims=True)
            ret = (ret - mean) * jax.lax.rsqrt(var + EPS)
            return ret.transpose(0, 2, 1, 3).reshape(b, s, d)
        Y = _retention(X, Wq, Wk, Wv)
        return jax.nn.silu(X @ W_G) * Y @ W_O

    def _L0_xattn_ref(query, key_value, mask, Wq, bq, Wk, bk, Wv, bv, Wo, bo):
        import jax, jax.numpy as jnp
        import numpy as np
        import math
        D_MODEL = 128
        N_HEADS = 16
        D_K = D_MODEL // N_HEADS
        B, SQ, _ = query.shape
        SK = key_value.shape[1]
        scale = math.sqrt(D_K)

        def proj(x, W, b):
            y = jnp.einsum('bsd,ed->bse', x, W) + b
            return y.reshape(x.shape[0], x.shape[1], N_HEADS, D_K).transpose(0, 2, 1, 3)
        Q = proj(query, Wq, bq)
        K = proj(key_value, Wk, bk)
        V = proj(key_value, Wv, bv)
        scores = jnp.einsum('bhqd,bhkd->bhqk', Q, K) / scale
        m = mask[:, None, None, :] == 0
        scores = jnp.where(m, jnp.float32(-1000000000.0), scores)
        attn = jax.nn.softmax(scores, axis=-1)
        ctx = jnp.einsum('bhqk,bhkd->bhqd', attn, V)
        ctx = ctx.transpose(0, 2, 1, 3).reshape(B, SQ, D_MODEL)
        out = jnp.einsum('bsd,ed->bse', ctx, Wo) + bo
        return out

    def _L0_ffn_ref(x, Wr, br, W1, b1, W2, b2):
        import jax, jax.numpy as jnp
        import numpy as np
        TOP_K = 2

        def _moe(x, Wr, br, W1, b1, W2, b2):
            B, S, D = x.shape
            E = Wr.shape[1]
            xt = x.reshape(-1, D)
            logits = xt @ Wr + br
            top_vals, top_idx = jax.lax.top_k(logits, TOP_K)
            mask = jnp.zeros_like(logits, dtype=bool).at[jnp.arange(xt.shape[0])[:, None], top_idx].set(True)
            sparse_logits = jnp.where(mask, logits, -jnp.inf)
            gate = jax.nn.softmax(sparse_logits, axis=-1)
            h = jax.nn.relu(jnp.einsum('td,edh->teh', xt, W1) + b1)
            y = jnp.einsum('teh,ehd->ted', h, W2) + b2
            out = jnp.einsum('ted,te->td', y, gate)
            return out.reshape(B, S, D)
        return _moe(x, Wr, br, W1, b1, W2, b2)

    def _L1_attn_ref(x, Wq, bq, Wk, bk, Wv, bv, W1, b1, W2, b2, W3, b3):
        import jax, jax.numpy as jnp
        import numpy as np
        B, S, D, H = (4, 256, 128, 512)
        EPS = 1e-12

        def _linear(x, W, b):
            return x @ W.T + b
        Q = _linear(x, Wq, bq)
        K = _linear(x, Wk, bk)
        V = _linear(x, Wv, bv)
        Q = Q / jnp.maximum(jnp.linalg.norm(Q, axis=2, keepdims=True), EPS)
        K = K / jnp.maximum(jnp.linalg.norm(K, axis=2, keepdims=True), EPS)
        sim = jnp.einsum('bqd,bkd->bqk', Q, K)
        attn = jax.nn.softmax(sim, axis=2)
        out = jnp.einsum('bqk,bkd->bqd', attn, V)
        h = jax.nn.relu(_linear(out, W1, b1))
        h = jax.nn.relu(_linear(h, W2, b2))
        return _linear(h, W3, b3)

    def _L1_xattn_ref(query, inputs, key_matrix, value_matrix):
        import jax, jax.numpy as jnp
        import numpy as np
        from math import sqrt
        QUERY_DIM = 128
        KEY_DIM = 128
        VALUE_DIM = 128
        k = jnp.einsum('bsk,kq->bsq', inputs, key_matrix)
        v = jnp.einsum('bsk,kv->bsv', inputs, value_matrix)
        scale = 1.0 / sqrt(QUERY_DIM)
        scores = jnp.einsum('bqd,bsd->bqs', query, k) * scale
        weights = jax.nn.softmax(scores, axis=-1)
        return jnp.einsum('bqs,bsv->bqv', weights, v)

    def _L1_ffn_ref(x, Wr, br, W1, b1, W2, b2):
        import jax, jax.numpy as jnp
        import numpy as np
        B, S, D, H, E = (4, 256, 128, 256, 8)
        d = x.shape[-1]
        tokens = x.reshape(-1, d)
        logits = tokens @ Wr + br
        probs = jax.nn.softmax(logits, axis=-1)
        expert = jnp.argmax(probs, axis=-1)
        max_prob = jnp.take_along_axis(probs, expert[:, None], axis=-1)
        h = jax.nn.relu(jnp.einsum('td,edh->teh', tokens, W1) + b1[None])
        y = jnp.einsum('teh,ehd->ted', h, W2) + b2[None]
        out = jnp.take_along_axis(y, expert[:, None, None], axis=1)[:, 0, :]
        return (out * max_prob).reshape(x.shape)

    def _L2_attn_ref(x, Wq, Wk, Wv):
        import jax, jax.numpy as jnp
        import numpy as np
        HIDDEN = 128
        BETA = 1.0
        SPARSITY_THRESHOLD = 1.0

        def _sparsemax(x):
            n = x.shape[-1]
            z = x - jnp.max(x, axis=-1, keepdims=True)
            sum_z = jnp.sum(z, axis=-1, keepdims=True)
            step = (sum_z - 1.0) / n
            sorted_z = -jnp.sort(-z, axis=-1)
            cumsum_z = jnp.cumsum(sorted_z, axis=-1)
            is_gt = sorted_z > step
            rng = jnp.arange(1, n + 1, dtype=jnp.int32)
            k = jnp.max(rng * is_gt, axis=-1, keepdims=True).astype(x.dtype)
            tau = (cumsum_z - 1.0 - step * k) / k
            return jnp.clip(z - tau, 0.0)
        Q = jnp.einsum('bsd,hd->bsh', x, Wq)
        K = jnp.einsum('bsd,hd->bsh', x, Wk)
        V = jnp.einsum('bsd,hd->bsh', x, Wv)
        energy = jnp.einsum('bsh,bth->bst', Q, K) / jnp.sqrt(jnp.asarray(HIDDEN, x.dtype))
        scores = energy * BETA
        sparsity = jnp.mean(jnp.abs(x))
        attention = jax.lax.cond(sparsity < SPARSITY_THRESHOLD, _sparsemax, lambda s: jax.nn.softmax(s, axis=-1), scores)
        return jnp.einsum('bst,bth->bsh', attention, V)

    def _L2_xattn_ref(x1, x2, Wq, bq, Wk, bk, Wv, bv, Wo, bo):
        import jax, jax.numpy as jnp
        import numpy as np
        D_MODEL = 128
        NUM_HEADS = 16
        HEAD_DIM = D_MODEL // NUM_HEADS
        B, SQ, _ = x1.shape
        SK = x2.shape[1]

        def split_heads(t, S):
            return t.reshape(B, S, NUM_HEADS, HEAD_DIM).transpose(0, 2, 1, 3)
        Q = split_heads(x1 @ Wq + bq, SQ)
        K = split_heads(x2 @ Wk + bk, SK)
        V = split_heads(x2 @ Wv + bv, SK)
        scores = jnp.einsum('bhqd,bhkd->bhqk', Q, K) / jnp.sqrt(jnp.asarray(HEAD_DIM, Q.dtype))
        attn = jax.nn.softmax(scores, axis=-1)
        ctx = jnp.einsum('bhqk,bhkd->bhqd', attn, V)
        ctx = ctx.transpose(0, 2, 1, 3).reshape(B, SQ, D_MODEL)
        return ctx @ Wo + bo

    def _L2_ffn_ref(x, base_w, base_b, gate_w, lora_A, lora_B):
        import jax, jax.numpy as jnp
        import numpy as np
        D_MODEL = 128
        D_OUT = 128
        RANK = 16
        NUM_TRUE = 8
        NUM_NULL = 2
        TOP_K = 2
        SCALING = 32.0 / 16.0
        xf = x.reshape(-1, x.shape[-1])
        logits = jnp.einsum('td,ed->te', xf, gate_w)
        probs = jax.nn.softmax(logits, axis=-1)
        weights, selected = jax.lax.top_k(probs, TOP_K)
        true_mask = (selected < NUM_TRUE).astype(weights.dtype)
        tw = weights * true_mask
        denom = tw.sum(axis=-1, keepdims=True)
        denom = jnp.where(denom > 0, denom, jnp.ones_like(denom))
        nw = tw / denom
        onehot = jax.nn.one_hot(selected, NUM_TRUE, dtype=nw.dtype)
        ew = jnp.einsum('tk,tke->te', nw, onehot)
        z = jnp.einsum('td,erd->ter', xf, lora_A)
        moe = jnp.einsum('ter,te,eor->to', z, ew, lora_B) * SCALING
        base = jnp.einsum('td,od->to', xf, base_w) + base_b
        out = (base + moe).reshape(x.shape[:-1] + (D_OUT,))
        return out

    def _L3_attn_ref(x, w_qkv, w_out, b_out, ln_gamma, ln_beta):
        import jax, jax.numpy as jnp
        import numpy as np
        HEADS = 32
        DIM_HEAD = 32
        EPS = 1e-06
        b, n, dim = x.shape
        scale = DIM_HEAD ** (-0.5)
        qkv = x @ w_qkv
        qkv = qkv.reshape(b, n, 3, HEADS, DIM_HEAD)
        qkv = jnp.transpose(qkv, (2, 0, 3, 1, 4))
        q, k, v = (qkv[0], qkv[1], qkv[2])
        dots = jnp.einsum('bhnd,bhmd->bhnm', q, k) * scale
        attn = jax.nn.softmax(dots, axis=-1)
        out = jnp.einsum('bhnm,bhmd->bhnd', attn, v)
        out = jnp.transpose(out, (0, 2, 1, 3)).reshape(b, n, HEADS * DIM_HEAD)
        out = out @ w_out + b_out
        mu = jnp.mean(out, axis=-1, keepdims=True)
        var = jnp.mean((out - mu) ** 2, axis=-1, keepdims=True)
        out = (out - mu) / jnp.sqrt(var + EPS) * ln_gamma + ln_beta
        return out

    def _L3_xattn_ref(q, k, v, attention_mask, Wq, bq, Wk, bk, Wv, bv, Wo, bo):
        import jax, jax.numpy as jnp
        import numpy as np
        N_HEADS = 16
        D_MODEL = 128
        HEAD_DIM = D_MODEL // N_HEADS
        MASK_FILL = -100000000.0

        def _split_heads(x):
            B, S, _ = x.shape
            return x.reshape(B, S, N_HEADS, HEAD_DIM).transpose(0, 2, 1, 3)
        qm = _split_heads(q @ Wq.T + bq)
        km = _split_heads(k @ Wk.T + bk)
        vm = _split_heads(v @ Wv.T + bv)
        scores = jnp.einsum('bnlh,bnph->bnlp', qm, km) / np.sqrt(HEAD_DIM).astype(np.float32)
        mask = attention_mask[:, None, None, :]
        scores = jnp.where(mask, scores, MASK_FILL)
        attn = jax.nn.softmax(scores, axis=-1)
        out = jnp.einsum('bnlp,bnph->bnlh', attn, vm)
        B, _, L, _ = out.shape
        out = out.transpose(0, 2, 1, 3).reshape(B, L, D_MODEL)
        return out @ Wo.T + bo

    def _L3_ffn_ref(x, weight, gamma, beta):
        import jax, jax.numpy as jnp
        import numpy as np
        EPS = 1e-05
        THRESHOLD = 0.7
        QMAX = 127.0

        def _fake_quant_act(x):
            scale = jnp.maximum(jnp.max(jnp.abs(x)), 1e-08) / QMAX
            q = jnp.round(jnp.clip(x / scale, -QMAX, QMAX)) * scale
            return x + jax.lax.stop_gradient(q - x)

        def _ternary_quant_weight(w):
            absw = jnp.abs(w)
            delta = THRESHOLD * jnp.mean(absw)
            mask = (absw > delta).astype(w.dtype)
            alpha = jnp.sum(absw * mask) / jnp.maximum(jnp.sum(mask), 1.0)
            wq = alpha * jnp.sign(w) * mask
            return w + jax.lax.stop_gradient(wq - w)
        mu = jnp.mean(x, axis=-1, keepdims=True)
        var = jnp.mean(jnp.square(x - mu), axis=-1, keepdims=True)
        xn = (x - mu) * jax.lax.rsqrt(var + EPS) * gamma + beta
        xq = _fake_quant_act(xn)
        wq = _ternary_quant_weight(weight)
        return jnp.einsum('bsi,oi->bso', xq, wq)
    x = _layernorm(x + _L0_attn_ref(x, L0_attn_Wq, L0_attn_Wk, L0_attn_Wv, L0_attn_W_G, L0_attn_W_O), axis=-1)
    x = _layernorm(x + _L0_xattn_ref(x, ctx_1024, mask_BxS2_ik0, L0_xattn_Wq, L0_xattn_bq, L0_xattn_Wk, L0_xattn_bk, L0_xattn_Wv, L0_xattn_bv, L0_xattn_Wo, L0_xattn_bo), axis=-1)
    x = _layernorm(x + _L0_ffn_ref(x, L0_ffn_Wr, L0_ffn_br, L0_ffn_W1, L0_ffn_b1, L0_ffn_W2, L0_ffn_b2), axis=-1)
    x = _layernorm(x + _L1_attn_ref(x, L1_attn_Wq, L1_attn_bq, L1_attn_Wk, L1_attn_bk, L1_attn_Wv, L1_attn_bv, L1_attn_W1, L1_attn_b1, L1_attn_W2, L1_attn_b2, L1_attn_W3, L1_attn_b3), axis=-1)
    x = _layernorm(x + _L1_xattn_ref(x, ctx_1024, L1_xattn_key_matrix, L1_xattn_value_matrix), axis=-1)
    x = _layernorm(x + _L1_ffn_ref(x, L1_ffn_Wr, L1_ffn_br, L1_ffn_W1, L1_ffn_b1, L1_ffn_W2, L1_ffn_b2), axis=-1)
    x = _layernorm(x + _L2_attn_ref(x, L2_attn_Wq, L2_attn_Wk, L2_attn_Wv), axis=-1)
    x = _layernorm(x + _L2_xattn_ref(x, ctx_1024, L2_xattn_Wq, L2_xattn_bq, L2_xattn_Wk, L2_xattn_bk, L2_xattn_Wv, L2_xattn_bv, L2_xattn_Wo, L2_xattn_bo), axis=-1)
    x = _layernorm(x + _L2_ffn_ref(x, L2_ffn_base_w, L2_ffn_base_b, L2_ffn_gate_w, L2_ffn_lora_A, L2_ffn_lora_B), axis=-1)
    x = _layernorm(x + _L3_attn_ref(x, L3_attn_w_qkv, L3_attn_w_out, L3_attn_b_out, L3_attn_ln_gamma, L3_attn_ln_beta), axis=-1)
    x = _layernorm(x + _L3_xattn_ref(x, ctx_1024, ctx_1024, mask_BxS2_bf1, L3_xattn_Wq, L3_xattn_bq, L3_xattn_Wk, L3_xattn_bk, L3_xattn_Wv, L3_xattn_bv, L3_xattn_Wo, L3_xattn_bo), axis=-1)
    x = _layernorm(x + _L3_ffn_ref(x, L3_ffn_weight, L3_ffn_gamma, L3_ffn_beta), axis=-1)
    return x

_drawn_inputs = setup_inputs


def setup_inputs(seed=0):
    import zlib

    import numpy as np

    out = dict(_drawn_inputs(seed))
    spreads = {'L0_xattn_bq': (0.0, 0.1),
     'L0_xattn_bk': (0.0, 0.8),
     'L0_xattn_bv': (0.0, 0.1),
     'L0_xattn_bo': (0.0, 0.1),
     'L0_ffn_br': (0.0, 0.1),
     'L0_ffn_b1': (0.0, 0.1),
     'L0_ffn_b2': (0.0, 0.1),
     'L1_ffn_br': (0.0, 0.394),
     'L1_ffn_b1': (0.0, 0.605),
     'L1_ffn_b2': (0.0, 0.273),
     'L2_xattn_bq': (0.0, 0.369),
     'L2_xattn_bk': (0.0, 0.8),
     'L2_xattn_bv': (0.0, 0.1),
     'L2_xattn_bo': (0.0, 0.1),
     'L3_attn_b_out': (0.0, 0.345),
     'L3_attn_ln_gamma': (1.0, 0.2),
     'L3_attn_ln_beta': (0.0, 0.1),
     'L3_xattn_bq': (0.0, 0.351),
     'L3_xattn_bk': (0.0, 0.8),
     'L3_xattn_bv': (0.0, 0.1),
     'L3_xattn_bo': (0.0, 0.1),
     'L3_ffn_gamma': (1.0, 0.2),
     'L3_ffn_beta': (0.0, 0.1)}
    factors = {'L1_attn_Wq': 4.759,
     'L1_attn_bq': 8.0,
     'L1_attn_Wk': 4.84,
     'L1_attn_bk': 8.0,
     'L1_attn_bv': 4.63,
     'L1_attn_b1': 4.835,
     'L1_attn_b2': 4.038,
     'L1_attn_b3': 3.835,
     'L1_ffn_W1': 3.661,
     'L1_ffn_W2': 3.12,
     'L2_ffn_base_b': 6.333}
    for name, (base, spread) in spreads.items():
        noise = np.random.default_rng([zlib.crc32(name.encode()), seed]).standard_normal(out[name].shape)
        drawn = base * np.exp(spread * noise) if base else spread * noise
        out[name] = jnp.asarray(drawn.astype(out[name].dtype))
    for name, factor in factors.items():
        out[name] = (out[name] * factor).astype(out[name].dtype)
    return out
```

```python
import numpy as np
import concourse.bass as bass
from concourse import mybir
from contextlib import ExitStack

ALU = mybir.AluOpType
ACT = mybir.ActivationFunctionType
AX = mybir.AxisListType
F32 = mybir.dt.float32
BF16 = mybir.dt.bfloat16
I32 = mybir.dt.int32
U32 = mybir.dt.uint32
U8 = mybir.dt.uint8

B, S, D, SK = 8, 256, 128, 64
P = 128
BATCHES_PER_STEP = 4
NB = BATCHES_PER_STEP
STEPS = B // NB
NC = NB // 2
T = NB * S
NT = T // P
CH = 512
EPS = 1e-5

W_COLS = [
    [("L0_attn_Wq", 128), ("L0_attn_Wk", 128), ("L0_attn_Wv", 128), ("L0_attn_W_G", 128), ("L0_attn_W_O", 128),
     ("L0_xattn_Wq", 128), ("L0_xattn_Wk", 128), ("L0_xattn_Wv", 128), ("L0_xattn_Wo", 128), ("L0_ffn_Wr", 8)],
    [("L0_ffn_W1", 8 * 512)],
    [("L0_ffn_W2", 32 * 128)],
    [("L1_attn_Wq", 128), ("L1_attn_Wk", 128), ("L1_attn_Wv", 128), ("L1_attn_W1", 128), ("L1_attn_W2", 512),
     ("L1_attn_W3", 512), ("L1_xattn_key_matrix", 128), ("L1_xattn_value_matrix", 128), ("L1_ffn_Wr", 8)],
    [("L1_ffn_W1", 8 * 256), ("L1_ffn_W2", 16 * 128)],
    [("L2_attn_Wq", 128), ("L2_attn_Wk", 128), ("L2_attn_Wv", 128),
     ("L2_xattn_Wq", 128), ("L2_xattn_Wk", 128), ("L2_xattn_Wv", 128), ("L2_xattn_Wo", 128),
     ("L2_ffn_gate_w", 10), ("L2_ffn_lora_A", 128), ("L2_ffn_lora_B", 128), ("L2_ffn_base_w", 128)],
    [("L3_attn_w_qkv", 3072), ("L3_attn_w_out", 1024),
     ("L3_xattn_Wq", 128), ("L3_xattn_Wk", 128), ("L3_xattn_Wv", 128), ("L3_xattn_Wo", 128),
     ("L3_ffn_weight", 128)],
]
W_AT, W_GROUP, _at = {}, {}, 0
GROUP_AT = []
for _g, _cols in enumerate(W_COLS):
    GROUP_AT.append(_at)
    for _n, _w in _cols:
        W_AT[_n], W_GROUP[_n] = (_at, _w), _g
        _at += _w
GROUP_AT.append(_at)
W_TOTAL = _at
B_COLS = [("L0_xattn_bq", 1), ("L0_xattn_bk", 1), ("L0_ffn_b1", 32), ("L1_attn_b1", 1), ("L1_attn_b2", 4),
          ("L1_ffn_b1", 16), ("L2_xattn_bq", 1), ("L2_xattn_bk", 1), ("L3_xattn_bq", 1), ("L3_xattn_bk", 1)]
ROWS = [("L0_xattn_bv", 128), ("L0_xattn_bo", 128), ("L0_ffn_br", 8), ("L1_attn_bq", 128), ("L1_attn_bk", 128),
        ("L1_attn_bv", 128), ("L1_attn_b3", 128), ("L1_ffn_br", 8), ("L2_xattn_bv", 128), ("L2_xattn_bo", 128),
        ("L2_ffn_base_b", 128), ("L3_attn_b_out", 128), ("L3_attn_ln_gamma", 128), ("L3_attn_ln_beta", 128),
        ("L3_xattn_bv", 128), ("L3_xattn_bo", 128), ("L3_ffn_gamma", 128), ("L3_ffn_beta", 128)]


def spots(cols):
    at, out = 0, {}
    for n, w in cols:
        out[n] = (at, w)
        at += w
    return out, at


B_AT, B_TOTAL = spots(B_COLS)
R_AT, R_TOTAL = spots(ROWS)

GAMMA = [1.0 - 2.0 ** (-5.0 - h) for h in range(8)]


def bf16_parts(value):
    parts = []
    for _ in range(3):
        part = (np.array(value, np.float32).view(np.uint32) & np.uint32(0xFFFF0000)).view(np.float32)
        parts.append(float(part))
        value = value - float(part)
    assert value == 0
    return parts


class Psum:

    def __init__(self, banks, full, read):
        self.banks, self.full, self.read_ = banks, full, read
        self.reset()

    def reset(self):
        self.next, self.place, self.uses, self.last, self.open = 0, {}, [0] * 8, [None] * 8, set()

    def take(self, pe, name, n=1):
        k = self.next
        while k + n > 8 or any(self.last[j] in self.open for j in range(k, k + n)):
            k = 0 if k + n > 8 else k + 1
        self.next = (k + n) % 8
        for old in {self.last[j] for j in range(k, k + n)} - {None}:
            first, count = self.place[old][0], self.place[old][2]
            pe.wait_ge(self.read_[first], count)
        self.uses[k] += 1
        self.place[name] = (k, n, self.uses[k])
        self.open.add(name)
        for j in range(k, k + n):
            self.last[j] = name
        return self.view(name)

    def view(self, name):
        k, n, _ = self.place[name]
        return self.banks[:, k] if n == 1 else self.banks[:, k:k + n]

    def filled(self, name):
        self.open.discard(name)
        return self.full[self.place[name][0]]

    def made(self, name):
        k, _, count = self.place[name]
        return self.full[k], count

    def copied(self, name):
        k, _, count = self.place[name]
        return self.read_[k], count


class Own:

    def __init__(self, eng, step_sem, psum, sig):
        self.eng, self.step_sem, self.psum, self.sig = eng, step_sem, psum, sig
        self.count, self.last = {}, (step_sem, 0)

    def _next(self, sem, name):
        self.count[name] = self.count.get(name, 0) + 1
        self.last = (sem, self.count[name])
        return sem

    def step(self):
        return self._next(self.step_sem, "step")

    def flag(self, name):
        return self._next(self.sig(name), name)

    def read(self, product):
        self.last = self.psum.copied(product)
        return self.last[0]

    def own(self):
        return self.last


def decoder(nc, x, x_t, ctx_t, ctx_d, keep0, keep3, weights, bcols, rows, b2s, out):
    ctx = ExitStack()
    with ctx:
        sb = lambda n, s, d=F32: ctx.enter_context(nc.sbuf_tensor(n, s, d))
        sem = lambda n: ctx.enter_context(nc.semaphore(n))

        w_loaded = [sem(f"w_loaded{g}") for g in range(len(W_COLS))]
        small_loaded, consts_made, x_stored = sem("small_loaded"), sem("consts_made"), sem("x_stored")
        setup_step, parity_made = sem("setup_step"), sem("parity_made")
        bank_full = [sem(f"bank_full{k}") for k in range(8)]
        bank_read = [sem(f"bank_read{k}") for k in range(8)]
        pe_step, dve_step, act_step, pool_step = (sem(n) for n in ("pe_step", "dve_step", "act_step", "pool_step"))
        loaded = sem("loaded")
        signals = {}

        def sig(name):
            if name not in signals:
                signals[name] = sem(name)
            return signals[name]

        psum = Psum(ctx.enter_context(nc.psum_tensor("banks", [P, 8, CH], F32)), bank_full, bank_read)

        WS = sb("WS", [P, W_TOTAL])
        W = lambda n: WS[:, W_AT[n][0]:W_AT[n][0] + W_AT[n][1]]
        BC = sb("BC", [P, B_TOTAL])
        bcol = lambda n, j=0: BC[:, B_AT[n][0] + j:B_AT[n][0] + j + 1]
        RW = sb("RW", [P, R_TOTAL])
        row = lambda n: RW[:, R_AT[n][0]:R_AT[n][0] + R_AT[n][1]]
        B2 = sb("B2", [8, 2, D])
        ident = sb("ident", [P, P])
        ident16 = sb("ident16", [P, P], BF16)
        ones16 = sb("ones16", [3, P], BF16)
        ones32 = sb("ones32", [P, 32])
        decay = sb("decay", [P, 8, S])
        head_of8 = sb("head_of8", [P, 16])
        parity16 = sb("parity16", [P, 2])
        pick = sb("pick", [64, 32, P], BF16)
        fills = sb("fills", [3, 2])
        expert = sb("expert", [P, 8])
        minus_half = sb("minus_half", [P, 32])
        zeros = sb("zeros", [P, S])
        XALL = sb("XALL", [P, B * S // P, D])
        ABSMAX = sb("ABSMAX", [P, B * S // P])

        X = sb("X", [P, NT, D])
        R = sb("R", [P, NT, D])
        XB = sb("XB", [P, NT, D])
        XT = sb("XT", [P, T])
        CT = sb("CT", [P, NB, SK])
        CD = sb("CD", [P, NB, 2 * SK])
        KEEP0 = sb("KEEP0", [P, NB, SK], I32)
        KEEP3 = sb("KEEP3", [P, NB, SK], U8)
        st = sb("st", [P, 16, 6])
        mv = sb("mv", [P, 16, 2])
        var = sb("var", [P, 16])
        rstd = sb("rstd", [P, 16])
        ARENA = (nc.sbuf_bytes_remaining - 64) // 4
        arena = sb("arena", [P, ARENA])

        class Carve:

            def __init__(self, top):
                self.top, self.at = top, ARENA if top else 0

            def __call__(self, *shape, dt=F32, parts=P):
                n = int(np.prod(shape))
                words = n if dt in (F32, I32, U32) else (n + 1) // 2
                if self.top:
                    self.at -= words
                a = arena[0:parts, self.at:self.at + words]
                if not self.top:
                    self.at += words
                assert 0 <= self.at <= ARENA, (self.at, shape)
                if dt not in (F32,):
                    a = a.bitcast(dt)
                if len(shape) > 1:
                    names = "abcd"[:len(shape)]
                    a = a.rearrange(f"p ({' '.join(names)}) -> p {' '.join(names)}", **dict(zip(names, shape)))
                return a

        def bc(ap, axis, n):
            a = ap.unsqueeze(axis)
            shape = list(a.shape)
            shape[axis] = n
            return a.broadcast_to(shape)

        tile = lambda t: slice(t * P, (t + 1) * P)
        chunk = lambda c: slice(c * CH, (c + 1) * CH)
        ctiles = lambda c: slice(4 * c, 4 * c + 4)

        with nc.Block(no_gpsimd_drain=True) as block:
            @block.sync
            def _(sp):
                sp.dma_start(RW[:], rows.partition_broadcast(P)).then_inc(small_loaded, 16)
                sp.dma_start(BC[:], bcols).then_inc(small_loaded, 16)
                sp.dma_start(B2[:], b2s.rearrange("l e d -> e l d")).then_inc(small_loaded, 16)
                for g in range(len(W_COLS)):
                    a, b = GROUP_AT[g], GROUP_AT[g + 1]
                    sp.dma_start(WS[:, a:b], weights[:, a:b]).then_inc(w_loaded[g], 16)

            @block.gpsimd
            def _(pool):
                pool.memset(ident[:], 0.0).then_inc(setup_step, 1)
                pool.memset(head_of8[:], 1.0).then_inc(setup_step, 1)
                pool.memset(parity16[:], 0.0).then_inc(setup_step, 1)
                pool.memset(pick[:], 0.0).then_inc(setup_step, 1)
                pool.memset(ones32[:], 1.0).then_inc(setup_step, 1)
                pool.memset(minus_half[:], -0.5).then_inc(setup_step, 1)
                pool.memset(zeros[:], 0.0).then_inc(setup_step, 1)
                pool.iota(expert[:], [[1, 8]], base=0, channel_multiplier=0,
                          allow_small_or_imprecise_dtypes=True).then_inc(setup_step, 1)
                for h in range(8):
                    pool.iota(decay[:, h, :], [[1, S]], base=0, channel_multiplier=-1,
                              allow_small_or_imprecise_dtypes=True).then_inc(setup_step, 1)
                pool.memset(fills[:], 0.0).then_inc(setup_step, 1)
                pool.memset(ones16[:], 1.0).then_inc(setup_step, 1)
                pool.wait_ge(setup_step, 18)
                pool.affine_select(ident[:], ident[:], pattern=[[-1, P]], compare_op=ALU.not_equal, fill=1.0,
                                   base=0, channel_multiplier=1).then_inc(setup_step, 1)
                for half in range(2):
                    pool.wait_ge(setup_step, 19 + half)
                    pool.affine_select(pick[32 * half:32 * half + 32], pick[32 * half:32 * half + 32],
                                       pattern=[[-1, 32], [0, P]], compare_op=ALU.not_equal, fill=1.0,
                                       base=0, channel_multiplier=1).then_inc(setup_step, 1)
                pool.wait_ge(setup_step, 21)
                pool.affine_select(head_of8[:], head_of8[:], pattern=[[-8, 16]], compare_op=ALU.is_ge, fill=0.0,
                                   base=0, channel_multiplier=1).then_inc(setup_step, 1)
                pool.wait_ge(setup_step, 22)
                pool.affine_select(head_of8[:], head_of8[:], pattern=[[8, 16]], compare_op=ALU.is_ge, fill=0.0,
                                   base=7, channel_multiplier=-1).then_inc(setup_step, 1)
                pool.tensor_copy(ident16[:], ident[:]).then_inc(setup_step, 1)
                for col, value in enumerate((1e9, 1e8)):
                    for j, part in enumerate(bf16_parts(value)):
                        pool.wait_ge(setup_step, 24 + 3 * col + j)
                        pool.affine_select(fills[:, col:col + 1], fills[:, col:col + 1], pattern=[[0, 1]],
                                           compare_op=ALU.not_equal, fill=part, base=-j,
                                           channel_multiplier=1).then_inc(setup_step, 1)
                pool.wait_ge(consts_made, 8)
                for h in range(8):
                    pool.affine_select(decay[:, h, :], decay[:, h, :], pattern=[[1, S]], compare_op=ALU.is_ge,
                                       fill=0.0, base=0, channel_multiplier=-1).then_inc(setup_step, 1)
                pool.wait_ge(setup_step, 38)

            @block.scalar
            def _(act):
                act.wait_ge(setup_step, 17)
                for h in range(8):
                    nc.scalar.activation(decay[:, h, :], decay[:, h, :], ACT.Exp,
                                         scale=float(np.log(GAMMA[h]))).then_inc(consts_made, 1)

            @block.vector
            def _(dve):
                dve.wait_ge(setup_step, 24)
                h4 = head_of8[:].rearrange("p (a b c) -> p b a c", a=4, b=2, c=2)
                nc.vector.tensor_reduce(parity16[:], h4, AX.XY, ALU.add).then_inc(parity_made, 1)
                dve.wait_ge(small_loaded, 48)

        V, A, G, PE = nc.vector, nc.scalar, nc.gpsimd, nc.tensor


        def norm_stats(dve, c, src, name, eps):
            dve.eng.wait_ge(*dve.own())
            for t in range(4):
                V.bn_stats(st[:, 4 * c + t, :], src[:, t, :]).then_inc(dve.step(), 1)
            dve.eng.wait_ge(*dve.own())
            for t in range(4):
                V.bn_aggr(mv[:, 4 * c + t, :], st[:, 4 * c + t, :]).then_inc(dve.step(), 1)
            dve.eng.wait_ge(*dve.own())
            V.tensor_scalar(var[:, ctiles(c)], mv[:, ctiles(c), 1], eps, None, ALU.add).then_inc(dve.flag(name + ".var"), 1)

        def norm_rstd(pool, c, name):
            pool.eng.wait_ge(sig(name + ".var"), c + 1)
            G.tensor_tensor(rstd[:, ctiles(c)], var[:, ctiles(c)], minus_half[:, 0:4], ALU.pow).then_inc(pool.flag(name + ".rstd"), 1)

        def norm_apply(dve, c, src, dst, name, ready=None):
            dve.eng.wait_ge(sig(name + ".rstd"), c + 1)
            for t in range(4):
                i = 4 * c + t
                ins = V.tensor_scalar(dst[:, t, :], src[:, t, :], mv[:, i, 0:1], rstd[:, i:i + 1],
                                      ALU.subtract, ALU.mult)
                if t == 3 and ready:
                    ins.then_inc(dve.flag(ready), 1)
                else:
                    ins.then_inc(dve.step(), 1)

        def end_dve(dve, L, product=None, base=None):
            for c in range(NC):
                if product:
                    if base is XB:
                        dve.eng.wait_ge(sig(L + ".xb"), c + 1)
                    dve.eng.wait_ge(*psum.made(f"{product}{c}"))
                    ps = psum.view(f"{product}{c}")
                    V.tensor_tensor(R[:, ctiles(c)], ps.rearrange("p (t d) -> p t d", t=4),
                                              base[:, ctiles(c)], ALU.add).then_inc(dve.read(f"{product}{c}"), 1)
                norm_stats(dve, c, R[:, ctiles(c)], L, EPS)
            for c in range(NC):
                norm_apply(dve, c, R[:, ctiles(c)], X[:, ctiles(c)], L, L + ".x")

        def end_pool(pool, L):
            for c in range(NC):
                norm_rstd(pool, c, L)

        def end_pe(pe, L):
            for c in range(NC):
                pe.wait_ge(sig(L + ".x"), c + 1)
                v = psum.take(pe, f"{L}.xT{c}")
                for t in range(4):
                    ins = PE.transpose(v[:, tile(t)], X[:, 4 * c + t, :], ident[:])
                ins.then_inc(psum.filled(f"{L}.xT{c}"), 1)

        def end_act(act, L):
            for c in range(NC):
                act.eng.wait_ge(*psum.made(f"{L}.xT{c}"))
                v = psum.view(f"{L}.xT{c}")
                A.copy(XT[:, chunk(c)], v).then_inc(act.read(f"{L}.xT{c}"), 1)

        def add_bias_pool(pool, L, before, bias):
            for c in range(NC):
                pool.eng.wait_ge(sig(before + ".x"), c + 1)
                G.tensor_tensor(XB[:, ctiles(c)], X[:, ctiles(c)], bc(row(bias), 1, 4), ALU.add).then_inc(pool.flag(L + ".xb"), 1)

        def x_t_ready(pe, before, c):
            if before:
                pe.wait_ge(*psum.copied(f"{before}.xT{c}"))
            else:
                pe.wait_ge(loaded, LOADS * 16)

        def project_out_pe(pe, name, src_t, w, product=None):
            for c in range(NC):
                pe.wait_ge(*psum.copied(f"{name}T{c}"))
                v = psum.take(pe, f"{product or name + '.out'}{c}")
                for t in range(4):
                    ins = PE.matmul(v[:, tile(t)], src_t[:, tile(4 * c + t)], w, start=True, stop=True)
                ins.then_inc(psum.filled(f"{product or name + '.out'}{c}"), 1)

        def turn_pe(pe, name, src, c):
            v = psum.take(pe, f"{name}T{c}")
            for t in range(4):
                ins = PE.transpose(v[:, tile(t)], src[:, 4 * c + t, :], ident[:])
            ins.then_inc(psum.filled(f"{name}T{c}"), 1)

        def move_act(act, product, dst):
            act.eng.wait_ge(*psum.made(product))
            v = psum.view(product)
            A.copy(dst, v).then_inc(act.read(product), 1)

        class ret:
            a = Carve(False)
            QT, KT = a(T), a(2, T)
            VG = a(NT, 2 * D)
            SG, Y = a(NT, D), a(NT, D)
            YT = QT
            SD = a(4, 2, 384)
            SQ = a(32, 16)
            m, v = a(NC, 32), a(NC, 32)
            rs = a(NC, 32)

        def retention_pe(pe):
            pe.wait_ge(w_loaded[0], 16)
            for c in range(NC):
                x_t_ready(pe, None, c)
                for n, w in (("q", "L0_attn_Wq"), ("k", "L0_attn_Wk")):
                    v = psum.take(pe, f"ret.{n}{c}")
                    PE.matmul(v, W(w), XT[:, chunk(c)], start=True, stop=True).then_inc(psum.filled(f"ret.{n}{c}"), 1)
                w0 = W_AT["L0_attn_Wv"][0]
                for half in range(2):
                    v = psum.take(pe, f"ret.vg{c}{half}")
                    for t in range(2):
                        ins = PE.matmul(v[:, t * 256:t * 256 + 256], XT[:, tile(4 * c + 2 * half + t)],
                                        WS[:, w0:w0 + 256], start=True, stop=True)
                    ins.then_inc(psum.filled(f"ret.vg{c}{half}"), 1)
            for c in range(NC):
                pe.wait_ge(*psum.copied(f"ret.q{c}"))
                pe.wait_ge(*psum.copied(f"ret.k{c}"))
                for b in (2 * c, 2 * c + 1):
                    q0 = b * S
                    for hp in range(4):
                        v = psum.take(pe, f"ret.s{b}.{hp}", 2)
                        r = slice(32 * hp, 32 * hp + 32)
                        for hh in range(2):
                            PE.matmul(v[:, hh, 0:256], ret.KT[r, hh, q0:q0 + 128], ret.QT[r, q0:q0 + 256],
                                      start=True, stop=True)
                            ins = PE.matmul(v[:, hh, 256:384], ret.KT[r, hh, q0 + 128:q0 + 256],
                                            ret.QT[r, q0 + 128:q0 + 256], start=True, stop=True)
                        ins.then_inc(psum.filled(f"ret.s{b}.{hp}"), 1)
                    if b % 2 == 0:
                        v_o = psum.take(pe, f"ret.o{c}")
                        pe.wait_ge(*psum.copied(f"ret.vg{c}0"))
                        pe.wait_ge(*psum.copied(f"ret.vg{c}1"))
                    t0 = (b % 2) * 256
                    for hp in range(4):
                        pe.wait_ge(*psum.copied(f"ret.s{b}.{hp}"))
                        for hh in range(2):
                            h = 2 * hp + hh
                            hd = slice(16 * h, 16 * h + 16)
                            PE.matmul(v_o[:, t0 + 16 * h:t0 + 16 * h + 16], ret.SD[:, hp, hh, 0:128],
                                      ret.VG[:, 2 * b, hd], start=True, stop=True)
                            PE.matmul(v_o[:, t0 + 128 + 16 * h:t0 + 144 + 16 * h], ret.SD[:, hp, hh, 128:256],
                                      ret.VG[:, 2 * b, hd], start=True, stop=False)
                            ins = PE.matmul(v_o[:, t0 + 128 + 16 * h:t0 + 144 + 16 * h], ret.SD[:, hp, hh, 256:384],
                                            ret.VG[:, 2 * b + 1, hd], start=False, stop=True)
                    if b % 2 == 1:
                        ins.then_inc(psum.filled(f"ret.o{c}"), 1)
                    else:
                        ins.then_inc(sig("ret.half"), 1)
            for c in range(NC):
                pe.wait_ge(sig("ret.y"), c + 1)
                turn_pe(pe, "ret.y", ret.Y, c)
            project_out_pe(pe, "ret.y", ret.YT, W("L0_attn_W_O"))
            end_pe(pe, "ret")

        def retention_act(act):
            for c in range(NC):
                move_act(act, f"ret.q{c}", ret.QT[:, chunk(c)])
                for half in range(2):
                    t = 4 * c + 2 * half
                    act.eng.wait_ge(*psum.made(f"ret.vg{c}{half}"))
                    v = psum.view(f"ret.vg{c}{half}")
                    A.copy(ret.VG[:, t:t + 2], v.rearrange("p (t d) -> p t d", t=2)).then_inc(act.read(f"ret.vg{c}{half}"), 1)
                act.eng.wait_ge(*act.own())
                A.activation(ret.SG[:, ctiles(c)], ret.VG[:, ctiles(c), D:2 * D], ACT.Exp, scale=-1.0).then_inc(act.flag("ret.gexp"), 1)
            for c in range(NC):
                move_act(act, f"ret.yT{c}", ret.YT[:, chunk(c)])
            end_act(act, "ret")

        def retention_dve(dve):
            for c in range(NC):
                dve.eng.wait_ge(*psum.made(f"ret.k{c}"))
                v = psum.view(f"ret.k{c}")
                V.tensor_scalar(ret.KT[:, 0, chunk(c)], v, parity16[:, 0:1], None, ALU.mult).then_inc(dve.step(), 1)
                V.tensor_scalar(ret.KT[:, 1, chunk(c)], v, parity16[:, 1:2], None, ALU.mult).then_inc(dve.read(f"ret.k{c}"), 1)
            for c in range(NC):
                dve.eng.wait_ge(sig("ret.gexp"), c + 1)
                g = ret.SG[:, ctiles(c)]
                V.tensor_scalar(g, g, 1.0, None, ALU.add).then_inc(dve.step(), 1)
                dve.eng.wait_ge(*dve.own())
                V.reciprocal(g, g).then_inc(dve.step(), 1)
                dve.eng.wait_ge(*dve.own())
                V.tensor_tensor(g, g, ret.VG[:, ctiles(c), D:2 * D], ALU.mult).then_inc(dve.step(), 1)
                for b in (2 * c, 2 * c + 1):
                    for hp in range(4):
                        dve.eng.wait_ge(*psum.made(f"ret.s{b}.{hp}"))
                        v = psum.view(f"ret.s{b}.{hp}")
                        if b:
                            if b % 2:
                                dve.eng.wait_ge(sig("ret.half"), c + 1)
                            else:
                                dve.eng.wait_ge(psum.full[psum.place[f"ret.o{c - 1}"][0]], psum.place[f"ret.o{c - 1}"][2])
                        d = decay[:, 2 * hp:2 * hp + 2, :]
                        V.tensor_tensor(ret.SD[:, hp, :, 0:256], v[:, :, 0:256], d, ALU.mult).then_inc(dve.step(), 1)
                        V.tensor_tensor(ret.SD[:, hp, :, 256:384], v[:, :, 256:384], d[:, :, 0:128],
                                                  ALU.mult).then_inc(dve.read(f"ret.s{b}.{hp}"), 1)
                dve.eng.wait_ge(*psum.made(f"ret.o{c}"))
                v = psum.view(f"ret.o{c}").rearrange("p (g w) -> p g w", w=16)
                y = ret.Y[:, ctiles(c)].rearrange("p t (h w) -> p (t h) w", w=16)
                V.tensor_reduce(ret.m[:, c], v, AX.X, ALU.add).then_inc(dve.step(), 1)
                dve.eng.wait_ge(*dve.own())
                V.tensor_scalar(ret.m[:, c], ret.m[:, c], 1.0 / 16, None, ALU.mult).then_inc(dve.step(), 1)
                dve.eng.wait_ge(*dve.own())
                V.tensor_tensor(y, v, bc(ret.m[:, c], 2, 16), ALU.subtract).then_inc(dve.read(f"ret.o{c}"), 1)
                dve.eng.wait_ge(*dve.own())
                V.tensor_tensor(ret.SQ, y, y, ALU.mult).then_inc(dve.step(), 1)
                dve.eng.wait_ge(*dve.own())
                V.tensor_reduce(ret.v[:, c], ret.SQ, AX.X, ALU.add).then_inc(dve.step(), 1)
                dve.eng.wait_ge(*dve.own())
                V.tensor_scalar(ret.v[:, c], ret.v[:, c], 1.0 / 16, 1e-6, ALU.mult, ALU.add).then_inc(dve.flag("ret.hvar"), 1)
                dve.eng.wait_ge(sig("ret.hrstd"), c + 1)
                V.tensor_tensor(y, y, bc(ret.rs[:, c], 2, 16), ALU.mult).then_inc(dve.step(), 1)
                dve.eng.wait_ge(*dve.own())
                V.tensor_tensor(ret.Y[:, ctiles(c)], ret.Y[:, ctiles(c)], g, ALU.mult).then_inc(dve.flag("ret.y"), 1)
            end_dve(dve, "ret", "ret.y.out", X)

        def retention_pool(pool):
            for c in range(NC):
                pool.eng.wait_ge(sig("ret.hvar"), c + 1)
                G.tensor_tensor(ret.rs[:, c], ret.v[:, c], minus_half[:], ALU.pow).then_inc(pool.flag("ret.hrstd"), 1)
            end_pool(pool, "ret")

        class Cross:
            def __init__(self, L, prefix, before, top, group, keep, fill, waits_all=False):
                self.L, self.p, self.before, self.group = L, prefix, before, group
                self.keep, self.fill, self.waits_all = keep, fill, waits_all
                a = Carve(top)
                self.QT = a(T)
                self.KT = a(NB, SK)
                self.KM = a(2, 16, SK)
                self.VB = a(2, 8, 18)
                self.SS = a(2, 16, SK)
                self.ET = a(2, 8, P)
                self.O = a(NT, D)
                self.OT = a(T)
                self.mx = a(2, 16)
                self.rc = a(2, 2, 16)
                self.keepf = a(NB, SK)
                self.fillr = a(NB, SK, dt=BF16)

            def w(self, n):
                return W(f"{self.p}_{n}")

            def start(self, eng):
                if self.waits_all:
                    eng.wait_ge(sig(self.before + ".x"), NC)

            def pe(self, pe):
                L = self.L
                pe.wait_ge(w_loaded[self.group], 16)
                self.start(pe)
                v = psum.take(pe, f"{L}.k")
                PE.matmul(v[:, 0:NB * SK], self.w("Wk"), CT[:].rearrange("p b k -> p (b k)"),
                                    start=True, stop=True).then_inc(psum.filled(f"{L}.k"), 1)
                for c in range(NC):
                    x_t_ready(pe, self.before, c)
                    v = psum.take(pe, f"{L}.q{c}")
                    PE.matmul(v, self.w("Wq"), XT[:, chunk(c)], start=True, stop=True).then_inc(psum.filled(f"{L}.q{c}"), 1)
                self.values_pe(pe, 0)
                self.scores_pe(pe, 0)
                for t in range(NT):
                    if t % 2 == 0 and t // 2 + 1 < NB:
                        self.values_pe(pe, t // 2 + 1)
                    if t + 1 < NT:
                        self.scores_pe(pe, t + 1)
                    self.probs_pe(pe, t)
                for c in range(NC):
                    pe.wait_ge(*psum.copied(f"{L}.pv{2 * c}"))
                    pe.wait_ge(*psum.copied(f"{L}.pv{2 * c + 1}"))
                    turn_pe(pe, f"{L}.o", self.O, c)
                project_out_pe(pe, f"{L}.o", self.OT, self.w("Wo"))
                end_pe(pe, L)

            def values_pe(self, pe, b):
                v = psum.take(pe, f"{self.L}.v{b}")
                PE.matmul(v[:, 0:D], CD[:, b, :], self.w("Wv"), start=True, stop=True).then_inc(psum.filled(f"{self.L}.v{b}"), 1)

            def scores_pe(self, pe, t):
                L, b = self.L, t // 2
                if t % 4 == 0:
                    pe.wait_ge(*psum.copied(f"{L}.q{t // 4}"))
                if t % 2 == 0:
                    pe.wait_ge(sig(L + ".km"), b + 1)
                    if self.keep is not None and t == 0:
                        pe.wait_ge(sig(L + ".fill"), 1)
                v = psum.take(pe, f"{L}.s{t}", 2)
                for half in range(2):
                    km = self.KM[:, b % 2, 8 * half:8 * half + 8, :].rearrange("p h k -> p (h k)")
                    ins = PE.matmul(v[:, half], self.QT[:, tile(t)], km, start=True, stop=self.keep is None)
                    if self.keep is not None:
                        ins = PE.matmul(v[:, half].rearrange("p (h k) -> p h k", h=8), ones16[0:3, :],
                                        bc(self.fillr[0:3, b, :], 1, 8), start=False, stop=True)
                ins.then_inc(psum.filled(f"{L}.s{t}"), 1)

            def probs_pe(self, pe, t):
                L, b = self.L, t // 2
                pe.wait_ge(sig(L + ".exp"), t + 1)
                v = psum.take(pe, f"{L}.eT{t}", 2)
                e = self.SS[:, t % 2].rearrange("p (a h) k -> p a (h k)", a=8)
                for pair in range(8):
                    ins = PE.transpose(v[:, pair // 4, tile(pair % 4)], e[:, pair, :], ident[:])
                ins.then_inc(psum.filled(f"{L}.eT{t}"), 1)
                if t % 2 == 0:
                    pe.wait_ge(*psum.copied(f"{L}.v{b}"))
                pe.wait_ge(*psum.copied(f"{L}.eT{t}"))
                if t % 2 == 0:
                    psum.take(pe, f"{L}.pv{b}")
                v = psum.view(f"{L}.pv{b}")
                for pair in range(8):
                    at = (t % 2) * 144 + 18 * pair
                    ins = PE.matmul(v[:, at:at + 18], self.ET[:, t % 2, pair, :], self.VB[:, b % 2, pair, :],
                                    start=True, stop=True)
                if t % 2:
                    ins.then_inc(psum.filled(f"{L}.pv{b}"), 1)
                else:
                    ins.then_inc(sig(L + ".half"), 1)

            def act(self, act):
                L = self.L
                self.start(act.eng)
                for t in range(NT):
                    act.eng.wait_ge(*psum.copied(f"{L}.s{t}"))
                    e = self.SS[:, t % 2]
                    A.activation(e, e, ACT.Exp).then_inc(act.flag(L + ".exp"), 1)
                    act.eng.wait_ge(*psum.made(f"{L}.eT{t}"))
                    v = psum.view(f"{L}.eT{t}")
                    if t >= 2:
                        if t % 2 == 0:
                            act.eng.wait_ge(sig(L + ".half"), t // 2)
                        else:
                            k, _, n = psum.place[f"{L}.pv{t // 2 - 1}"]
                            act.eng.wait_ge(psum.full[k], n)
                    A.copy(self.ET[:, t % 2].rearrange("p (a b) q -> p a (b q)", a=2), v).then_inc(act.read(f"{L}.eT{t}"), 1)
                for c in range(NC):
                    move_act(act, f"{L}.oT{c}", self.OT[:, chunk(c)])
                end_act(act, L)

            def dve(self, dve):
                L = self.L
                self.start(dve.eng)
                if self.keep is not None:
                    V.tensor_scalar(self.keepf, self.keep[:], 0.0, None, ALU.not_equal).then_inc(dve.step(), 1)
                    dve.eng.wait_ge(*dve.own())
                    V.tensor_scalar(self.fillr[0:3], self.keepf[0:3], 1.0, fills[:, self.fill:self.fill + 1],
                                               ALU.subtract, ALU.mult).then_inc(dve.flag(L + ".fill"), 1)
                dve.eng.wait_ge(*psum.made(f"{L}.k"))
                v = psum.view(f"{L}.k")
                kt = self.KT.rearrange("p b k -> p (b k)")
                if self.keep is not None:
                    V.scalar_tensor_tensor(kt, v[:, 0:NB * SK], bcol(self.p + "_bk"),
                                                     self.keepf.rearrange("p b k -> p (b k)"), ALU.add, ALU.mult).then_inc(dve.read(f"{L}.k"), 1)
                else:
                    V.tensor_scalar(kt, v[:, 0:NB * SK], bcol(self.p + "_bk"), None, ALU.add).then_inc(dve.read(f"{L}.k"), 1)
                for j in range(2):
                    V.memset(self.VB[:, j], 0.0).then_inc(dve.step(), 1)
                dve.eng.wait_ge(*dve.own())
                for j in range(2):
                    V.memset(self.VB[0:64, j, :, 16], 1.0).then_inc(dve.step(), 1)
                    V.memset(self.VB[64:128, j, :, 17], 1.0).then_inc(dve.step(), 1)
                for c in range(NC):
                    dve.eng.wait_ge(*psum.made(f"{L}.q{c}"))
                    v = psum.view(f"{L}.q{c}")
                    V.tensor_scalar(self.QT[:, chunk(c)], v, bcol(self.p + "_bq"), 8 ** -0.5,
                                              ALU.add, ALU.mult).then_inc(dve.read(f"{L}.q{c}"), 1)
                self.values_dve(dve, 0)
                for t in range(NT):
                    if t % 2 == 0 and t // 2 + 1 < NB and t == 0:
                        self.values_dve(dve, 1)
                    if t % 2 and t >= 3:
                        self.out_dve(dve, t // 2 - 1)
                    dve.eng.wait_ge(*psum.made(f"{L}.s{t}"))
                    v = psum.view(f"{L}.s{t}").rearrange("p a (h k) -> p (a h) k", h=8)
                    V.tensor_reduce(self.mx[:, t % 2], v, AX.X, ALU.max).then_inc(dve.step(), 1)
                    dve.eng.wait_ge(*dve.own())
                    if t >= 2:
                        k, _, n = psum.place[f"{L}.eT{t - 2}"]
                        dve.eng.wait_ge(psum.full[k], n)
                    V.tensor_tensor(self.SS[:, t % 2], v, bc(self.mx[:, t % 2], 2, SK), ALU.subtract).then_inc(dve.read(f"{L}.s{t}"), 1)
                self.out_dve(dve, NB - 1)
                end_dve(dve, L, f"{L}.o.out", XB)

            def values_dve(self, dve, b):
                L = self.L
                dve.eng.wait_ge(*psum.made(f"{L}.v{b}"))
                v = psum.view(f"{L}.v{b}")[:, 0:D].rearrange("p (a j w) -> p a j w", j=2, w=8)
                bias = row(self.p + "_bv").rearrange("p (a j w) -> p a j w", j=2, w=8)
                dve.eng.wait_ge(*dve.own())
                V.tensor_tensor(self.VB[0:64, b % 2, :, 0:8], v[0:64, :, 0], bias[0:64, :, 0], ALU.add).then_inc(dve.step(), 1)
                V.tensor_tensor(self.VB[64:128, b % 2, :, 8:16], v[64:128, :, 1], bias[64:128, :, 1],
                                          ALU.add).then_inc(dve.read(f"{L}.v{b}"), 1)

            def out_dve(self, dve, b):
                L = self.L
                dve.eng.wait_ge(*psum.made(f"{L}.pv{b}"))
                v = psum.view(f"{L}.pv{b}")[:, 0:288].rearrange("p (a x) -> p a x", x=18)
                rc = self.rc[:, b % 2].rearrange("p a (b j) -> p (a b) j", j=2)
                dve.eng.wait_ge(*dve.own())
                V.reciprocal(rc, v[:, :, 16:18]).then_inc(dve.step(), 1)
                dve.eng.wait_ge(*dve.own())
                o = self.O[:, 2 * b:2 * b + 2].rearrange("p t (a j w) -> p (t a) j w", j=2, w=8)
                V.tensor_tensor(o, v[:, :, 0:16].rearrange("p a (j w) -> p a j w", j=2), bc(rc, 3, 8),
                                          ALU.mult).then_inc(dve.read(f"{L}.pv{b}"), 1)
                if b + 2 < NB:
                    self.values_dve(dve, b + 2)

            def pool(self, pool):
                L = self.L
                self.start(pool.eng)
                pool.eng.wait_ge(*psum.copied(f"{L}.k"))
                for b in range(NB):
                    if b >= 2:
                        k, _, n = psum.place[f"{L}.s{2 * b - 3}"]
                        pool.eng.wait_ge(psum.full[k], n)
                    if b == min(2, NB - 1):
                        add_bias_pool(pool, L, self.before, self.p + "_bo")
                    G.tensor_tensor(self.KM[:, b % 2], bc(self.KT[:, b, :], 1, 16), bc(head_of8[:], 2, SK),
                                                ALU.mult).then_inc(pool.flag(L + ".km"), 1)
                end_pool(pool, L)

        class Moe:
            def __init__(self, L, prefix, before, top, group1, group2, J, b2, top2):
                self.L, self.p, self.before, self.g1, self.g2, self.J, self.b2, self.top2 = \
                    L, prefix, before, group1, group2, J, b2, top2
                a = Carve(top)
                self.HT = a(2, NC, J, CH)
                self.LG, self.EL, self.GW = a(NT, 8), a(NT, 8), a(NT, 8)
                self.M8, self.I8, self.IF = a(NT, 8), a(NT, 8, dt=U32), a(NT, 8)
                self.H2 = a(NT, 8)
                self.dn = a(NT)
                self.GT = a(T, parts=8)
                self.W1 = W(prefix + "_W1").rearrange("p (e j h) -> p e j h", e=8, j=J)
                self.W2 = W(prefix + "_W2").rearrange("p (e j d) -> p e j d", e=8, j=J)

            def pe(self, pe):
                L = self.L
                for c in range(NC):
                    x_t_ready(pe, self.before, c)
                    v = psum.take(pe, f"{L}.lg{c}")
                    for t in range(4):
                        ins = PE.matmul(v[:, 8 * t:8 * t + 8], XT[:, tile(4 * c + t)], W(self.p + "_Wr"),
                                        start=True, stop=True)
                    ins.then_inc(psum.filled(f"{L}.lg{c}"), 1)
                pe.wait_ge(w_loaded[self.g1], 16)
                for c in range(NC):
                    self.hidden_pe(pe, 0, c)
                for c in range(NC):
                    pe.wait_ge(sig(L + ".gates"), c + 1)
                    v = psum.take(pe, f"{L}.gT{c}")
                    for t in range(4):
                        ins = PE.transpose(v[0:8, tile(t)], self.GW[:, 4 * c + t, :], ident[:])
                    ins.then_inc(psum.filled(f"{L}.gT{c}"), 1)
                pe.wait_ge(w_loaded[self.g2], 16)
                for e in range(8):
                    for c in range(NC):
                        if e + 1 < 8:
                            self.hidden_pe(pe, e + 1, c)
                        if e == 0:
                            pe.wait_ge(*psum.copied(f"{L}.gT{c}"))
                            v = psum.take(pe, f"{L}.b2{c}")
                            for t in range(4):
                                ins = PE.matmul(v[:, tile(t)], self.GT[:, tile(4 * c + t)], B2[:, self.b2, :],
                                                start=True, stop=True)
                            ins.then_inc(psum.filled(f"{L}.b2{c}"), 1)
                        for j in range(self.J):
                            pe.wait_ge(*psum.copied(f"{L}.h{e}.{c}.{j}"))
                        v = psum.take(pe, f"{L}.y{e}.{c}")
                        for t in range(4):
                            for j in range(self.J):
                                ins = PE.matmul(v[:, tile(t)], self.HT[:, e % 2, c, j, tile(t)], self.W2[:, e, j],
                                                start=j == 0, stop=j == self.J - 1)
                        ins.then_inc(psum.filled(f"{L}.y{e}.{c}"), 1)
                end_pe(pe, L)

            def hidden_pe(self, pe, e, c):
                for j in range(self.J):
                    v = psum.take(pe, f"{self.L}.h{e}.{c}.{j}")
                    PE.matmul(v, self.W1[:, e, j], XT[:, chunk(c)], start=True, stop=True).then_inc(psum.filled(f"{self.L}.h{e}.{c}.{j}"), 1)

            def hidden_free(self, eng, e, c):
                if e >= 2:
                    k, _, n = psum.place[f"{self.L}.y{e - 2}.{c}"]
                    eng.wait_ge(psum.full[k], n)

            def act_share(self, j):
                return j % 4 != 3

            def act(self, act):
                L = self.L
                for c in range(NC):
                    self.hidden_act(act, 0, c)
                for c in range(NC):
                    act.eng.wait_ge(sig(L + ".shifted"), c + 1)
                    A.activation(self.EL[:, ctiles(c)], self.EL[:, ctiles(c)], ACT.Exp).then_inc(act.flag(L + ".exp"), 1)
                for c in range(NC):
                    act.eng.wait_ge(*psum.made(f"{L}.gT{c}"))
                    v = psum.view(f"{L}.gT{c}")
                    A.copy(self.GT[:, chunk(c)], v[0:8]).then_inc(act.read(f"{L}.gT{c}"), 1)
                for e in range(1, 8):
                    for c in range(NC):
                        self.hidden_act(act, e, c)
                end_act(act, L)

            def hidden_act(self, act, e, c):
                for j in range(self.J):
                    if self.act_share(j):
                        act.eng.wait_ge(*psum.made(f"{self.L}.h{e}.{c}.{j}"))
                        v = psum.view(f"{self.L}.h{e}.{c}.{j}")
                        self.hidden_free(act.eng, e, c)
                        A.activation(self.HT[:, e % 2, c, j], v, ACT.Relu,
                                               bias=bcol(self.p + "_b1", e * self.J + j)).then_inc(act.read(f"{self.L}.h{e}.{c}.{j}"), 1)

            def hidden_dve(self, dve, e, c):
                for j in range(self.J):
                    if not self.act_share(j):
                        dve.eng.wait_ge(*psum.made(f"{self.L}.h{e}.{c}.{j}"))
                        v = psum.view(f"{self.L}.h{e}.{c}.{j}")
                        self.hidden_free(dve.eng, e, c)
                        V.tensor_scalar(self.HT[:, e % 2, c, j], v, bcol(self.p + "_b1", e * self.J + j), 0.0,
                                                  ALU.add, ALU.max).then_inc(dve.read(f"{self.L}.h{e}.{c}.{j}"), 1)

            def dve(self, dve):
                L = self.L
                for c in range(NC):
                    dve.eng.wait_ge(*psum.made(f"{L}.lg{c}"))
                    v = psum.view(f"{L}.lg{c}")
                    lg = self.LG[:, ctiles(c)]
                    V.tensor_tensor(lg, v[:, 0:32].rearrange("p (t e) -> p t e", t=4),
                                              bc(row(self.p + "_br"), 1, 4), ALU.add).then_inc(dve.read(f"{L}.lg{c}"), 1)
                    dve.eng.wait_ge(*dve.own())
                    for t in range(4 * c, 4 * c + 4):
                        V.max(self.M8[:, t], self.LG[:, t]).then_inc(dve.step(), 1)
                    dve.eng.wait_ge(*dve.own())
                    for t in range(4 * c, 4 * c + 4):
                        V.max_index(self.I8[:, t], self.M8[:, t], self.LG[:, t]).then_inc(dve.step(), 1)
                    V.tensor_tensor(self.EL[:, ctiles(c)], lg, bc(self.M8[:, ctiles(c), 0], 2, 8),
                                               ALU.subtract).then_inc(dve.flag(L + ".shifted"), 1)
                    dve.eng.wait_ge(*dve.own())
                    V.tensor_copy(self.IF[:, ctiles(c)], self.I8[:, ctiles(c)]).then_inc(dve.step(), 1)
                for c in range(NC):
                    self.hidden_dve(dve, 0, c)
                for c in range(NC):
                    g, h2 = self.GW[:, ctiles(c)], self.H2[:, ctiles(c)]
                    ex = bc(expert[:], 1, 4)
                    dve.eng.wait_ge(*dve.own())
                    V.tensor_tensor(g, ex, bc(self.IF[:, ctiles(c), 0], 2, 8), ALU.is_equal).then_inc(dve.step(), 1)
                    dve.eng.wait_ge(sig(L + ".exp"), c + 1)
                    if self.top2:
                        V.tensor_tensor(h2, ex, bc(self.IF[:, ctiles(c), 1], 2, 8), ALU.is_equal).then_inc(dve.step(), 1)
                        dve.eng.wait_ge(*dve.own())
                        V.tensor_tensor(g, g, h2, ALU.add).then_inc(dve.step(), 1)
                        dve.eng.wait_ge(*dve.own())
                        V.tensor_tensor(g, g, self.EL[:, ctiles(c)], ALU.mult).then_inc(dve.step(), 1)
                        dve.eng.wait_ge(*dve.own())
                        V.tensor_reduce(self.dn[:, ctiles(c)], g, AX.X, ALU.add).then_inc(dve.step(), 1)
                    else:
                        V.tensor_reduce(self.dn[:, ctiles(c)], self.EL[:, ctiles(c)], AX.X, ALU.add).then_inc(dve.step(), 1)
                    dve.eng.wait_ge(*dve.own())
                    V.reciprocal(self.dn[:, ctiles(c)], self.dn[:, ctiles(c)]).then_inc(dve.step(), 1)
                    dve.eng.wait_ge(*dve.own())
                    V.tensor_tensor(g, g, bc(self.dn[:, ctiles(c)], 2, 8), ALU.mult).then_inc(dve.flag(L + ".gates"), 1)
                for e in range(8):
                    for c in range(NC):
                        if e + 1 < 8:
                            self.hidden_dve(dve, e + 1, c)
                        r = R[:, ctiles(c)]
                        if e == 0:
                            dve.eng.wait_ge(*psum.made(f"{L}.b2{c}"))
                            v = psum.view(f"{L}.b2{c}")
                            V.tensor_tensor(r, v.rearrange("p (t d) -> p t d", t=4), X[:, ctiles(c)],
                                                      ALU.add).then_inc(dve.read(f"{L}.b2{c}"), 1)
                        dve.eng.wait_ge(*psum.made(f"{L}.y{e}.{c}"))
                        v = psum.view(f"{L}.y{e}.{c}")
                        dve.eng.wait_ge(*dve.own())
                        for t in range(4):
                            ins = V.scalar_tensor_tensor(r[:, t], v[:, tile(t)], self.GW[:, 4 * c + t, e:e + 1],
                                                         r[:, t], ALU.mult, ALU.add)
                            if t < 3:
                                ins.then_inc(dve.step(), 1)
                        ins.then_inc(dve.read(f"{L}.y{e}.{c}"), 1)
                end_dve(dve, L)

            def pool(self, pool):
                end_pool(pool, self.L)

        class cos:
            a = Carve(True)
            QKV = a(NT, 3 * D)
            QT, KT = a(T), a(T)
            PR = a(NT, S)
            PT = a(2, 2, S)
            OT, H1 = a(T), a(T)
            H2 = a(NC, 4, CH)
            sq = a(D)
            ssq, rn = a(NT, 2), a(NT, 2)
            mx, nb, sm = a(NT), a(NT), a(NT)

        def cosine_pe(pe):
            pe.wait_ge(w_loaded[3], 16)
            w0 = W_AT["L1_attn_Wq"][0]
            for c in range(NC):
                x_t_ready(pe, "moe0", c)
                for t in range(4 * c, 4 * c + 4):
                    v = psum.take(pe, f"cos.qkv{t}")
                    PE.matmul(v[:, 0:384], XT[:, tile(t)], WS[:, w0:w0 + 384], start=True, stop=True).then_inc(psum.filled(f"cos.qkv{t}"), 1)
            for c in range(NC):
                pe.wait_ge(*psum.copied(f"cos.qkv{4 * c + 3}"))
                turn_pe(pe, "cos.q", cos.QKV[:, :, 0:D], c)
                pe.wait_ge(sig("cos.khat"), c + 1)
                turn_pe(pe, "cos.k", cos.QKV[:, :, D:2 * D], c)
            for c in range(NC):
                pe.wait_ge(*psum.copied(f"cos.qT{c}"))
                pe.wait_ge(*psum.copied(f"cos.kT{c}"))
                for b in (2 * c, 2 * c + 1):
                    v = psum.take(pe, f"cos.s{b}")
                    for t in range(2):
                        ins = PE.matmul(v[:, t * S:t * S + S], cos.QT[:, tile(2 * b + t)], cos.KT[:, b * S:b * S + S],
                                        start=True, stop=True)
                    ins.then_inc(psum.filled(f"cos.s{b}"), 1)
            attend_pe(pe, "cos", cos.PR, cos.PT, lambda b: (sig("cos.probs"), b + 1))
            for c in range(NC):
                for b in (2 * c, 2 * c + 1):
                    if b % 2 == 0:
                        v = psum.take(pe, f"cos.oT{c}")
                    pe.wait_ge(*psum.copied(f"cos.pT{b}"))
                    for kt in range(2):
                        ins = PE.matmul(v[:, (b % 2) * S:(b % 2) * S + S], cos.QKV[:, 2 * b + kt, 2 * D:3 * D],
                                        cos.PT[:, b % 2, kt, :], start=kt == 0, stop=kt == 1)
                    if b % 2 == 0 and NC > 1:
                        ins.then_inc(sig("cos.half"), 1)
                ins.then_inc(psum.filled(f"cos.oT{c}"), 1)
                if c + 1 < NC:
                    for b in (2 * c + 2, 2 * c + 3):
                        turn_probs_pe(pe, "cos", cos.PR, b, lambda b: (sig("cos.probs"), b + 1))
            for c in range(NC):
                pe.wait_ge(*psum.copied(f"cos.oT{c}"))
                v = psum.take(pe, f"cos.h1{c}")
                PE.matmul(v, W("L1_attn_W1"), cos.OT[:, chunk(c)], start=True, stop=True).then_inc(psum.filled(f"cos.h1{c}"), 1)
            for c in range(NC):
                pe.wait_ge(*psum.copied(f"cos.h1{c}"))
                for j in range(4):
                    v = psum.take(pe, f"cos.h2{c}.{j}")
                    PE.matmul(v, W("L1_attn_W2")[:, tile(j)], cos.H1[:, chunk(c)], start=True, stop=True).then_inc(psum.filled(f"cos.h2{c}.{j}"), 1)
            for c in range(NC):
                for j in range(4):
                    pe.wait_ge(*psum.copied(f"cos.h2{c}.{j}"))
                v = psum.take(pe, f"cos.out{c}")
                for t in range(4):
                    for j in range(4):
                        ins = PE.matmul(v[:, tile(t)], cos.H2[:, c, j, tile(t)], W("L1_attn_W3")[:, tile(j)],
                                        start=j == 0, stop=j == 3)
                ins.then_inc(psum.filled(f"cos.out{c}"), 1)
            end_pe(pe, "cos")

        def turn_probs_pe(pe, name, src, b, ready):
            pe.wait_ge(*ready(b))
            v = psum.take(pe, f"{name}.pT{b}")
            for kt in range(2):
                for t in range(2):
                    ins = PE.transpose(v[:, kt * S + t * P:kt * S + t * P + P], src[:, 2 * b + t, tile(kt)], ident[:])
            ins.then_inc(psum.filled(f"{name}.pT{b}"), 1)

        def attend_pe(pe, name, src, dst, ready):
            for b in range(2):
                turn_probs_pe(pe, name, src, b, ready)

        def cosine_act(act):
            for t in range(NT):
                act.eng.wait_ge(*psum.copied(f"cos.qkv{t}"))
                for j in range(2):
                    act.eng.wait_ge(*act.own())
                    ins = A.activation(cos.sq, cos.QKV[:, t, j * D:j * D + D], ACT.Square,
                                       accum_out=cos.ssq[:, t, j:j + 1])
                    if t % 4 == 3 and j == 1:
                        ins.then_inc(act.flag("cos.ssq"), 1)
                    else:
                        ins.then_inc(act.step(), 1)
            for c in range(NC):
                move_act(act, f"cos.qT{c}", cos.QT[:, chunk(c)])
                move_act(act, f"cos.kT{c}", cos.KT[:, chunk(c)])
            for b in range(NB):
                act.eng.wait_ge(*psum.made(f"cos.s{b}"))
                v = psum.view(f"cos.s{b}")
                act.eng.wait_ge(sig("cos.nb"), b + 1)
                for t in range(2):
                    i = 2 * b + t
                    ins = A.activation(cos.PR[:, i], v[:, t * S:t * S + S], ACT.Exp, bias=cos.nb[:, i:i + 1],
                                       scale=cos.rn[:, i, 0:1], accum_out=cos.sm[:, i:i + 1])
                    if t == 0:
                        ins.then_inc(act.step(), 1)
                ins.then_inc(act.read(f"cos.s{b}"), 1)
            for c in range(NC):
                for b in (2 * c, 2 * c + 1):
                    if b >= 2:
                        if b % 2:
                            k, _, n = psum.place[f"cos.oT{c - 1}"]
                            act.eng.wait_ge(psum.full[k], n)
                        else:
                            act.eng.wait_ge(sig("cos.half"), c)
                    move_act(act, f"cos.pT{b}", cos.PT[:, b % 2].rearrange("p a q -> p (a q)"))
                move_act(act, f"cos.oT{c}", cos.OT[:, chunk(c)])
            for c in range(NC):
                act.eng.wait_ge(*psum.made(f"cos.h1{c}"))
                v = psum.view(f"cos.h1{c}")
                A.activation(cos.H1[:, chunk(c)], v, ACT.Relu, bias=bcol("L1_attn_b1")).then_inc(act.read(f"cos.h1{c}"), 1)
            for c in range(NC):
                for j in range(0, 4, 2):
                    act.eng.wait_ge(*psum.made(f"cos.h2{c}.{j}"))
                    v = psum.view(f"cos.h2{c}.{j}")
                    A.activation(cos.H2[:, c, j], v, ACT.Relu, bias=bcol("L1_attn_b2", j)).then_inc(act.read(f"cos.h2{c}.{j}"), 1)
            end_act(act, "cos")

        def cosine_dve(dve):
            bias = RW[:, R_AT["L1_attn_bq"][0]:R_AT["L1_attn_bq"][0] + 384]
            for t in range(NT):
                dve.eng.wait_ge(*psum.made(f"cos.qkv{t}"))
                v = psum.view(f"cos.qkv{t}")
                V.tensor_tensor(cos.QKV[:, t], v[:, 0:384], bias, ALU.add).then_inc(dve.read(f"cos.qkv{t}"), 1)
            for c in range(NC):
                dve.eng.wait_ge(sig("cos.pow"), c + 1)
                rn = cos.rn[:, ctiles(c)]
                V.tensor_scalar(rn, rn, 1e12, None, ALU.min).then_inc(dve.step(), 1)
                dve.eng.wait_ge(*dve.own())
                for t in range(4 * c, 4 * c + 4):
                    k = cos.QKV[:, t, D:2 * D]
                    ins = V.tensor_scalar(k, k, cos.rn[:, t, 1:2], None, ALU.mult)
                    if t % 4 < 3:
                        ins.then_inc(dve.step(), 1)
                ins.then_inc(dve.flag("cos.khat"), 1)
            for b in range(NB):
                dve.eng.wait_ge(*psum.made(f"cos.s{b}"))
                v = psum.view(f"cos.s{b}").rearrange("p (t k) -> p t k", t=2)
                mx = cos.mx[:, 2 * b:2 * b + 2]
                V.tensor_reduce(mx, v, AX.X, ALU.max, negate=True).then_inc(dve.step(), 1)
                dve.eng.wait_ge(*dve.own())
                V.tensor_tensor(cos.nb[:, 2 * b:2 * b + 2], mx, cos.rn[:, 2 * b:2 * b + 2, 0], ALU.mult).then_inc(dve.flag("cos.nb"), 1)
            for b in range(NB):
                dve.eng.wait_ge(*psum.copied(f"cos.s{b}"))
                sm = cos.sm[:, 2 * b:2 * b + 2]
                V.reciprocal(sm, sm).then_inc(dve.step(), 1)
                dve.eng.wait_ge(*dve.own())
                for t in (2 * b, 2 * b + 1):
                    ins = V.tensor_scalar(cos.PR[:, t], cos.PR[:, t], cos.sm[:, t:t + 1], None, ALU.mult)
                    if t % 2 == 0:
                        ins.then_inc(dve.step(), 1)
                ins.then_inc(dve.flag("cos.probs"), 1)
            for c in range(NC):
                for j in (1, 3):
                    dve.eng.wait_ge(*psum.made(f"cos.h2{c}.{j}"))
                    v = psum.view(f"cos.h2{c}.{j}")
                    V.tensor_scalar(cos.H2[:, c, j], v, bcol("L1_attn_b2", j), 0.0, ALU.add, ALU.max).then_inc(dve.read(f"cos.h2{c}.{j}"), 1)
            end_dve(dve, "cos", "cos.out", XB)

        def cosine_pool(pool):
            for c in range(NC):
                pool.eng.wait_ge(sig("cos.ssq"), c + 1)
                G.tensor_tensor(cos.rn[:, ctiles(c)].rearrange("p t j -> p (t j)"),
                                            cos.ssq[:, ctiles(c)].rearrange("p t j -> p (t j)"),
                                            minus_half[:, 0:8], ALU.pow).then_inc(pool.flag("cos.pow"), 1)
            add_bias_pool(pool, "cos", "moe0", "L1_attn_b3")
            end_pool(pool, "cos")

        class one:
            a = Carve(False)
            KT = a(NB, SK)
            VV = a(NB, D, parts=64)
            PR = a(NT, SK)
            PT = a(T, parts=64)
            mx, sm = a(NT), a(NT)

        def one_pe(pe):
            v = psum.take(pe, "one.k")
            PE.matmul(v[:, 0:NB * SK], W("L1_xattn_key_matrix"), CT[:].rearrange("p b k -> p (b k)"),
                                start=True, stop=True).then_inc(psum.filled("one.k"), 1)
            v = psum.take(pe, "one.v")
            for b in range(NB):
                ins = PE.matmul(v[0:64, b * D:b * D + D], CT[:, b, :], W("L1_xattn_value_matrix"), start=True, stop=True)
            ins.then_inc(psum.filled("one.v"), 1)
            pe.wait_ge(*psum.copied("one.k"))
            for c in range(NC):
                x_t_ready(pe, "cos", c)
                v = psum.take(pe, f"one.s{c}")
                for t in range(4):
                    i = 4 * c + t
                    ins = PE.matmul(v[:, t * SK:t * SK + SK], XT[:, tile(i)], one.KT[:, i // 2, :], start=True, stop=True)
                ins.then_inc(psum.filled(f"one.s{c}"), 1)
            for c in range(NC):
                pe.wait_ge(*psum.copied(f"one.s{c}"))
                v = psum.take(pe, f"one.pT{c}")
                for t in range(4):
                    ins = PE.transpose(v[0:64, tile(t)], one.PR[:, 4 * c + t, :], ident[:])
                ins.then_inc(psum.filled(f"one.pT{c}"), 1)
            for c in range(NC):
                pe.wait_ge(*psum.copied(f"one.pT{c}"))
                if c == 0:
                    pe.wait_ge(*psum.copied("one.v"))
                v = psum.take(pe, f"one.out{c}")
                for t in range(4):
                    i = 4 * c + t
                    ins = PE.matmul(v[:, tile(t)], one.PT[:, tile(i)], one.VV[:, i // 2, :], start=True, stop=True)
                ins.then_inc(psum.filled(f"one.out{c}"), 1)
            end_pe(pe, "one")

        def one_act(act):
            act.eng.wait_ge(*psum.made("one.k"))
            v = psum.view("one.k")
            A.copy(one.KT.rearrange("p b k -> p (b k)"), v[:, 0:NB * SK]).then_inc(act.read("one.k"), 1)
            act.eng.wait_ge(*psum.made("one.v"))
            v = psum.view("one.v")
            A.copy(one.VV.rearrange("p b k -> p (b k)"), v[0:64, 0:NB * D]).then_inc(act.read("one.v"), 1)
            for c in range(NC):
                act.eng.wait_ge(*psum.made(f"one.s{c}"))
                v = psum.view(f"one.s{c}")
                act.eng.wait_ge(sig("one.mx"), c + 1)
                for t in range(4):
                    i = 4 * c + t
                    ins = A.activation(one.PR[:, i], v[:, t * SK:t * SK + SK], ACT.Exp, bias=one.mx[:, i:i + 1],
                                       scale=D ** -0.5, accum_out=one.sm[:, i:i + 1])
                    if t < 3:
                        ins.then_inc(act.step(), 1)
                ins.then_inc(act.read(f"one.s{c}"), 1)
            for c in range(NC):
                act.eng.wait_ge(*psum.made(f"one.pT{c}"))
                v = psum.view(f"one.pT{c}")
                A.copy(one.PT[:, chunk(c)], v[0:64]).then_inc(act.read(f"one.pT{c}"), 1)
            end_act(act, "one")

        def one_dve(dve):
            for c in range(NC):
                dve.eng.wait_ge(*psum.made(f"one.s{c}"))
                v = psum.view(f"one.s{c}")[:, 0:4 * SK].rearrange("p (t k) -> p t k", t=4)
                mx = one.mx[:, ctiles(c)]
                V.tensor_reduce(mx, v, AX.X, ALU.max, negate=True).then_inc(dve.step(), 1)
                dve.eng.wait_ge(*dve.own())
                V.tensor_scalar(mx, mx, D ** -0.5, None, ALU.mult).then_inc(dve.flag("one.mx"), 1)
            for c in range(NC):
                dve.eng.wait_ge(*psum.copied(f"one.s{c}"))
                sm = one.sm[:, ctiles(c)]
                V.reciprocal(sm, sm).then_inc(dve.step(), 1)
                dve.eng.wait_ge(*dve.own())
                dve.eng.wait_ge(*psum.made(f"one.out{c}"))
                v = psum.view(f"one.out{c}")
                for t in range(4):
                    i = 4 * c + t
                    ins = V.scalar_tensor_tensor(R[:, i], v[:, tile(t)], one.sm[:, i:i + 1], X[:, i], ALU.mult, ALU.add)
                    if t < 3:
                        ins.then_inc(dve.step(), 1)
                ins.then_inc(dve.read(f"one.out{c}"), 1)
            end_dve(dve, "one")

        def one_pool(pool):
            end_pool(pool, "one")

        class spm:
            a = Carve(False)
            QT, KT = a(T), a(T)
            VV = a(NT, D)
            Z, SA, SB = a(NT, S), a(NT, S), a(NT, S)
            mx, sz, stp, cnt, rk, add_ = a(NT), a(NT), a(NT), a(NT), a(NT), a(NT)
            PT = a(2, 2, S)

        def sparse_pe(pe):
            pe.wait_ge(w_loaded[5], 16)
            for c in range(NC):
                x_t_ready(pe, "moe1", c)
                for n, w in (("q", "L2_attn_Wq"), ("k", "L2_attn_Wk")):
                    v = psum.take(pe, f"spm.{n}{c}")
                    PE.matmul(v, W(w), XT[:, chunk(c)], start=True, stop=True).then_inc(psum.filled(f"spm.{n}{c}"), 1)
                v = psum.take(pe, f"spm.v{c}")
                for t in range(4):
                    ins = PE.matmul(v[:, tile(t)], XT[:, tile(4 * c + t)], W("L2_attn_Wv"), start=True, stop=True)
                ins.then_inc(psum.filled(f"spm.v{c}"), 1)
            for c in range(NC):
                pe.wait_ge(*psum.copied(f"spm.q{c}"))
                pe.wait_ge(*psum.copied(f"spm.k{c}"))
                for b in (2 * c, 2 * c + 1):
                    v = psum.take(pe, f"spm.s{b}")
                    for t in range(2):
                        ins = PE.matmul(v[:, t * S:t * S + S], spm.QT[:, tile(2 * b + t)], spm.KT[:, b * S:b * S + S],
                                        start=True, stop=True)
                    ins.then_inc(psum.filled(f"spm.s{b}"), 1)
            for b in range(NB):
                turn_probs_pe(pe, "spm", spm.Z, b, lambda b: (sig("spm.probs"), b // 2 + 1))
                pe.wait_ge(*psum.copied(f"spm.pT{b}"))
                if b % 2 == 0:
                    v = psum.take(pe, f"spm.out{b // 2}")
                for t in range(2):
                    at = tile((b % 2) * 2 + t)
                    for kt in range(2):
                        ins = PE.matmul(v[:, at], spm.PT[:, b % 2, kt, tile(t)], spm.VV[:, 2 * b + kt, :],
                                        start=kt == 0, stop=kt == 1)
                if b % 2 == 0:
                    ins.then_inc(sig("spm.half"), 1)
                else:
                    ins.then_inc(psum.filled(f"spm.out{b // 2}"), 1)
            end_pe(pe, "spm")

        def sparse_act(act):
            for c in range(NC):
                move_act(act, f"spm.q{c}", spm.QT[:, chunk(c)])
                move_act(act, f"spm.k{c}", spm.KT[:, chunk(c)])
                move_act(act, f"spm.v{c}", spm.VV[:, ctiles(c)].rearrange("p t d -> p (t d)"))
            for b in range(NB):
                act.eng.wait_ge(*psum.made(f"spm.s{b}"))
                v = psum.view(f"spm.s{b}")
                act.eng.wait_ge(sig("spm.mx"), b + 1)
                for t in range(2):
                    i = 2 * b + t
                    ins = A.activation(spm.Z[:, i], v[:, t * S:t * S + S], ACT.Identity, bias=spm.mx[:, i:i + 1],
                                       scale=D ** -0.5, accum_out=spm.sz[:, i:i + 1])
                    if t == 0:
                        ins.then_inc(act.step(), 1)
                ins.then_inc(act.read(f"spm.s{b}"), 1)
            for b in range(NB):
                if b >= 2:
                    if b % 2:
                        k, _, n = psum.place[f"spm.out{b // 2 - 1}"]
                        act.eng.wait_ge(psum.full[k], n)
                    else:
                        act.eng.wait_ge(sig("spm.half"), b // 2)
                move_act(act, f"spm.pT{b}", spm.PT[:, b % 2].rearrange("p a q -> p (a q)"))
            end_act(act, "spm")

        def sort_descending(dve, src, bufs):
            rows_of = lambda a, w: a.rearrange("p t (n w) -> p (t n) w", w=w)
            cur, k = src, 2
            other = 0
            while k <= S:
                d = k // 2
                first = True
                while d >= 1:
                    nxt = bufs[other]
                    other ^= 1
                    w = k if first else 2 * d
                    i, o = rows_of(cur, w), rows_of(nxt, w)
                    lo = i[:, :, 0:d]
                    mirror = slice(k - 1, d - 1, -1) if first else slice(d, 2 * d)
                    hi, hi_o = i[:, :, mirror], o[:, :, mirror]
                    dve.eng.wait_ge(*dve.own())
                    V.tensor_tensor(o[:, :, 0:d], lo, hi, ALU.max).then_inc(dve.step(), 1)
                    V.tensor_tensor(hi_o, lo, hi, ALU.min).then_inc(dve.step(), 1)
                    cur, first = nxt, False
                    d //= 2
                k *= 2
            return cur

        def sparse_dve(dve):
            for b in range(NB):
                dve.eng.wait_ge(*psum.made(f"spm.s{b}"))
                v = psum.view(f"spm.s{b}").rearrange("p (t k) -> p t k", t=2)
                mx = spm.mx[:, 2 * b:2 * b + 2]
                V.tensor_reduce(mx, v, AX.X, ALU.max, negate=True).then_inc(dve.step(), 1)
                dve.eng.wait_ge(*dve.own())
                V.tensor_scalar(mx, mx, D ** -0.5, None, ALU.mult).then_inc(dve.flag("spm.mx"), 1)
            for c in range(NC):
                z = spm.Z[:, ctiles(c)]
                dve.eng.wait_ge(*psum.copied(f"spm.s{2 * c}"))
                dve.eng.wait_ge(*psum.copied(f"spm.s{2 * c + 1}"))
                stp, cnt, rk, ad = (a[:, ctiles(c)] for a in (spm.stp, spm.cnt, spm.rk, spm.add_))
                V.tensor_scalar(stp, spm.sz[:, ctiles(c)], 1.0, 1.0 / S, ALU.subtract, ALU.mult).then_inc(dve.step(), 1)
                dve.eng.wait_ge(*dve.own())
                for t in range(4 * c, 4 * c + 4):
                    V.tensor_scalar(spm.SA[:, t], spm.Z[:, t], spm.stp[:, t:t + 1], None, ALU.is_gt, ALU.add,
                                            accum_out=spm.cnt[:, t:t + 1]).then_inc(dve.step(), 1)
                dve.eng.wait_ge(*dve.own())
                V.reciprocal(rk, cnt).then_inc(dve.step(), 1)
                dve.eng.wait_ge(*dve.own())
                V.tensor_tensor(ad, stp, rk, ALU.add).then_inc(dve.step(), 1)
                cur = sort_descending(dve, z, (spm.SA[:, ctiles(c)], spm.SB[:, ctiles(c)]))
                oth = spm.SA[:, ctiles(c)]
                dve.eng.wait_ge(*dve.own())
                for t in range(4):
                    V.tensor_tensor_scan(oth[:, t], cur[:, t], zeros[:], 0.0, ALU.add, ALU.add).then_inc(dve.step(), 1)
                dve.eng.wait_ge(*dve.own())
                for t in range(4):
                    V.tensor_scalar(oth[:, t], oth[:, t], spm.rk[:, 4 * c + t:4 * c + t + 1],
                                            spm.add_[:, 4 * c + t:4 * c + t + 1], ALU.mult, ALU.subtract).then_inc(dve.step(), 1)
                dve.eng.wait_ge(*dve.own())
                V.tensor_tensor(z, z, oth, ALU.subtract).then_inc(dve.step(), 1)
                dve.eng.wait_ge(*dve.own())
                V.tensor_scalar(z, z, 0.0, None, ALU.max).then_inc(dve.flag("spm.probs"), 1)
            end_dve(dve, "spm", "spm.out", X)

        def sparse_pool(pool):
            end_pool(pool, "spm")

        class lora:
            a = Carve(True)
            LZ = a(NT, 138)
            ZT = a(T)
            M8, I8, IF = a(NT, 8), a(NT, 8, dt=U32), a(NT, 8)
            G, H2, EL = a(NT, 8), a(NT, 8), a(NT, 8)
            dn, zr = a(NT), a(NT)

        def lora_pe(pe):
            w0 = W_AT["L2_ffn_gate_w"][0]
            for c in range(NC):
                x_t_ready(pe, "x2", c)
                for half in range(2):
                    v = psum.take(pe, f"lora.lz{c}{half}")
                    for t in range(2):
                        ins = PE.matmul(v[:, t * 138:t * 138 + 138], XT[:, tile(4 * c + 2 * half + t)],
                                        WS[:, w0:w0 + 138], start=True, stop=True)
                    ins.then_inc(psum.filled(f"lora.lz{c}{half}"), 1)
            for c in range(NC):
                pe.wait_ge(sig("lora.z"), c + 1)
                turn_pe(pe, "lora.z", lora.LZ[:, :, 10:138], c)
            for c in range(NC):
                pe.wait_ge(*psum.copied(f"lora.zT{c}"))
                v = psum.take(pe, f"lora.out{c}")
                for t in range(4):
                    PE.matmul(v[:, tile(t)], XT[:, tile(4 * c + t)], W("L2_ffn_base_w"), start=True, stop=False)
                    ins = PE.matmul(v[:, tile(t)], lora.ZT[:, tile(4 * c + t)], W("L2_ffn_lora_B"),
                                    start=False, stop=True)
                ins.then_inc(psum.filled(f"lora.out{c}"), 1)
            end_pe(pe, "lora")

        def lora_act(act):
            for c in range(NC):
                act.eng.wait_ge(sig("lora.shifted"), c + 1)
                A.activation(lora.EL[:, ctiles(c)], lora.EL[:, ctiles(c)], ACT.Exp).then_inc(act.flag("lora.exp"), 1)
            for c in range(NC):
                move_act(act, f"lora.zT{c}", lora.ZT[:, chunk(c)])
            end_act(act, "lora")

        def lora_dve(dve):
            for c in range(NC):
                for half in range(2):
                    dve.eng.wait_ge(*psum.made(f"lora.lz{c}{half}"))
                    v = psum.view(f"lora.lz{c}{half}")
                    t = 4 * c + 2 * half
                    V.tensor_copy(lora.LZ[:, t:t + 2], v[:, 0:276].rearrange("p (t n) -> p t n", t=2)).then_inc(dve.read(f"lora.lz{c}{half}"), 1)
                dve.eng.wait_ge(*dve.own())
                for t in range(4 * c, 4 * c + 4):
                    V.max(lora.M8[:, t], lora.LZ[:, t, 0:10]).then_inc(dve.step(), 1)
                dve.eng.wait_ge(*dve.own())
                for t in range(4 * c, 4 * c + 4):
                    V.max_index(lora.I8[:, t], lora.M8[:, t], lora.LZ[:, t, 0:10]).then_inc(dve.step(), 1)
                V.tensor_tensor(lora.EL[:, ctiles(c)], lora.LZ[:, ctiles(c), 0:8],
                                           bc(lora.M8[:, ctiles(c), 0], 2, 8), ALU.subtract).then_inc(dve.flag("lora.shifted"), 1)
                dve.eng.wait_ge(*dve.own())
                V.tensor_copy(lora.IF[:, ctiles(c)], lora.I8[:, ctiles(c)]).then_inc(dve.step(), 1)
            for c in range(NC):
                g, h2, ex = lora.G[:, ctiles(c)], lora.H2[:, ctiles(c)], bc(expert[:], 1, 4)
                dn, zr = lora.dn[:, ctiles(c)], lora.zr[:, ctiles(c)]
                dve.eng.wait_ge(*dve.own())
                V.tensor_tensor(g, ex, bc(lora.IF[:, ctiles(c), 0], 2, 8), ALU.is_equal).then_inc(dve.step(), 1)
                V.tensor_tensor(h2, ex, bc(lora.IF[:, ctiles(c), 1], 2, 8), ALU.is_equal).then_inc(dve.step(), 1)
                dve.eng.wait_ge(*dve.own())
                V.tensor_tensor(g, g, h2, ALU.add).then_inc(dve.step(), 1)
                dve.eng.wait_ge(*dve.own())
                dve.eng.wait_ge(sig("lora.exp"), c + 1)
                V.tensor_tensor(g, g, lora.EL[:, ctiles(c)], ALU.mult).then_inc(dve.step(), 1)
                dve.eng.wait_ge(*dve.own())
                V.tensor_reduce(dn, g, AX.X, ALU.add).then_inc(dve.step(), 1)
                dve.eng.wait_ge(*dve.own())
                V.tensor_scalar(zr, dn, 0.0, None, ALU.is_equal).then_inc(dve.step(), 1)
                dve.eng.wait_ge(*dve.own())
                V.tensor_tensor(dn, dn, zr, ALU.add).then_inc(dve.step(), 1)
                dve.eng.wait_ge(*dve.own())
                V.reciprocal(dn, dn).then_inc(dve.step(), 1)
                dve.eng.wait_ge(*dve.own())
                V.tensor_scalar(dn, dn, 32.0 / 16.0, None, ALU.mult).then_inc(dve.step(), 1)
                dve.eng.wait_ge(*dve.own())
                V.tensor_tensor(g, g, bc(dn, 2, 8), ALU.mult).then_inc(dve.step(), 1)
                dve.eng.wait_ge(*dve.own())
                for t in range(4 * c, 4 * c + 4):
                    z = lora.LZ[:, t, 10:138].rearrange("p (e r) -> p e r", e=8)
                    ins = V.tensor_tensor(z, z, bc(lora.G[:, t], 2, 16), ALU.mult)
                    if t % 4 < 3:
                        ins.then_inc(dve.step(), 1)
                ins.then_inc(dve.flag("lora.z"), 1)
            end_dve(dve, "lora", "lora.out", XB)

        def lora_pool(pool):
            add_bias_pool(pool, "lora", "x2", "L2_ffn_base_b")
            end_pool(pool, "lora")

        class big:
            a = Carve(False)
            QT, KT = a(8, S), a(8, S)
            Q16, K16 = a(8, S, dt=BF16), a(8, S, dt=BF16)
            VV = a(2, 8 * D)
            mx = a(2, 32)
            hl = a(2, 64, dt=BF16)
            HL = a(2 * P, dt=BF16, parts=64)
            E = a(2, 2, 2, S)
            rc = a(S)
            OT = a(8, S)
            Y = a(NT, D)

        def big_pe(pe):
            pe.wait_ge(w_loaded[6], 16)
            pe.wait_ge(sig("lora.x"), NC)
            wq = W("L3_attn_w_qkv")
            for b in range(NB):
                if b % 2 == 0:
                    x_t_ready(pe, "lora", b // 2)
                xb = XT[:, b * S:b * S + S]
                for g in range(8):
                    v = psum.take(pe, f"big.qk{b}.{g}")
                    PE.matmul(v[:, 0:S], wq[:, tile(g)], xb, start=True, stop=True)
                    ins = PE.matmul(v[:, S:2 * S], wq[:, 1024 + g * P:1024 + g * P + P], xb, start=True, stop=True)
                    ins.then_inc(psum.filled(f"big.qk{b}.{g}"), 1)
                for t in range(2):
                    for half in range(2):
                        v = psum.take(pe, f"big.v{b}.{t}{half}")
                        PE.matmul(v, XT[:, tile(2 * b + t)], wq[:, 2048 + half * CH:2048 + half * CH + CH],
                                            start=True, stop=True).then_inc(psum.filled(f"big.v{b}.{t}{half}"), 1)
                for h in range(32):
                    g, r = h // 4, slice(32 * (h % 4), 32 * (h % 4) + 32)
                    if h % 4 == 0:
                        pe.wait_ge(sig("big.k16"), 8 * b + g + 1)
                    v = psum.take(pe, f"big.m{b}.{h}")
                    for t in range(2):
                        ins = PE.matmul(v[:, t * S:t * S + S], big.Q16[r, g, tile(t)], big.K16[r, g, :],
                                        start=True, stop=True)
                    ins.then_inc(psum.filled(f"big.m{b}.{h}"), 1)
                pe.wait_ge(sig("big.shift"), b + 1)
                v = psum.take(pe, f"big.hT{b}")
                v16 = v.bitcast(BF16)
                for t in range(2):
                    ins = PE.transpose(v16[0:64, tile(t)], big.hl[:, t, :], ident16[:])
                ins.then_inc(psum.filled(f"big.hT{b}"), 1)
                pe.wait_ge(*psum.copied(f"big.hT{b}"))
                pe.wait_ge(*psum.copied(f"big.v{b}.11"))
                self_scores = lambda p: big_scores_pe(pe, b, p)
                self_scores(0)
                for p in range(16):
                    if p + 1 < 16:
                        self_scores(p + 1)
                    pe.wait_ge(*psum.copied(f"big.e{b}.{p}"))
                    g = p // 2
                    if p % 2 == 0:
                        v = psum.take(pe, f"big.o{b}.{g}")
                    for hh in range(2):
                        j = 2 * (p % 2) + hh
                        h = 4 * g + j
                        for kt in range(2):
                            PE.matmul(v[32 * j:32 * j + 32, 0:S], big.VV[:, kt, 32 * h:32 * h + 32],
                                      big.E[:, p % 2, hh, kt, :], start=kt == 0, stop=kt == 1)
                        for kt in range(2):
                            ins = PE.matmul(v[32 * j:32 * j + 32, S:2 * S], ones32[:], big.E[:, p % 2, hh, kt, :],
                                            start=kt == 0, stop=kt == 1)
                    if p % 2 == 0:
                        ins.then_inc(sig("big.half"), 1)
                    else:
                        ins.then_inc(psum.filled(f"big.o{b}.{g}"), 1)
                v = psum.take(pe, f"big.out{b}")
                for g in range(8):
                    pe.wait_ge(*psum.copied(f"big.o{b}.{g}"))
                for t in range(2):
                    for g in range(8):
                        ins = PE.matmul(v[:, tile(t)], big.OT[:, g, tile(t)], W("L3_attn_w_out")[:, tile(g)],
                                        start=g == 0, stop=g == 7)
                ins.then_inc(psum.filled(f"big.out{b}"), 1)
            end_pe(pe, "big")

        def big_scores_pe(pe, b, p):
            v = psum.take(pe, f"big.e{b}.{p}", 2)
            for hh in range(2):
                h = 2 * p + hh
                g, r = h // 4, slice(32 * (h % 4), 32 * (h % 4) + 32)
                PE.matmul(v[:, hh].rearrange("p (a q) -> p a q", a=2), pick[:, h, :], bc(big.HL[:, :], 1, 2),
                          start=True, stop=True)
                for kt in range(2):
                    ins = PE.matmul(v[:, hh, kt * S:kt * S + S], big.KT[r, g, tile(kt)], big.QT[r, g, :],
                                    start=False, stop=True, skip_group_check=True)
            ins.then_inc(psum.filled(f"big.e{b}.{p}"), 1)

        def big_act(act):
            act.eng.wait_ge(sig("lora.x"), NC)
            for b in range(NB):
                for g in range(8):
                    act.eng.wait_ge(*psum.made(f"big.qk{b}.{g}"))
                    v = psum.view(f"big.qk{b}.{g}")
                    A.copy(big.QT[:, g], v[:, 0:S]).then_inc(act.step(), 1)
                    A.copy(big.KT[:, g], v[:, S:2 * S]).then_inc(act.read(f"big.qk{b}.{g}"), 1)
                for t in range(2):
                    for half in range(2):
                        move_act(act, f"big.v{b}.{t}{half}", big.VV[:, t, half * CH:half * CH + CH])
                act.eng.wait_ge(*psum.made(f"big.hT{b}"))
                v = psum.view(f"big.hT{b}").bitcast(BF16)
                A.copy(big.HL, v[0:64, 0:2 * P]).then_inc(act.read(f"big.hT{b}"), 1)
                for p in range(16):
                    act.eng.wait_ge(*psum.made(f"big.e{b}.{p}"))
                    v = psum.view(f"big.e{b}.{p}")
                    if p % 2 == 0 and (p or b):
                        act.eng.wait_ge(sig("big.half"), 8 * b + p // 2)
                    elif p >= 2 or b:
                        k, _, n = psum.place[f"big.o{b}.{p // 2 - 1}" if p >= 2 else f"big.o{b - 1}.7"]
                        act.eng.wait_ge(psum.full[k], n)
                    A.activation(big.E[:, p % 2].rearrange("p a b q -> p a (b q)"), v, ACT.Exp,
                                           scale=32 ** -0.5).then_inc(act.read(f"big.e{b}.{p}"), 1)
            end_act(act, "big")

        def big_dve(dve):
            dve.eng.wait_ge(sig("lora.x"), NC)
            for b in range(NB):
                for g in range(8):
                    dve.eng.wait_ge(*psum.copied(f"big.qk{b}.{g}"))
                    V.tensor_copy(big.Q16[:, g], big.QT[:, g]).then_inc(dve.step(), 1)
                    V.tensor_copy(big.K16[:, g], big.KT[:, g]).then_inc(dve.flag("big.k16"), 1)
                for h in range(32):
                    dve.eng.wait_ge(*psum.made(f"big.m{b}.{h}"))
                    v = psum.view(f"big.m{b}.{h}").rearrange("p (t k) -> p t k", t=2)
                    V.tensor_reduce(big.mx[:, :, h], v, AX.X, ALU.max, negate=True).then_inc(dve.read(f"big.m{b}.{h}"), 1)
                dve.eng.wait_ge(*dve.own())
                V.tensor_copy(big.hl[:, :, 0:32], big.mx).then_inc(dve.step(), 1)
                dve.eng.wait_ge(*dve.own())
                V.tensor_tensor(big.hl[:, :, 32:64], big.mx, big.hl[:, :, 0:32], ALU.subtract).then_inc(dve.flag("big.shift"), 1)
                for g in range(8):
                    dve.eng.wait_ge(*psum.made(f"big.o{b}.{g}"))
                    v = psum.view(f"big.o{b}.{g}")
                    dve.eng.wait_ge(*dve.own())
                    V.reciprocal(big.rc, v[:, S:2 * S]).then_inc(dve.step(), 1)
                    dve.eng.wait_ge(*dve.own())
                    V.tensor_tensor(big.OT[:, g], v[:, 0:S], big.rc, ALU.mult).then_inc(dve.read(f"big.o{b}.{g}"), 1)
                dve.eng.wait_ge(*psum.made(f"big.out{b}"))
                v = psum.view(f"big.out{b}")[:, 0:2 * P].rearrange("p (t d) -> p t d", t=2)
                V.tensor_tensor(R[:, 2 * b:2 * b + 2], v, bc(row("L3_attn_b_out"), 1, 2), ALU.add).then_inc(dve.read(f"big.out{b}"), 1)
            for c in range(NC):
                norm_stats(dve, c, R[:, ctiles(c)], "bign", 1e-6)
            for c in range(NC):
                y, r = big.Y[:, ctiles(c)], R[:, ctiles(c)]
                norm_apply(dve, c, r, y, "bign")
                dve.eng.wait_ge(*dve.own())
                V.tensor_tensor(y, y, bc(row("L3_attn_ln_gamma"), 1, 4), ALU.mult).then_inc(dve.step(), 1)
                dve.eng.wait_ge(*dve.own())
                V.tensor_tensor(y, y, bc(row("L3_attn_ln_beta"), 1, 4), ALU.add).then_inc(dve.step(), 1)
                dve.eng.wait_ge(*dve.own())
                V.tensor_tensor(r, y, X[:, ctiles(c)], ALU.add).then_inc(dve.step(), 1)
            end_dve(dve, "big")

        def big_pool(pool):
            for c in range(NC):
                norm_rstd(pool, c, "bign")
            end_pool(pool, "big")

        def absmax_dve(dve):
            for c in range(NC):
                norm_stats(dve, c, X[:, ctiles(c)], "fin", EPS)
            for c in range(NC):
                y = R[:, ctiles(c)]
                normed_dve(dve, c, X[:, ctiles(c)], y, "fin")
                dve.eng.wait_ge(*dve.own())
                V.tensor_reduce(ABSMAX[:, bass.ds(step * NT + 4 * c, 4)], y, AX.X, ALU.max,
                                        apply_absolute_value=True).then_inc(dve.step(), 1)
                V.tensor_copy(XALL[:, bass.ds(step * NT + 4 * c, 4), :], X[:, ctiles(c)]).then_inc(dve.step(), 1)

        def normed_dve(dve, c, src, y, name):
            norm_apply(dve, c, src, y, name)
            dve.eng.wait_ge(*dve.own())
            V.tensor_tensor(y, y, bc(row("L3_ffn_gamma"), 1, 4), ALU.mult).then_inc(dve.step(), 1)
            dve.eng.wait_ge(*dve.own())
            V.tensor_tensor(y, y, bc(row("L3_ffn_beta"), 1, 4), ALU.add).then_inc(dve.step(), 1)

        def absmax_pool(pool):
            for c in range(NC):
                norm_rstd(pool, c, "fin")


        NCH = B // 2

        class last:
            a = Carve(False)
            amax, scale, inv, f = a(1), a(1), a(1), a(1)
            wsum, wtot, delta, ndelta = a(1), a(1), a(1), a(1)
            tern, neg, aw = a(D), a(D), a(D)
            sums, tots = a(2), a(2)
            tern16 = a(D, dt=BF16)
            Q = a(2, 4, D)
            Q16 = a(NCH, 4, D, dt=BF16)
            QT = a(NCH, 4 * P, dt=BF16)
            RR = a(NCH, 4, D)
            OUT = a(NCH, 4, D)

        def last_ffn():
            ROUND = 1.5 * 2.0 ** 23
            RMAX, RADD = bass.bass_isa.ReduceOp.max, bass.bass_isa.ReduceOp.add
            psum.reset()
            with nc.Block(no_gpsimd_drain=True) as block:
                @block.tensor
                def _(pe):
                    for c in range(NCH):
                        pe.wait_ge(sig("last.q"), c + 1)
                        v = psum.take(pe, f"last.qT{c}").bitcast(BF16)
                        for t in range(4):
                            ins = PE.transpose(v[:, tile(t)], last.Q16[:, c, t], ident16[:])
                        ins.then_inc(psum.filled(f"last.qT{c}"), 1)
                    pe.wait_ge(sig("last.tern16"), 1)
                    for c in range(NCH):
                        pe.wait_ge(*psum.copied(f"last.qT{c}"))
                        v = psum.take(pe, f"last.y{c}")
                        for t in range(4):
                            ins = PE.matmul(v[:, tile(t)], last.QT[:, c, tile(t)], last.tern16, start=True, stop=True)
                        ins.then_inc(psum.filled(f"last.y{c}"), 1)

                @block.gpsimd
                def _(eng):
                    pool = Own(eng, pool_step, psum, sig)
                    eng.wait_ge(sig("last.rowmax"), 1)
                    G.partition_all_reduce(last.scale, last.amax, P, RMAX).then_inc(pool.flag("last.max"), 1)
                    eng.wait_ge(sig("last.wrows"), 1)
                    G.partition_all_reduce(last.wtot, last.wsum, P, RADD).then_inc(pool.flag("last.wsum"), 1)
                    eng.wait_ge(sig("last.sums"), 1)
                    G.partition_all_reduce(last.tots, last.sums, P, RADD).then_inc(pool.flag("last.tots"), 1)
                    for c in range(NCH):
                        norm_rstd(pool, c, "fin")
                    for c in range(NCH):
                        norm_rstd(pool, c, "last")

                @block.vector
                def _(eng):
                    dve = Own(eng, dve_step, psum, sig)
                    w = W("L3_ffn_weight")
                    V.tensor_reduce(last.amax, ABSMAX[:], AX.X, ALU.max).then_inc(dve.flag("last.rowmax"), 1)
                    V.tensor_reduce(last.wsum, w, AX.X, ALU.add, apply_absolute_value=True).then_inc(dve.flag("last.wrows"), 1)
                    eng.wait_ge(sig("last.wsum"), 1)
                    V.tensor_scalar(last.delta, last.wtot, 1.0 / (D * D), 0.7, ALU.mult, ALU.mult).then_inc(dve.step(), 1)
                    dve.eng.wait_ge(*dve.own())
                    V.tensor_scalar(last.ndelta, last.delta, -1.0, None, ALU.mult).then_inc(dve.step(), 1)
                    V.tensor_scalar(last.tern, w, last.delta, None, ALU.is_gt).then_inc(dve.step(), 1)
                    dve.eng.wait_ge(*dve.own())
                    V.tensor_scalar(last.neg, w, last.ndelta, None, ALU.is_lt).then_inc(dve.step(), 1)
                    dve.eng.wait_ge(*dve.own())
                    V.tensor_tensor(last.tern, last.tern, last.neg, ALU.subtract).then_inc(dve.step(), 1)
                    dve.eng.wait_ge(*dve.own())
                    V.tensor_copy(last.tern16, last.tern).then_inc(dve.flag("last.tern16"), 1)
                    V.tensor_tensor(last.aw, last.tern, w, ALU.mult).then_inc(dve.step(), 1)
                    V.tensor_reduce(last.sums[:, 1:2], last.tern, AX.X, ALU.add, apply_absolute_value=True).then_inc(dve.step(), 1)
                    dve.eng.wait_ge(*dve.own())
                    V.tensor_reduce(last.sums[:, 0:1], last.aw, AX.X, ALU.add).then_inc(dve.flag("last.sums"), 1)
                    eng.wait_ge(sig("last.tots"), 1)
                    V.tensor_scalar(last.tots[:, 1:2], last.tots[:, 1:2], 1.0, None, ALU.max).then_inc(dve.step(), 1)
                    eng.wait_ge(sig("last.max"), 1)
                    V.tensor_scalar(last.scale, last.scale, 1e-8, 1.0 / 127, ALU.max, ALU.mult).then_inc(dve.step(), 1)
                    dve.eng.wait_ge(*dve.own())
                    V.reciprocal(last.inv, last.scale).then_inc(dve.step(), 1)
                    V.reciprocal(last.f, last.tots[:, 1:2]).then_inc(dve.step(), 1)
                    dve.eng.wait_ge(*dve.own())
                    V.tensor_tensor(last.f, last.f, last.tots[:, 0:1], ALU.mult).then_inc(dve.step(), 1)
                    dve.eng.wait_ge(*dve.own())
                    V.tensor_tensor(last.f, last.f, last.scale, ALU.mult).then_inc(dve.step(), 1)
                    for c in range(NCH):
                        norm_stats(dve, c, XALL[:, ctiles(c)], "fin", EPS)
                    for c in range(NCH):
                        q = last.Q[:, c % 2]
                        normed_dve(dve, c, XALL[:, ctiles(c)], q, "fin")
                        dve.eng.wait_ge(*dve.own())
                        V.tensor_scalar(q, q, last.inv, 127.0, ALU.mult, ALU.min).then_inc(dve.step(), 1)
                        dve.eng.wait_ge(*dve.own())
                        V.tensor_scalar(q, q, -127.0, ROUND, ALU.max, ALU.add).then_inc(dve.step(), 1)
                        dve.eng.wait_ge(*dve.own())
                        V.tensor_scalar(last.Q16[:, c], q, ROUND, None, ALU.subtract).then_inc(dve.flag("last.q"), 1)
                    for c in range(NCH):
                        eng.wait_ge(*psum.made(f"last.y{c}"))
                        v = psum.view(f"last.y{c}")
                        V.scalar_tensor_tensor(last.RR[:, c].rearrange("p t d -> p (t d)"), v, last.f,
                                                         XALL[:, ctiles(c)].rearrange("p t d -> p (t d)"),
                                                         ALU.mult, ALU.add).then_inc(dve.read(f"last.y{c}"), 1)
                        norm_stats(dve, c, last.RR[:, c], "last", EPS)
                    for c in range(NCH):
                        norm_apply(dve, c, last.RR[:, c], last.OUT[:, c], "last", "last.out")

                @block.scalar
                def _(eng):
                    act = Own(eng, act_step, psum, sig)
                    for c in range(NCH):
                        eng.wait_ge(*psum.made(f"last.qT{c}"))
                        v = psum.view(f"last.qT{c}").bitcast(BF16)
                        A.copy(last.QT[:, c], v[:, 0:4 * P]).then_inc(act.read(f"last.qT{c}"), 1)

                @block.sync
                def _(sp):
                    for c in range(NCH):
                        sp.wait_ge(sig("last.out"), c + 1)
                        sp.dma_start(out[:, ctiles(c), :], last.OUT[:, c]).then_inc(x_stored, 16)
                    sp.wait_ge(x_stored, 16 * NCH)

        LOADS = 6

        def clear_counts():
            counts = sorted(s.num for s in bank_full + bank_read + [pe_step, dve_step, act_step, pool_step, loaded]
                            + list(signals.values()))
            assert counts == list(range(counts[0], counts[-1] + 1))
            nc.sync.sem_clear(range(counts[0], counts[-1] + 1))
            nc.all_engine_barrier(sem_only=True)

        x0 = Cross("x0", "L0_xattn", "ret", True, 0, KEEP0, 0)
        moe0 = Moe("moe0", "L0_ffn", "x0", False, 1, 2, 4, 0, True)
        moe1 = Moe("moe1", "L1_ffn", "one", True, 4, 4, 2, 1, False)
        x2 = Cross("x2", "L2_xattn", "spm", True, 5, None, 0)
        x3 = Cross("x3", "L3_xattn", "big", True, 6, KEEP3, 1, waits_all=True)

        with nc.Fori(0, STEPS) as step:
            with nc.Block(no_gpsimd_drain=True) as block:
                @block.sync
                def _(sp):
                    sp.dma_start(X[:], x[:, bass.ds(step * NT, NT), :]).then_inc(loaded, 16)
                    sp.dma_start(XT[:], x_t[:, bass.ds(step * T, T)]).then_inc(loaded, 16)
                    sp.dma_start(CT[:], ctx_t[:, bass.ds(step * NB, NB), :]).then_inc(loaded, 16)
                    sp.dma_start(CD[:], ctx_d[:, bass.ds(step * NB, NB), :]).then_inc(loaded, 16)
                    sp.dma_start(KEEP0[:], keep0[bass.ds(step * NB, NB), :].partition_broadcast(P)).then_inc(loaded, 16)
                    sp.dma_start(KEEP3[:], keep3[bass.ds(step * NB, NB), :].partition_broadcast(P)).then_inc(loaded, 16)

                @block.tensor
                def _(eng):
                    retention_pe(eng)
                    x0.pe(eng)
                    moe0.pe(eng)
                    cosine_pe(eng)
                    one_pe(eng)
                    moe1.pe(eng)
                    sparse_pe(eng)
                    x2.pe(eng)
                    lora_pe(eng)
                    big_pe(eng)
                    x3.pe(eng)

                @block.scalar
                def _(eng):
                    act = Own(eng, act_step, psum, sig)
                    retention_act(act)
                    x0.act(act)
                    moe0.act(act)
                    cosine_act(act)
                    one_act(act)
                    moe1.act(act)
                    sparse_act(act)
                    x2.act(act)
                    lora_act(act)
                    big_act(act)
                    x3.act(act)

                @block.vector
                def _(eng):
                    eng.wait_ge(loaded, LOADS * 16)
                    dve = Own(eng, dve_step, psum, sig)
                    retention_dve(dve)
                    x0.dve(dve)
                    moe0.dve(dve)
                    cosine_dve(dve)
                    one_dve(dve)
                    moe1.dve(dve)
                    sparse_dve(dve)
                    x2.dve(dve)
                    lora_dve(dve)
                    big_dve(dve)
                    x3.dve(dve)
                    absmax_dve(dve)

                @block.gpsimd
                def _(eng):
                    pool = Own(eng, pool_step, psum, sig)
                    retention_pool(pool)
                    x0.pool(pool)
                    moe0.pool(pool)
                    cosine_pool(pool)
                    one_pool(pool)
                    moe1.pool(pool)
                    sparse_pool(pool)
                    x2.pool(pool)
                    lora_pool(pool)
                    big_pool(pool)
                    x3.pool(pool)
                    absmax_pool(pool)
            clear_counts()

        last_ffn()


def kernel(**inputs):
    import numpy as _np
    import concourse.bacc as _bacc
    from concourse import mybir as _mybir
    from concourse.bass_utils import run_bass_kernel_spmd as _run

    i = {n: _np.asarray(a) for n, a in inputs.items()}
    blocks = lambda w, j: w.reshape(j, 128, -1).transpose(1, 0, 2).reshape(128, -1)
    experts_in = lambda w: w.transpose(1, 0, 2).reshape(128, -1)
    experts_out = lambda w: blocks(w.reshape(-1, 128), w.shape[0] * w.shape[1] // 128)
    turned = {"L0_xattn_Wq", "L0_xattn_Wk", "L0_xattn_Wv", "L0_xattn_Wo", "L1_attn_Wq", "L1_attn_Wk", "L1_attn_Wv",
              "L1_attn_W1", "L1_attn_W2", "L2_attn_Wq", "L2_attn_Wk", "L2_attn_Wv", "L2_ffn_gate_w", "L2_ffn_base_w",
              "L3_xattn_Wq", "L3_xattn_Wk", "L3_xattn_Wv", "L3_xattn_Wo", "L3_ffn_weight"}

    def laid(n):
        w = i[n]
        if n in turned:
            return w.T
        if n in ("L0_ffn_W1", "L1_ffn_W1"):
            return experts_in(w)
        if n in ("L0_ffn_W2", "L1_ffn_W2"):
            return experts_out(w)
        if n == "L1_attn_W3":
            return blocks(w.T, 4)
        if n == "L3_attn_w_out":
            return blocks(w, 8)
        if n == "L2_ffn_lora_A":
            return w.reshape(128, 128).T
        if n == "L2_ffn_lora_B":
            return w.transpose(0, 2, 1).reshape(128, 128)
        return w

    weights = _np.concatenate([laid(n) for cols in W_COLS for n, _ in cols], axis=1)
    bcols = _np.concatenate([i[n].reshape(-1, 128).T for n, _ in B_COLS], axis=1)
    rows = _np.concatenate([i[n].reshape(-1) for n, _ in ROWS])
    ctx_t = i["ctx_1024"].transpose(2, 0, 1)
    arrays = {
        "x": i["x"].reshape(B * S // 128, 128, D).transpose(1, 0, 2),
        "x_t": i["x"].reshape(B * S, D).T,
        "ctx_t": ctx_t,
        "ctx_d": _np.concatenate([ctx_t, ctx_t], axis=2),
        "keep0": i["mask_BxS2_ik0"],
        "keep3": i["mask_BxS2_bf1"].view(_np.uint8),
        "weights": weights, "bcols": bcols, "rows": rows,
        "b2s": _np.stack([i["L0_ffn_b2"], i["L1_ffn_b2"]]),
    }
    nc = _bacc.Bacc("TRN2", target_bir_lowering=False, num_devices=1)
    args = []
    for name in arrays:
        arrays[name] = _np.ascontiguousarray(arrays[name])
        a = arrays[name]
        args.append(nc.dram_tensor(f"in_{name}", a.shape, _mybir.dt.from_np(a.dtype), kind="ExternalInput").ap())
    args.append(nc.dram_tensor("out_0_dram", (P, B * S // P, D), F32, kind="ExternalOutput").ap())
    decoder(nc, *args)
    r = _run(nc, [{f"in_{n}": a for n, a in arrays.items()}], core_ids=[0])
    return r.results[0]["out_0_dram"].transpose(1, 0, 2).reshape(B, S, D)
```

```python
import numpy as np
import concourse.bass as bass
from concourse import mybir
from contextlib import ExitStack

ALU = mybir.AluOpType
ACT = mybir.ActivationFunctionType
AX = mybir.AxisListType
F32 = mybir.dt.float32
BF16 = mybir.dt.bfloat16
I32 = mybir.dt.int32
U32 = mybir.dt.uint32
U8 = mybir.dt.uint8

B, S, D, SK = 8, 256, 128, 64
P = 128
BATCHES_PER_STEP = 4
NB = BATCHES_PER_STEP
STEPS = B // NB
NC = NB // 2
T = NB * S
NT = T // P
CH = 512
EPS = 1e-5

W_COLS = [
    [("L0_attn_Wq", 128), ("L0_attn_Wk", 128), ("L0_attn_Wv", 128), ("L0_attn_W_G", 128), ("L0_attn_W_O", 128),
     ("L0_xattn_Wq", 128), ("L0_xattn_Wk", 128), ("L0_xattn_Wv", 128), ("L0_xattn_Wo", 128), ("L0_ffn_Wr", 8)],
    [("L0_ffn_W1", 8 * 512)],
    [("L0_ffn_W2", 32 * 128)],
    [("L1_attn_Wq", 128), ("L1_attn_Wk", 128), ("L1_attn_Wv", 128), ("L1_attn_W1", 128), ("L1_attn_W2", 512),
     ("L1_attn_W3", 512), ("L1_xattn_key_matrix", 128), ("L1_xattn_value_matrix", 128), ("L1_ffn_Wr", 8)],
    [("L1_ffn_W1", 8 * 256), ("L1_ffn_W2", 16 * 128)],
    [("L2_attn_Wq", 128), ("L2_attn_Wk", 128), ("L2_attn_Wv", 128),
     ("L2_xattn_Wq", 128), ("L2_xattn_Wk", 128), ("L2_xattn_Wv", 128), ("L2_xattn_Wo", 128),
     ("L2_ffn_gate_w", 10), ("L2_ffn_lora_A", 128), ("L2_ffn_lora_B", 128), ("L2_ffn_base_w", 128)],
    [("L3_attn_w_qkv", 3072), ("L3_attn_w_out", 1024),
     ("L3_xattn_Wq", 128), ("L3_xattn_Wk", 128), ("L3_xattn_Wv", 128), ("L3_xattn_Wo", 128),
     ("L3_ffn_weight", 128)],
]
W_AT, W_GROUP, _at = {}, {}, 0
GROUP_AT = []
for _g, _cols in enumerate(W_COLS):
    GROUP_AT.append(_at)
    for _n, _w in _cols:
        W_AT[_n], W_GROUP[_n] = (_at, _w), _g
        _at += _w
GROUP_AT.append(_at)
W_TOTAL = _at
B_COLS = [("L0_xattn_bq", 1), ("L0_xattn_bk", 1), ("L0_ffn_b1", 32), ("L1_attn_b1", 1), ("L1_attn_b2", 4),
          ("L1_ffn_b1", 16), ("L2_xattn_bq", 1), ("L2_xattn_bk", 1), ("L3_xattn_bq", 1), ("L3_xattn_bk", 1)]
ROWS = [("L0_xattn_bv", 128), ("L0_xattn_bo", 128), ("L0_ffn_br", 8), ("L1_attn_bq", 128), ("L1_attn_bk", 128),
        ("L1_attn_bv", 128), ("L1_attn_b3", 128), ("L1_ffn_br", 8), ("L2_xattn_bv", 128), ("L2_xattn_bo", 128),
        ("L2_ffn_base_b", 128), ("L3_attn_b_out", 128), ("L3_attn_ln_gamma", 128), ("L3_attn_ln_beta", 128),
        ("L3_xattn_bv", 128), ("L3_xattn_bo", 128), ("L3_ffn_gamma", 128), ("L3_ffn_beta", 128)]


def spots(cols):
    at, out = 0, {}
    for n, w in cols:
        out[n] = (at, w)
        at += w
    return out, at


B_AT, B_TOTAL = spots(B_COLS)
R_AT, R_TOTAL = spots(ROWS)

GAMMA = [1.0 - 2.0 ** (-5.0 - h) for h in range(8)]


def bf16_parts(value):
    parts = []
    for _ in range(3):
        part = (np.array(value, np.float32).view(np.uint32) & np.uint32(0xFFFF0000)).view(np.float32)
        parts.append(float(part))
        value = value - float(part)
    assert value == 0
    return parts


class Psum:

    def __init__(self, banks, full, read):
        self.banks, self.full, self.read_ = banks, full, read
        self.reset()

    def reset(self):
        self.next, self.place, self.uses, self.last, self.open = 0, {}, [0] * 8, [None] * 8, set()

    def take(self, pe, name, n=1):
        k = self.next
        while k + n > 8 or any(self.last[j] in self.open for j in range(k, k + n)):
            k = 0 if k + n > 8 else k + 1
        self.next = (k + n) % 8
        for old in {self.last[j] for j in range(k, k + n)} - {None}:
            first, count = self.place[old][0], self.place[old][2]
            pe.wait_ge(self.read_[first], count)
        self.uses[k] += 1
        self.place[name] = (k, n, self.uses[k])
        self.open.add(name)
        for j in range(k, k + n):
            self.last[j] = name
        return self.view(name)

    def view(self, name):
        k, n, _ = self.place[name]
        return self.banks[:, k] if n == 1 else self.banks[:, k:k + n]

    def filled(self, name):
        self.open.discard(name)
        return self.full[self.place[name][0]]

    def made(self, name):
        k, _, count = self.place[name]
        return self.full[k], count

    def copied(self, name):
        k, _, count = self.place[name]
        return self.read_[k], count


class Own:

    def __init__(self, eng, step_sem, psum, sig):
        self.eng, self.step_sem, self.psum, self.sig = eng, step_sem, psum, sig
        self.count, self.last = {}, (step_sem, 0)

    def _next(self, sem, name):
        self.count[name] = self.count.get(name, 0) + 1
        self.last = (sem, self.count[name])
        return sem

    def step(self):
        return self._next(self.step_sem, "step")

    def flag(self, name):
        return self._next(self.sig(name), name)

    def read(self, product):
        self.last = self.psum.copied(product)
        return self.last[0]

    def own(self):
        return self.last


def decoder(nc, x, x_t, ctx_t, ctx_d, keep0, keep3, weights, bcols, rows, b2s, out):
    ctx = ExitStack()
    with ctx:
        sb = lambda n, s, d=F32: ctx.enter_context(nc.sbuf_tensor(n, s, d))
        sem = lambda n: ctx.enter_context(nc.semaphore(n))

        w_loaded = [sem(f"w_loaded{g}") for g in range(len(W_COLS))]
        small_loaded, consts_made, x_stored = sem("small_loaded"), sem("consts_made"), sem("x_stored")
        setup_step, parity_made = sem("setup_step"), sem("parity_made")
        bank_full = [sem(f"bank_full{k}") for k in range(8)]
        bank_read = [sem(f"bank_read{k}") for k in range(8)]
        pe_step, dve_step, act_step, pool_step = (sem(n) for n in ("pe_step", "dve_step", "act_step", "pool_step"))
        loaded = sem("loaded")
        signals = {}

        def sig(name):
            if name not in signals:
                signals[name] = sem(name)
            return signals[name]

        psum = Psum(ctx.enter_context(nc.psum_tensor("banks", [P, 8, CH], F32)), bank_full, bank_read)

        WS = sb("WS", [P, W_TOTAL])
        W = lambda n: WS[:, W_AT[n][0]:W_AT[n][0] + W_AT[n][1]]
        BC = sb("BC", [P, B_TOTAL])
        bcol = lambda n, j=0: BC[:, B_AT[n][0] + j:B_AT[n][0] + j + 1]
        RW = sb("RW", [P, R_TOTAL])
        row = lambda n: RW[:, R_AT[n][0]:R_AT[n][0] + R_AT[n][1]]
        B2 = sb("B2", [8, 2, D])
        ident = sb("ident", [P, P])
        ident16 = sb("ident16", [P, P], BF16)
        ones16 = sb("ones16", [P, P], BF16)
        ones32 = sb("ones32", [P, 32])
        decay = sb("decay", [P, 8, S])
        head_of8 = sb("head_of8", [P, 16])
        parity16 = sb("parity16", [P, 2])
        shift_parts = sb("shift_parts", [P, 2, 2, 4, 32], BF16)
        head_of4 = sb("head_of4", [P, 4])
        pick = sb("pick", [P, 4, P], BF16)
        fills = sb("fills", [3, 2])
        expert = sb("expert", [P, 8])
        minus_half = sb("minus_half", [P, 32])
        zeros = sb("zeros", [P, S])
        XALL = sb("XALL", [P, B * S // P, D])
        ABSMAX = sb("ABSMAX", [P, B * S // P])

        X = sb("X", [P, NT, D])
        R = sb("R", [P, NT, D])
        XB = sb("XB", [P, NT, D])
        XT = sb("XT", [P, T])
        CT = sb("CT", [P, NB, SK])
        CD = sb("CD", [P, NB, 2 * SK])
        KEEP0 = sb("KEEP0", [P, NB, SK], I32)
        KEEP3 = sb("KEEP3", [P, NB, SK], U8)
        st = sb("st", [P, 16, 6])
        mv = sb("mv", [P, 16, 2])
        var = sb("var", [P, 16])
        rstd = sb("rstd", [P, 16])
        ARENA = (nc.sbuf_bytes_remaining - 64) // 4
        arena = sb("arena", [P, ARENA])

        class Carve:

            def __init__(self, top):
                self.top, self.at = top, ARENA if top else 0

            def __call__(self, *shape, dt=F32, parts=P):
                n = int(np.prod(shape))
                words = n if dt in (F32, I32, U32) else (n + 1) // 2
                if self.top:
                    self.at -= words
                a = arena[0:parts, self.at:self.at + words]
                if not self.top:
                    self.at += words
                assert 0 <= self.at <= ARENA, (self.at, shape)
                if dt not in (F32,):
                    a = a.bitcast(dt)
                if len(shape) > 1:
                    names = "abcd"[:len(shape)]
                    a = a.rearrange(f"p ({' '.join(names)}) -> p {' '.join(names)}", **dict(zip(names, shape)))
                return a

        def bc(ap, axis, n):
            a = ap.unsqueeze(axis)
            shape = list(a.shape)
            shape[axis] = n
            return a.broadcast_to(shape)

        tile = lambda t: slice(t * P, (t + 1) * P)
        chunk = lambda c: slice(c * CH, (c + 1) * CH)
        ctiles = lambda c: slice(4 * c, 4 * c + 4)

        with nc.Block(no_gpsimd_drain=True) as block:
            @block.sync
            def _(sp):
                sp.dma_start(RW[:], rows.partition_broadcast(P)).then_inc(small_loaded, 16)
                sp.dma_start(BC[:], bcols).then_inc(small_loaded, 16)
                sp.dma_start(B2[:], b2s.rearrange("l e d -> e l d")).then_inc(small_loaded, 16)
                for g in range(len(W_COLS)):
                    a, b = GROUP_AT[g], GROUP_AT[g + 1]
                    sp.dma_start(WS[:, a:b], weights[:, a:b]).then_inc(w_loaded[g], 16)

            @block.gpsimd
            def _(pool):
                pool.memset(ident[:], 0.0).then_inc(setup_step, 1)
                pool.memset(head_of8[:], 1.0).then_inc(setup_step, 1)
                pool.memset(parity16[:], 0.0).then_inc(setup_step, 1)
                pool.memset(shift_parts[:], 0.0).then_inc(setup_step, 1)
                pool.memset(ones32[:], 1.0).then_inc(setup_step, 1)
                pool.memset(minus_half[:], -0.5).then_inc(setup_step, 1)
                pool.memset(zeros[:], 0.0).then_inc(setup_step, 1)
                pool.iota(expert[:], [[1, 8]], base=0, channel_multiplier=0,
                          allow_small_or_imprecise_dtypes=True).then_inc(setup_step, 1)
                for h in range(8):
                    pool.iota(decay[:, h, :], [[1, S]], base=0, channel_multiplier=-1,
                              allow_small_or_imprecise_dtypes=True).then_inc(setup_step, 1)
                pool.memset(fills[:], 0.0).then_inc(setup_step, 1)
                pool.memset(ones16[:], 1.0).then_inc(setup_step, 1)
                pool.wait_ge(setup_step, 18)
                pool.affine_select(ident[:], ident[:], pattern=[[-1, P]], compare_op=ALU.not_equal, fill=1.0,
                                   base=0, channel_multiplier=1).then_inc(setup_step, 1)
                pool.wait_ge(setup_step, 19)
                pool.affine_select(head_of8[:], head_of8[:], pattern=[[-8, 16]], compare_op=ALU.is_ge, fill=0.0,
                                   base=0, channel_multiplier=1).then_inc(setup_step, 1)
                pool.wait_ge(setup_step, 20)
                pool.affine_select(head_of8[:], head_of8[:], pattern=[[8, 16]], compare_op=ALU.is_ge, fill=0.0,
                                   base=7, channel_multiplier=-1).then_inc(setup_step, 1)
                pool.tensor_copy(ident16[:], ident[:]).then_inc(setup_step, 1)
                for col, value in enumerate((1e9, 1e8)):
                    for j, part in enumerate(bf16_parts(value)):
                        pool.wait_ge(setup_step, 22 + 3 * col + j)
                        pool.affine_select(fills[:, col:col + 1], fills[:, col:col + 1], pattern=[[0, 1]],
                                           compare_op=ALU.not_equal, fill=part, base=-j,
                                           channel_multiplier=1).then_inc(setup_step, 1)
                pool.wait_ge(consts_made, 8)
                for h in range(8):
                    pool.affine_select(decay[:, h, :], decay[:, h, :], pattern=[[1, S]], compare_op=ALU.is_ge,
                                       fill=0.0, base=0, channel_multiplier=-1).then_inc(setup_step, 1)
                pool.wait_ge(setup_step, 36)

            @block.scalar
            def _(act):
                act.wait_ge(setup_step, 17)
                for h in range(8):
                    nc.scalar.activation(decay[:, h, :], decay[:, h, :], ACT.Exp,
                                         scale=float(np.log(GAMMA[h]))).then_inc(consts_made, 1)

            @block.vector
            def _(dve):
                dve.wait_ge(setup_step, 22)
                h4 = head_of8[:].rearrange("p (a b c) -> p b a c", a=4, b=2, c=2)
                nc.vector.tensor_reduce(parity16[:], h4, AX.XY, ALU.add).then_inc(parity_made, 1)
                h4 = head_of8[:].rearrange("p (h b) -> p h b", b=4)
                nc.vector.tensor_reduce(head_of4[:], h4, AX.X, ALU.add).then_inc(parity_made, 1)
                dve.wait_ge(parity_made, 2)
                nc.vector.tensor_copy(pick[:], bc(head_of4[:], 2, P)).then_inc(parity_made, 1)
                dve.wait_ge(small_loaded, 48)

        V, A, G, PE = nc.vector, nc.scalar, nc.gpsimd, nc.tensor


        def norm_stats(dve, c, src, name, eps):
            dve.eng.wait_ge(*dve.own())
            for t in range(4):
                V.bn_stats(st[:, 4 * c + t, :], src[:, t, :]).then_inc(dve.step(), 1)
            dve.eng.wait_ge(*dve.own())
            for t in range(4):
                V.bn_aggr(mv[:, 4 * c + t, :], st[:, 4 * c + t, :]).then_inc(dve.step(), 1)
            dve.eng.wait_ge(*dve.own())
            V.tensor_scalar(var[:, ctiles(c)], mv[:, ctiles(c), 1], eps, None, ALU.add).then_inc(dve.flag(name + ".var"), 1)

        def norm_rstd(pool, c, name):
            pool.eng.wait_ge(sig(name + ".var"), c + 1)
            G.tensor_tensor(rstd[:, ctiles(c)], var[:, ctiles(c)], minus_half[:, 0:4], ALU.pow).then_inc(pool.flag(name + ".rstd"), 1)

        def norm_apply(dve, c, src, dst, name, ready=None):
            dve.eng.wait_ge(sig(name + ".rstd"), c + 1)
            for t in range(4):
                i = 4 * c + t
                ins = V.tensor_scalar(dst[:, t, :], src[:, t, :], mv[:, i, 0:1], rstd[:, i:i + 1],
                                      ALU.subtract, ALU.mult)
                if t == 3 and ready:
                    ins.then_inc(dve.flag(ready), 1)
                else:
                    ins.then_inc(dve.step(), 1)

        def end_sum_dve(dve, L, c, product=None, base=None):
            if product:
                if base is XB:
                    dve.eng.wait_ge(sig(L + ".xb"), c + 1)
                dve.eng.wait_ge(*psum.made(f"{product}{c}"))
                ps = psum.view(f"{product}{c}")
                V.tensor_tensor(R[:, ctiles(c)], ps.rearrange("p (t d) -> p t d", t=4),
                                base[:, ctiles(c)], ALU.add).then_inc(dve.read(f"{product}{c}"), 1)
            norm_stats(dve, c, R[:, ctiles(c)], L, EPS)

        def end_norm_dve(dve, L, c):
            norm_apply(dve, c, R[:, ctiles(c)], X[:, ctiles(c)], L, L + ".x")

        def end_dve(dve, L, product=None, base=None):
            for c in range(NC):
                end_sum_dve(dve, L, c, product, base)
            for c in range(NC):
                end_norm_dve(dve, L, c)

        def end_pool(pool, L):
            for c in range(NC):
                norm_rstd(pool, c, L)

        def end_pe(pe, L, c):
            pe.wait_ge(sig(L + ".x"), c + 1)
            v = psum.take(pe, f"{L}.xT{c}")
            for t in range(4):
                ins = PE.transpose(v[:, tile(t)], X[:, 4 * c + t, :], ident[:])
            ins.then_inc(psum.filled(f"{L}.xT{c}"), 1)

        def end_act(act, L, c):
            act.eng.wait_ge(*psum.made(f"{L}.xT{c}"))
            A.copy(XT[:, chunk(c)], psum.view(f"{L}.xT{c}")).then_inc(act.read(f"{L}.xT{c}"), 1)

        def add_bias_pool(pool, L, before, bias):
            for c in range(NC):
                pool.eng.wait_ge(sig(before + ".x"), c + 1)
                G.tensor_tensor(XB[:, ctiles(c)], X[:, ctiles(c)], bc(row(bias), 1, 4), ALU.add).then_inc(pool.flag(L + ".xb"), 1)

        def x_t_ready(pe, before, c):
            if before:
                pe.wait_ge(*psum.copied(f"{before}.xT{c}"))
            else:
                pe.wait_ge(loaded, LOADS * 16)

        def project_out_pe(pe, name, src_t, w, c):
            pe.wait_ge(*psum.copied(f"{name}T{c}"))
            v = psum.take(pe, f"{name}.out{c}")
            for t in range(4):
                ins = PE.matmul(v[:, tile(t)], src_t[:, tile(4 * c + t)], w, start=True, stop=True)
            ins.then_inc(psum.filled(f"{name}.out{c}"), 1)

        def turn_pe(pe, name, src, c):
            v = psum.take(pe, f"{name}T{c}")
            for t in range(4):
                ins = PE.transpose(v[:, tile(t)], src[:, 4 * c + t, :], ident[:])
            ins.then_inc(psum.filled(f"{name}T{c}"), 1)

        def move_act(act, product, dst):
            act.eng.wait_ge(*psum.made(product))
            v = psum.view(product)
            A.copy(dst, v).then_inc(act.read(product), 1)

        class ret:
            a = Carve(False)
            QT, KT = a(T), a(2, T)
            VG = a(NT, 2 * D)
            SG, Y = a(NT, D), a(NT, D)
            YT = QT
            SD = a(4, 2, 384)
            SQ = a(32, 16)
            m, v = a(NC, 32), a(NC, 32)
            rs = a(NC, 32)

        def retention_pe(pe):
            pe.wait_ge(w_loaded[0], 16)
            for c in range(NC):
                x_t_ready(pe, None, c)
                for n, w in (("q", "L0_attn_Wq"), ("k", "L0_attn_Wk")):
                    v = psum.take(pe, f"ret.{n}{c}")
                    PE.matmul(v, W(w), XT[:, chunk(c)], start=True, stop=True).then_inc(psum.filled(f"ret.{n}{c}"), 1)
                w0 = W_AT["L0_attn_Wv"][0]
                for half in range(2):
                    v = psum.take(pe, f"ret.vg{c}{half}")
                    for t in range(2):
                        ins = PE.matmul(v[:, t * 256:t * 256 + 256], XT[:, tile(4 * c + 2 * half + t)],
                                        WS[:, w0:w0 + 256], start=True, stop=True)
                    ins.then_inc(psum.filled(f"ret.vg{c}{half}"), 1)
            for c in range(NC):
                pe.wait_ge(*psum.copied(f"ret.q{c}"))
                pe.wait_ge(*psum.copied(f"ret.k{c}"))
                for b in (2 * c, 2 * c + 1):
                    q0 = b * S
                    for hp in range(4):
                        v = psum.take(pe, f"ret.s{b}.{hp}", 2)
                        r = slice(32 * hp, 32 * hp + 32)
                        for hh in range(2):
                            PE.matmul(v[:, hh, 0:256], ret.KT[r, hh, q0:q0 + 128], ret.QT[r, q0:q0 + 256],
                                      start=True, stop=True)
                            ins = PE.matmul(v[:, hh, 256:384], ret.KT[r, hh, q0 + 128:q0 + 256],
                                            ret.QT[r, q0 + 128:q0 + 256], start=True, stop=True)
                        ins.then_inc(psum.filled(f"ret.s{b}.{hp}"), 1)
                    if b % 2 == 0:
                        v_o = psum.take(pe, f"ret.o{c}")
                        pe.wait_ge(*psum.copied(f"ret.vg{c}0"))
                        pe.wait_ge(*psum.copied(f"ret.vg{c}1"))
                    t0 = (b % 2) * 256
                    for hp in range(4):
                        pe.wait_ge(*psum.copied(f"ret.s{b}.{hp}"))
                        for hh in range(2):
                            h = 2 * hp + hh
                            hd = slice(16 * h, 16 * h + 16)
                            PE.matmul(v_o[:, t0 + 16 * h:t0 + 16 * h + 16], ret.SD[:, hp, hh, 0:128],
                                      ret.VG[:, 2 * b, hd], start=True, stop=True)
                            PE.matmul(v_o[:, t0 + 128 + 16 * h:t0 + 144 + 16 * h], ret.SD[:, hp, hh, 128:256],
                                      ret.VG[:, 2 * b, hd], start=True, stop=False)
                            ins = PE.matmul(v_o[:, t0 + 128 + 16 * h:t0 + 144 + 16 * h], ret.SD[:, hp, hh, 256:384],
                                            ret.VG[:, 2 * b + 1, hd], start=False, stop=True)
                    if b % 2 == 1:
                        ins.then_inc(psum.filled(f"ret.o{c}"), 1)
                    else:
                        ins.then_inc(sig("ret.half"), 1)
            for c in range(NC):
                pe.wait_ge(sig("ret.y"), c + 1)
                turn_pe(pe, "ret.y", ret.Y, c)
            for c in range(NC):
                project_out_pe(pe, "ret.y", ret.YT, W("L0_attn_W_O"), c)
            for c in range(NC):
                end_pe(pe, "ret", c)

        def retention_act(act):
            for c in range(NC):
                move_act(act, f"ret.q{c}", ret.QT[:, chunk(c)])
                for half in range(2):
                    t = 4 * c + 2 * half
                    act.eng.wait_ge(*psum.made(f"ret.vg{c}{half}"))
                    v = psum.view(f"ret.vg{c}{half}")
                    A.copy(ret.VG[:, t:t + 2], v.rearrange("p (t d) -> p t d", t=2)).then_inc(act.read(f"ret.vg{c}{half}"), 1)
                act.eng.wait_ge(*act.own())
                A.activation(ret.SG[:, ctiles(c)], ret.VG[:, ctiles(c), D:2 * D], ACT.Exp, scale=-1.0).then_inc(act.flag("ret.gexp"), 1)
            for c in range(NC):
                move_act(act, f"ret.yT{c}", ret.YT[:, chunk(c)])
            for c in range(NC):
                end_act(act, "ret", c)

        def retention_dve(dve):
            for c in range(NC):
                dve.eng.wait_ge(*psum.made(f"ret.k{c}"))
                v = psum.view(f"ret.k{c}")
                V.tensor_scalar(ret.KT[:, 0, chunk(c)], v, parity16[:, 0:1], None, ALU.mult).then_inc(dve.step(), 1)
                V.tensor_scalar(ret.KT[:, 1, chunk(c)], v, parity16[:, 1:2], None, ALU.mult).then_inc(dve.read(f"ret.k{c}"), 1)
            for c in range(NC):
                dve.eng.wait_ge(sig("ret.gexp"), c + 1)
                g = ret.SG[:, ctiles(c)]
                V.tensor_scalar(g, g, 1.0, None, ALU.add).then_inc(dve.step(), 1)
                dve.eng.wait_ge(*dve.own())
                V.reciprocal(g, g).then_inc(dve.step(), 1)
                dve.eng.wait_ge(*dve.own())
                V.tensor_tensor(g, g, ret.VG[:, ctiles(c), D:2 * D], ALU.mult).then_inc(dve.step(), 1)
                for b in (2 * c, 2 * c + 1):
                    for hp in range(4):
                        dve.eng.wait_ge(*psum.made(f"ret.s{b}.{hp}"))
                        v = psum.view(f"ret.s{b}.{hp}")
                        if b:
                            if b % 2:
                                dve.eng.wait_ge(sig("ret.half"), c + 1)
                            else:
                                dve.eng.wait_ge(psum.full[psum.place[f"ret.o{c - 1}"][0]], psum.place[f"ret.o{c - 1}"][2])
                        d = decay[:, 2 * hp:2 * hp + 2, :]
                        V.tensor_tensor(ret.SD[:, hp, :, 0:256], v[:, :, 0:256], d, ALU.mult).then_inc(dve.step(), 1)
                        V.tensor_tensor(ret.SD[:, hp, :, 256:384], v[:, :, 256:384], d[:, :, 0:128],
                                                  ALU.mult).then_inc(dve.read(f"ret.s{b}.{hp}"), 1)
                dve.eng.wait_ge(*psum.made(f"ret.o{c}"))
                v = psum.view(f"ret.o{c}").rearrange("p (g w) -> p g w", w=16)
                y = ret.Y[:, ctiles(c)].rearrange("p t (h w) -> p (t h) w", w=16)
                V.tensor_reduce(ret.m[:, c], v, AX.X, ALU.add).then_inc(dve.step(), 1)
                dve.eng.wait_ge(*dve.own())
                V.tensor_scalar(ret.m[:, c], ret.m[:, c], 1.0 / 16, None, ALU.mult).then_inc(dve.step(), 1)
                dve.eng.wait_ge(*dve.own())
                V.tensor_tensor(y, v, bc(ret.m[:, c], 2, 16), ALU.subtract).then_inc(dve.read(f"ret.o{c}"), 1)
                dve.eng.wait_ge(*dve.own())
                V.tensor_tensor(ret.SQ, y, y, ALU.mult).then_inc(dve.step(), 1)
                dve.eng.wait_ge(*dve.own())
                V.tensor_reduce(ret.v[:, c], ret.SQ, AX.X, ALU.add).then_inc(dve.step(), 1)
                dve.eng.wait_ge(*dve.own())
                V.tensor_scalar(ret.v[:, c], ret.v[:, c], 1.0 / 16, 1e-6, ALU.mult, ALU.add).then_inc(dve.flag("ret.hvar"), 1)
                dve.eng.wait_ge(sig("ret.hrstd"), c + 1)
                V.tensor_tensor(y, y, bc(ret.rs[:, c], 2, 16), ALU.mult).then_inc(dve.step(), 1)
                dve.eng.wait_ge(*dve.own())
                V.tensor_tensor(ret.Y[:, ctiles(c)], ret.Y[:, ctiles(c)], g, ALU.mult).then_inc(dve.flag("ret.y"), 1)
            end_dve(dve, "ret", "ret.y.out", X)

        def retention_pool(pool):
            for c in range(NC):
                pool.eng.wait_ge(sig("ret.hvar"), c + 1)
                G.tensor_tensor(ret.rs[:, c], ret.v[:, c], minus_half[:], ALU.pow).then_inc(pool.flag("ret.hrstd"), 1)
            end_pool(pool, "ret")

        class Cross:
            def __init__(self, L, prefix, before, top, group, keep, fill):
                self.L, self.p, self.before, self.group = L, prefix, before, group
                self.keep, self.fill = keep, fill
                a = Carve(top)
                self.QT = a(T)
                self.KT = a(NB, SK)
                self.KM = a(2, 16, SK)
                self.VB = a(2, 8, 18)
                self.SS = a(3, 16, SK)
                self.ET = a(2, 8, P)
                self.O = a(NT, D)
                self.OT = self.QT
                self.mx = a(2, 16)
                self.rc = a(2, 2, 16)
                self.keepf = a(NB, SK)
                self.fillr = a(NB, SK, dt=BF16)

            def w(self, n):
                return W(f"{self.p}_{n}")

            def pe(self, pe):
                L = self.L
                pe.wait_ge(w_loaded[self.group], 16)
                v = psum.take(pe, f"{L}.k")
                PE.matmul(v[:, 0:NB * SK], self.w("Wk"), CT[:].rearrange("p b k -> p (b k)"),
                          start=True, stop=True).then_inc(psum.filled(f"{L}.k"), 1)
                for c in range(NC):
                    x_t_ready(pe, self.before, c)
                    v = psum.take(pe, f"{L}.q{c}")
                    PE.matmul(v, self.w("Wq"), XT[:, chunk(c)], start=True, stop=True)\
                        .then_inc(psum.filled(f"{L}.q{c}"), 1)
                self.values_pe(pe, 0)
                self.scores_pe(pe, 0)
                self.scores_pe(pe, 1)
                for t in range(NT + 1):
                    if t % 2 == 0 and t // 2 + 1 < NB:
                        self.values_pe(pe, t // 2 + 1)
                    if t + 2 < NT:
                        self.scores_pe(pe, t + 2)
                    if t < NT:
                        self.turn_pe(pe, t)
                    if t >= 1:
                        self.probs_pe(pe, t - 1)
                    if t == NT - 2:
                        self.turn_out_pe(pe, 0)
                    if t == NT - 1:
                        project_out_pe(pe, f"{L}.o", self.OT, self.w("Wo"), 0)
                self.turn_out_pe(pe, 1)
                end_pe(pe, L, 0)
                project_out_pe(pe, f"{L}.o", self.OT, self.w("Wo"), 1)
                end_pe(pe, L, 1)

            def values_pe(self, pe, b):
                v = psum.take(pe, f"{self.L}.v{b}")
                PE.matmul(v[:, 0:D], CD[:, b, :], self.w("Wv"), start=True, stop=True)\
                    .then_inc(psum.filled(f"{self.L}.v{b}"), 1)

            def scores_pe(self, pe, t):
                L, b = self.L, t // 2
                if t % 4 == 0:
                    pe.wait_ge(*psum.copied(f"{L}.q{t // 4}"))
                if t % 2 == 0:
                    pe.wait_ge(sig(L + ".km"), b + 1)
                    if self.keep is not None and t == 0:
                        pe.wait_ge(sig(L + ".fill"), 1)
                v = psum.take(pe, f"{L}.s{t}", 2)
                for half in range(2):
                    km = self.KM[:, b % 2, 8 * half:8 * half + 8, :].rearrange("p h k -> p (h k)")
                    ins = PE.matmul(v[:, half], self.QT[:, tile(t)], km, start=True, stop=self.keep is None)
                    if self.keep is not None:
                        ins = PE.matmul(v[:, half].rearrange("p (h k) -> p h k", h=8), ones16[0:3, :],
                                        bc(self.fillr[0:3, b, :], 1, 8), start=False, stop=True)
                ins.then_inc(psum.filled(f"{L}.s{t}"), 1)

            def turn_pe(self, pe, t):
                L = self.L
                pe.wait_ge(sig(L + ".exp"), t + 1)
                v = psum.take(pe, f"{L}.eT{t}", 2)
                e = self.SS[:, t % 3].rearrange("p (a h) k -> p a (h k)", a=8)
                for pair in range(8):
                    ins = PE.transpose(v[:, pair // 4, tile(pair % 4)], e[:, pair, :], ident[:])
                ins.then_inc(psum.filled(f"{L}.eT{t}"), 1)

            def probs_pe(self, pe, t):
                L, b = self.L, t // 2
                if t % 2 == 0:
                    pe.wait_ge(*psum.copied(f"{L}.v{b}"))
                    psum.take(pe, f"{L}.pv{b}")
                pe.wait_ge(*psum.copied(f"{L}.eT{t}"))
                v = psum.view(f"{L}.pv{b}")
                for pair in range(8):
                    at = (t % 2) * 144 + 18 * pair
                    ins = PE.matmul(v[:, at:at + 18], self.ET[:, t % 2, pair, :], self.VB[:, b % 2, pair, :],
                                    start=True, stop=True)
                if t % 2:
                    ins.then_inc(psum.filled(f"{L}.pv{b}"), 1)
                else:
                    ins.then_inc(sig(L + ".half"), 1)

            def turn_out_pe(self, pe, c):
                pe.wait_ge(*psum.copied(f"{self.L}.pv{2 * c + 1}"))
                turn_pe(pe, f"{self.L}.o", self.O, c)

            def act(self, act):
                L = self.L
                self.exp_act(act, 0)
                for t in range(NT):
                    if t + 1 < NT:
                        self.exp_act(act, t + 1)
                    if t == NT - 1:
                        move_act(act, f"{L}.oT0", self.OT[:, chunk(0)])
                    act.eng.wait_ge(*psum.made(f"{L}.eT{t}"))
                    v = psum.view(f"{L}.eT{t}")
                    if t >= 2:
                        if t % 2 == 0:
                            act.eng.wait_ge(sig(L + ".half"), t // 2)
                        else:
                            act.eng.wait_ge(*psum.made(f"{L}.pv{t // 2 - 1}"))
                    A.copy(self.ET[:, t % 2].rearrange("p (a b) q -> p a (b q)", a=2), v)\
                        .then_inc(act.read(f"{L}.eT{t}"), 1)
                move_act(act, f"{L}.oT1", self.OT[:, chunk(1)])
                for c in range(NC):
                    end_act(act, L, c)

            def exp_act(self, act, t):
                act.eng.wait_ge(*psum.copied(f"{self.L}.s{t}"))
                e = self.SS[:, t % 3]
                A.activation(e, e, ACT.Exp).then_inc(act.flag(self.L + ".exp"), 1)

            def dve(self, dve):
                L = self.L
                if self.keep is not None:
                    V.tensor_scalar(self.keepf, self.keep[:], 0.0, None, ALU.not_equal).then_inc(dve.step(), 1)
                    dve.eng.wait_ge(*dve.own())
                    V.tensor_scalar(self.fillr[0:3], self.keepf[0:3], 1.0, fills[:, self.fill:self.fill + 1],
                                    ALU.subtract, ALU.mult).then_inc(dve.flag(L + ".fill"), 1)
                dve.eng.wait_ge(*psum.made(f"{L}.k"))
                v = psum.view(f"{L}.k")
                kt = self.KT.rearrange("p b k -> p (b k)")
                if self.keep is not None:
                    V.scalar_tensor_tensor(kt, v[:, 0:NB * SK], bcol(self.p + "_bk"),
                                           self.keepf.rearrange("p b k -> p (b k)"), ALU.add, ALU.mult)\
                        .then_inc(dve.read(f"{L}.k"), 1)
                else:
                    V.tensor_scalar(kt, v[:, 0:NB * SK], bcol(self.p + "_bk"), None, ALU.add)\
                        .then_inc(dve.read(f"{L}.k"), 1)
                for j in range(2):
                    V.memset(self.VB[:, j], 0.0).then_inc(dve.step(), 1)
                dve.eng.wait_ge(*dve.own())
                for j in range(2):
                    V.memset(self.VB[0:64, j, :, 16], 1.0).then_inc(dve.step(), 1)
                    V.memset(self.VB[64:128, j, :, 17], 1.0).then_inc(dve.step(), 1)
                for c in range(NC):
                    dve.eng.wait_ge(*psum.made(f"{L}.q{c}"))
                    v = psum.view(f"{L}.q{c}")
                    V.tensor_scalar(self.QT[:, chunk(c)], v, bcol(self.p + "_bq"), 8 ** -0.5,
                                    ALU.add, ALU.mult).then_inc(dve.read(f"{L}.q{c}"), 1)
                self.values_dve(dve, 0)
                for t in range(NT):
                    if t >= 4 and t % 2 == 0:
                        self.out_dve(dve, t // 2 - 2)
                    self.shift_dve(dve, t)
                    if t == 1:
                        self.values_dve(dve, 1)
                self.out_dve(dve, NB - 2)
                end_sum_dve(dve, L, 0, f"{L}.o.out", XB)
                self.out_dve(dve, NB - 1)
                end_norm_dve(dve, L, 0)
                end_sum_dve(dve, L, 1, f"{L}.o.out", XB)
                end_norm_dve(dve, L, 1)

            def shift_dve(self, dve, t):
                L = self.L
                dve.eng.wait_ge(*psum.made(f"{L}.s{t}"))
                v = psum.view(f"{L}.s{t}").rearrange("p a (h k) -> p (a h) k", h=8)
                V.tensor_reduce(self.mx[:, t % 2], v, AX.X, ALU.max).then_inc(dve.step(), 1)
                dve.eng.wait_ge(*dve.own())
                if t >= 3:
                    dve.eng.wait_ge(*psum.made(f"{L}.eT{t - 3}"))
                V.tensor_tensor(self.SS[:, t % 3], v, bc(self.mx[:, t % 2], 2, SK), ALU.subtract)\
                    .then_inc(dve.read(f"{L}.s{t}"), 1)

            def values_dve(self, dve, b):
                L = self.L
                dve.eng.wait_ge(*psum.made(f"{L}.v{b}"))
                v = psum.view(f"{L}.v{b}")[:, 0:D].rearrange("p (a j w) -> p a j w", j=2, w=8)
                bias = row(self.p + "_bv").rearrange("p (a j w) -> p a j w", j=2, w=8)
                dve.eng.wait_ge(*dve.own())
                V.tensor_tensor(self.VB[0:64, b % 2, :, 0:8], v[0:64, :, 0], bias[0:64, :, 0], ALU.add)\
                    .then_inc(dve.step(), 1)
                V.tensor_tensor(self.VB[64:128, b % 2, :, 8:16], v[64:128, :, 1], bias[64:128, :, 1],
                                ALU.add).then_inc(dve.read(f"{L}.v{b}"), 1)

            def out_dve(self, dve, b):
                L = self.L
                dve.eng.wait_ge(*psum.made(f"{L}.pv{b}"))
                v = psum.view(f"{L}.pv{b}")[:, 0:288].rearrange("p (a x) -> p a x", x=18)
                rc = self.rc[:, b % 2].rearrange("p a (b j) -> p (a b) j", j=2)
                dve.eng.wait_ge(*dve.own())
                V.reciprocal(rc, v[:, :, 16:18]).then_inc(dve.step(), 1)
                dve.eng.wait_ge(*dve.own())
                o = self.O[:, 2 * b:2 * b + 2].rearrange("p t (a j w) -> p (t a) j w", j=2, w=8)
                V.tensor_tensor(o, v[:, :, 0:16].rearrange("p a (j w) -> p a j w", j=2), bc(rc, 3, 8),
                                ALU.mult).then_inc(dve.read(f"{L}.pv{b}"), 1)
                if b + 2 < NB:
                    self.values_dve(dve, b + 2)

            def pool(self, pool):
                L = self.L
                pool.eng.wait_ge(*psum.copied(f"{L}.k"))
                for b in range(NB):
                    if b >= 2:
                        pool.eng.wait_ge(*psum.made(f"{L}.s{2 * b - 3}"))
                    if b == min(2, NB - 1):
                        add_bias_pool(pool, L, self.before, self.p + "_bo")
                    G.tensor_tensor(self.KM[:, b % 2], bc(self.KT[:, b, :], 1, 16), bc(head_of8[:], 2, SK),
                                    ALU.mult).then_inc(pool.flag(L + ".km"), 1)
                for c in range(NC):
                    norm_rstd(pool, c, L)

        class Moe:
            def __init__(self, L, prefix, before, top, group1, group2, J, b2, top2):
                self.L, self.p, self.before, self.g1, self.g2, self.J, self.b2, self.top2 = \
                    L, prefix, before, group1, group2, J, b2, top2
                a = Carve(top)
                self.HT = a(2, NC, J, CH)
                self.LG, self.EL, self.GW = a(NT, 8), a(NT, 8), a(NT, 8)
                self.M8, self.I8, self.IF = a(NT, 8), a(NT, 8, dt=U32), a(NT, 8)
                self.H2 = a(NT, 8)
                self.dn = a(NT)
                self.GT = a(T, parts=8)
                self.W1 = W(prefix + "_W1").rearrange("p (e j h) -> p e j h", e=8, j=J)
                self.W2 = W(prefix + "_W2").rearrange("p (e j d) -> p e j d", e=8, j=J)

            def pe(self, pe):
                L = self.L
                for c in range(NC):
                    x_t_ready(pe, self.before, c)
                    v = psum.take(pe, f"{L}.lg{c}")
                    for t in range(4):
                        ins = PE.matmul(v[:, 8 * t:8 * t + 8], XT[:, tile(4 * c + t)], W(self.p + "_Wr"),
                                        start=True, stop=True)
                    ins.then_inc(psum.filled(f"{L}.lg{c}"), 1)
                pe.wait_ge(w_loaded[self.g1], 16)
                for c in range(NC):
                    self.hidden_pe(pe, 0, c)
                for c in range(NC):
                    pe.wait_ge(sig(L + ".gates"), c + 1)
                    v = psum.take(pe, f"{L}.gT{c}")
                    for t in range(4):
                        ins = PE.transpose(v[0:8, tile(t)], self.GW[:, 4 * c + t, :], ident[:])
                    ins.then_inc(psum.filled(f"{L}.gT{c}"), 1)
                pe.wait_ge(w_loaded[self.g2], 16)
                for e in range(8):
                    for c in range(NC):
                        if e + 1 < 8:
                            self.hidden_pe(pe, e + 1, c)
                        if e == 0:
                            pe.wait_ge(*psum.copied(f"{L}.gT{c}"))
                            v = psum.take(pe, f"{L}.b2{c}")
                            for t in range(4):
                                ins = PE.matmul(v[:, tile(t)], self.GT[:, tile(4 * c + t)], B2[:, self.b2, :],
                                                start=True, stop=True)
                            ins.then_inc(psum.filled(f"{L}.b2{c}"), 1)
                        for j in range(self.J):
                            pe.wait_ge(*psum.copied(f"{L}.h{e}.{c}.{j}"))
                        v = psum.take(pe, f"{L}.y{e}.{c}")
                        for t in range(4):
                            for j in range(self.J):
                                ins = PE.matmul(v[:, tile(t)], self.HT[:, e % 2, c, j, tile(t)], self.W2[:, e, j],
                                                start=j == 0, stop=j == self.J - 1)
                        ins.then_inc(psum.filled(f"{L}.y{e}.{c}"), 1)
                for c in range(NC):
                    end_pe(pe, L, c)

            def hidden_pe(self, pe, e, c):
                for j in range(self.J):
                    v = psum.take(pe, f"{self.L}.h{e}.{c}.{j}")
                    PE.matmul(v, self.W1[:, e, j], XT[:, chunk(c)], start=True, stop=True).then_inc(psum.filled(f"{self.L}.h{e}.{c}.{j}"), 1)

            def hidden_free(self, eng, e, c):
                if e >= 2:
                    k, _, n = psum.place[f"{self.L}.y{e - 2}.{c}"]
                    eng.wait_ge(psum.full[k], n)

            def act_share(self, j):
                return j % 4 != 3

            def act(self, act):
                L = self.L
                for c in range(NC):
                    self.hidden_act(act, 0, c)
                for c in range(NC):
                    act.eng.wait_ge(sig(L + ".shifted"), c + 1)
                    A.activation(self.EL[:, ctiles(c)], self.EL[:, ctiles(c)], ACT.Exp).then_inc(act.flag(L + ".exp"), 1)
                for c in range(NC):
                    act.eng.wait_ge(*psum.made(f"{L}.gT{c}"))
                    v = psum.view(f"{L}.gT{c}")
                    A.copy(self.GT[:, chunk(c)], v[0:8]).then_inc(act.read(f"{L}.gT{c}"), 1)
                for e in range(1, 8):
                    for c in range(NC):
                        self.hidden_act(act, e, c)
                for c in range(NC):
                    end_act(act, L, c)

            def hidden_act(self, act, e, c):
                for j in range(self.J):
                    if self.act_share(j):
                        act.eng.wait_ge(*psum.made(f"{self.L}.h{e}.{c}.{j}"))
                        v = psum.view(f"{self.L}.h{e}.{c}.{j}")
                        self.hidden_free(act.eng, e, c)
                        A.activation(self.HT[:, e % 2, c, j], v, ACT.Relu,
                                               bias=bcol(self.p + "_b1", e * self.J + j)).then_inc(act.read(f"{self.L}.h{e}.{c}.{j}"), 1)

            def hidden_dve(self, dve, e, c):
                for j in range(self.J):
                    if not self.act_share(j):
                        dve.eng.wait_ge(*psum.made(f"{self.L}.h{e}.{c}.{j}"))
                        v = psum.view(f"{self.L}.h{e}.{c}.{j}")
                        self.hidden_free(dve.eng, e, c)
                        V.tensor_scalar(self.HT[:, e % 2, c, j], v, bcol(self.p + "_b1", e * self.J + j), 0.0,
                                                  ALU.add, ALU.max).then_inc(dve.read(f"{self.L}.h{e}.{c}.{j}"), 1)

            def dve(self, dve):
                L = self.L
                for c in range(NC):
                    dve.eng.wait_ge(*psum.made(f"{L}.lg{c}"))
                    v = psum.view(f"{L}.lg{c}")
                    lg = self.LG[:, ctiles(c)]
                    V.tensor_tensor(lg, v[:, 0:32].rearrange("p (t e) -> p t e", t=4),
                                              bc(row(self.p + "_br"), 1, 4), ALU.add).then_inc(dve.read(f"{L}.lg{c}"), 1)
                    dve.eng.wait_ge(*dve.own())
                    for t in range(4 * c, 4 * c + 4):
                        V.max(self.M8[:, t], self.LG[:, t]).then_inc(dve.step(), 1)
                    dve.eng.wait_ge(*dve.own())
                    for t in range(4 * c, 4 * c + 4):
                        V.max_index(self.I8[:, t], self.M8[:, t], self.LG[:, t]).then_inc(dve.step(), 1)
                    V.tensor_tensor(self.EL[:, ctiles(c)], lg, bc(self.M8[:, ctiles(c), 0], 2, 8),
                                               ALU.subtract).then_inc(dve.flag(L + ".shifted"), 1)
                    dve.eng.wait_ge(*dve.own())
                    V.tensor_copy(self.IF[:, ctiles(c)], self.I8[:, ctiles(c)]).then_inc(dve.step(), 1)
                for c in range(NC):
                    self.hidden_dve(dve, 0, c)
                for c in range(NC):
                    g, h2 = self.GW[:, ctiles(c)], self.H2[:, ctiles(c)]
                    ex = bc(expert[:], 1, 4)
                    dve.eng.wait_ge(*dve.own())
                    V.tensor_tensor(g, ex, bc(self.IF[:, ctiles(c), 0], 2, 8), ALU.is_equal).then_inc(dve.step(), 1)
                    dve.eng.wait_ge(sig(L + ".exp"), c + 1)
                    if self.top2:
                        V.tensor_tensor(h2, ex, bc(self.IF[:, ctiles(c), 1], 2, 8), ALU.is_equal).then_inc(dve.step(), 1)
                        dve.eng.wait_ge(*dve.own())
                        V.tensor_tensor(g, g, h2, ALU.add).then_inc(dve.step(), 1)
                        dve.eng.wait_ge(*dve.own())
                        V.tensor_tensor(g, g, self.EL[:, ctiles(c)], ALU.mult).then_inc(dve.step(), 1)
                        dve.eng.wait_ge(*dve.own())
                        V.tensor_reduce(self.dn[:, ctiles(c)], g, AX.X, ALU.add).then_inc(dve.step(), 1)
                    else:
                        V.tensor_reduce(self.dn[:, ctiles(c)], self.EL[:, ctiles(c)], AX.X, ALU.add).then_inc(dve.step(), 1)
                    dve.eng.wait_ge(*dve.own())
                    V.reciprocal(self.dn[:, ctiles(c)], self.dn[:, ctiles(c)]).then_inc(dve.step(), 1)
                    dve.eng.wait_ge(*dve.own())
                    V.tensor_tensor(g, g, bc(self.dn[:, ctiles(c)], 2, 8), ALU.mult).then_inc(dve.flag(L + ".gates"), 1)
                for e in range(8):
                    for c in range(NC):
                        if e + 1 < 8:
                            self.hidden_dve(dve, e + 1, c)
                        r = R[:, ctiles(c)]
                        if e == 0:
                            dve.eng.wait_ge(*psum.made(f"{L}.b2{c}"))
                            v = psum.view(f"{L}.b2{c}")
                            V.tensor_tensor(r, v.rearrange("p (t d) -> p t d", t=4), X[:, ctiles(c)],
                                                      ALU.add).then_inc(dve.read(f"{L}.b2{c}"), 1)
                        dve.eng.wait_ge(*psum.made(f"{L}.y{e}.{c}"))
                        v = psum.view(f"{L}.y{e}.{c}")
                        dve.eng.wait_ge(*dve.own())
                        for t in range(4):
                            ins = V.scalar_tensor_tensor(r[:, t], v[:, tile(t)], self.GW[:, 4 * c + t, e:e + 1],
                                                         r[:, t], ALU.mult, ALU.add)
                            if t < 3:
                                ins.then_inc(dve.step(), 1)
                        ins.then_inc(dve.read(f"{L}.y{e}.{c}"), 1)
                end_dve(dve, L)

            def pool(self, pool):
                end_pool(pool, self.L)

        class cos:
            a = Carve(True)
            QKV = a(NT, 3 * D)
            QT, KT = a(T), a(T)
            PR = a(NT, S)
            PT = a(2, 2, S)
            OT, H1 = a(T), a(T)
            H2 = a(NC, 4, CH)
            sq = a(D)
            ssq, rn = a(NT, 2), a(NT, 2)
            mx, nb, sm = a(NT), a(NT), a(NT)

        def cosine_pe(pe):
            pe.wait_ge(w_loaded[3], 16)
            w0 = W_AT["L1_attn_Wq"][0]
            for c in range(NC):
                x_t_ready(pe, "moe0", c)
                for t in range(4 * c, 4 * c + 4):
                    v = psum.take(pe, f"cos.qkv{t}")
                    PE.matmul(v[:, 0:384], XT[:, tile(t)], WS[:, w0:w0 + 384], start=True, stop=True).then_inc(psum.filled(f"cos.qkv{t}"), 1)
            for c in range(NC):
                pe.wait_ge(*psum.copied(f"cos.qkv{4 * c + 3}"))
                turn_pe(pe, "cos.q", cos.QKV[:, :, 0:D], c)
                pe.wait_ge(sig("cos.khat"), c + 1)
                turn_pe(pe, "cos.k", cos.QKV[:, :, D:2 * D], c)
            for c in range(NC):
                pe.wait_ge(*psum.copied(f"cos.qT{c}"))
                pe.wait_ge(*psum.copied(f"cos.kT{c}"))
                for b in (2 * c, 2 * c + 1):
                    v = psum.take(pe, f"cos.s{b}")
                    for t in range(2):
                        ins = PE.matmul(v[:, t * S:t * S + S], cos.QT[:, tile(2 * b + t)], cos.KT[:, b * S:b * S + S],
                                        start=True, stop=True)
                    ins.then_inc(psum.filled(f"cos.s{b}"), 1)
            attend_pe(pe, "cos", cos.PR, cos.PT, lambda b: (sig("cos.probs"), b + 1))
            for c in range(NC):
                for b in (2 * c, 2 * c + 1):
                    if b % 2 == 0:
                        v = psum.take(pe, f"cos.oT{c}")
                    pe.wait_ge(*psum.copied(f"cos.pT{b}"))
                    for kt in range(2):
                        ins = PE.matmul(v[:, (b % 2) * S:(b % 2) * S + S], cos.QKV[:, 2 * b + kt, 2 * D:3 * D],
                                        cos.PT[:, b % 2, kt, :], start=kt == 0, stop=kt == 1)
                    if b % 2 == 0 and NC > 1:
                        ins.then_inc(sig("cos.half"), 1)
                ins.then_inc(psum.filled(f"cos.oT{c}"), 1)
                if c + 1 < NC:
                    for b in (2 * c + 2, 2 * c + 3):
                        turn_probs_pe(pe, "cos", cos.PR, b, lambda b: (sig("cos.probs"), b + 1))
            for c in range(NC):
                pe.wait_ge(*psum.copied(f"cos.oT{c}"))
                v = psum.take(pe, f"cos.h1{c}")
                PE.matmul(v, W("L1_attn_W1"), cos.OT[:, chunk(c)], start=True, stop=True).then_inc(psum.filled(f"cos.h1{c}"), 1)
            for c in range(NC):
                pe.wait_ge(*psum.copied(f"cos.h1{c}"))
                for j in range(4):
                    v = psum.take(pe, f"cos.h2{c}.{j}")
                    PE.matmul(v, W("L1_attn_W2")[:, tile(j)], cos.H1[:, chunk(c)], start=True, stop=True).then_inc(psum.filled(f"cos.h2{c}.{j}"), 1)
            for c in range(NC):
                for j in range(4):
                    pe.wait_ge(*psum.copied(f"cos.h2{c}.{j}"))
                v = psum.take(pe, f"cos.out{c}")
                for t in range(4):
                    for j in range(4):
                        ins = PE.matmul(v[:, tile(t)], cos.H2[:, c, j, tile(t)], W("L1_attn_W3")[:, tile(j)],
                                        start=j == 0, stop=j == 3)
                ins.then_inc(psum.filled(f"cos.out{c}"), 1)
            for c in range(NC):
                end_pe(pe, "cos", c)

        def turn_probs_pe(pe, name, src, b, ready):
            pe.wait_ge(*ready(b))
            v = psum.take(pe, f"{name}.pT{b}")
            for kt in range(2):
                for t in range(2):
                    ins = PE.transpose(v[:, kt * S + t * P:kt * S + t * P + P], src[:, 2 * b + t, tile(kt)], ident[:])
            ins.then_inc(psum.filled(f"{name}.pT{b}"), 1)

        def attend_pe(pe, name, src, dst, ready):
            for b in range(2):
                turn_probs_pe(pe, name, src, b, ready)

        def cosine_act(act):
            for t in range(NT):
                act.eng.wait_ge(*psum.copied(f"cos.qkv{t}"))
                for j in range(2):
                    act.eng.wait_ge(*act.own())
                    ins = A.activation(cos.sq, cos.QKV[:, t, j * D:j * D + D], ACT.Square,
                                       accum_out=cos.ssq[:, t, j:j + 1])
                    if t % 4 == 3 and j == 1:
                        ins.then_inc(act.flag("cos.ssq"), 1)
                    else:
                        ins.then_inc(act.step(), 1)
            for c in range(NC):
                move_act(act, f"cos.qT{c}", cos.QT[:, chunk(c)])
                move_act(act, f"cos.kT{c}", cos.KT[:, chunk(c)])
            for b in range(NB):
                act.eng.wait_ge(*psum.made(f"cos.s{b}"))
                v = psum.view(f"cos.s{b}")
                act.eng.wait_ge(sig("cos.nb"), b + 1)
                for t in range(2):
                    i = 2 * b + t
                    ins = A.activation(cos.PR[:, i], v[:, t * S:t * S + S], ACT.Exp, bias=cos.nb[:, i:i + 1],
                                       scale=cos.rn[:, i, 0:1], accum_out=cos.sm[:, i:i + 1])
                    if t == 0:
                        ins.then_inc(act.step(), 1)
                ins.then_inc(act.read(f"cos.s{b}"), 1)
            for c in range(NC):
                for b in (2 * c, 2 * c + 1):
                    if b >= 2:
                        if b % 2:
                            k, _, n = psum.place[f"cos.oT{c - 1}"]
                            act.eng.wait_ge(psum.full[k], n)
                        else:
                            act.eng.wait_ge(sig("cos.half"), c)
                    move_act(act, f"cos.pT{b}", cos.PT[:, b % 2].rearrange("p a q -> p (a q)"))
                move_act(act, f"cos.oT{c}", cos.OT[:, chunk(c)])
            for c in range(NC):
                act.eng.wait_ge(*psum.made(f"cos.h1{c}"))
                v = psum.view(f"cos.h1{c}")
                A.activation(cos.H1[:, chunk(c)], v, ACT.Relu, bias=bcol("L1_attn_b1")).then_inc(act.read(f"cos.h1{c}"), 1)
            for c in range(NC):
                for j in range(0, 4, 2):
                    act.eng.wait_ge(*psum.made(f"cos.h2{c}.{j}"))
                    v = psum.view(f"cos.h2{c}.{j}")
                    A.activation(cos.H2[:, c, j], v, ACT.Relu, bias=bcol("L1_attn_b2", j)).then_inc(act.read(f"cos.h2{c}.{j}"), 1)
            for c in range(NC):
                end_act(act, "cos", c)

        def cosine_dve(dve):
            bias = RW[:, R_AT["L1_attn_bq"][0]:R_AT["L1_attn_bq"][0] + 384]
            for t in range(NT):
                dve.eng.wait_ge(*psum.made(f"cos.qkv{t}"))
                v = psum.view(f"cos.qkv{t}")
                V.tensor_tensor(cos.QKV[:, t], v[:, 0:384], bias, ALU.add).then_inc(dve.read(f"cos.qkv{t}"), 1)
            for c in range(NC):
                dve.eng.wait_ge(sig("cos.pow"), c + 1)
                rn = cos.rn[:, ctiles(c)]
                V.tensor_scalar(rn, rn, 1e12, None, ALU.min).then_inc(dve.step(), 1)
                dve.eng.wait_ge(*dve.own())
                for t in range(4 * c, 4 * c + 4):
                    k = cos.QKV[:, t, D:2 * D]
                    ins = V.tensor_scalar(k, k, cos.rn[:, t, 1:2], None, ALU.mult)
                    if t % 4 < 3:
                        ins.then_inc(dve.step(), 1)
                ins.then_inc(dve.flag("cos.khat"), 1)
            for b in range(NB):
                dve.eng.wait_ge(*psum.made(f"cos.s{b}"))
                v = psum.view(f"cos.s{b}").rearrange("p (t k) -> p t k", t=2)
                mx = cos.mx[:, 2 * b:2 * b + 2]
                V.tensor_reduce(mx, v, AX.X, ALU.max, negate=True).then_inc(dve.step(), 1)
                dve.eng.wait_ge(*dve.own())
                V.tensor_tensor(cos.nb[:, 2 * b:2 * b + 2], mx, cos.rn[:, 2 * b:2 * b + 2, 0], ALU.mult).then_inc(dve.flag("cos.nb"), 1)
            for b in range(NB):
                dve.eng.wait_ge(*psum.copied(f"cos.s{b}"))
                sm = cos.sm[:, 2 * b:2 * b + 2]
                V.reciprocal(sm, sm).then_inc(dve.step(), 1)
                dve.eng.wait_ge(*dve.own())
                for t in (2 * b, 2 * b + 1):
                    ins = V.tensor_scalar(cos.PR[:, t], cos.PR[:, t], cos.sm[:, t:t + 1], None, ALU.mult)
                    if t % 2 == 0:
                        ins.then_inc(dve.step(), 1)
                ins.then_inc(dve.flag("cos.probs"), 1)
            for c in range(NC):
                for j in (1, 3):
                    dve.eng.wait_ge(*psum.made(f"cos.h2{c}.{j}"))
                    v = psum.view(f"cos.h2{c}.{j}")
                    V.tensor_scalar(cos.H2[:, c, j], v, bcol("L1_attn_b2", j), 0.0, ALU.add, ALU.max).then_inc(dve.read(f"cos.h2{c}.{j}"), 1)
            end_dve(dve, "cos", "cos.out", XB)

        def cosine_pool(pool):
            for c in range(NC):
                pool.eng.wait_ge(sig("cos.ssq"), c + 1)
                G.tensor_tensor(cos.rn[:, ctiles(c)].rearrange("p t j -> p (t j)"),
                                            cos.ssq[:, ctiles(c)].rearrange("p t j -> p (t j)"),
                                            minus_half[:, 0:8], ALU.pow).then_inc(pool.flag("cos.pow"), 1)
            add_bias_pool(pool, "cos", "moe0", "L1_attn_b3")
            end_pool(pool, "cos")

        class one:
            a = Carve(False)
            KT = a(NB, SK)
            VV = a(NB, D, parts=64)
            PR = a(NT, SK)
            PT = a(T, parts=64)
            mx, sm = a(NT), a(NT)

        def one_pe(pe):
            v = psum.take(pe, "one.k")
            PE.matmul(v[:, 0:NB * SK], W("L1_xattn_key_matrix"), CT[:].rearrange("p b k -> p (b k)"),
                                start=True, stop=True).then_inc(psum.filled("one.k"), 1)
            v = psum.take(pe, "one.v")
            for b in range(NB):
                ins = PE.matmul(v[0:64, b * D:b * D + D], CT[:, b, :], W("L1_xattn_value_matrix"), start=True, stop=True)
            ins.then_inc(psum.filled("one.v"), 1)
            pe.wait_ge(*psum.copied("one.k"))
            for c in range(NC):
                x_t_ready(pe, "cos", c)
                v = psum.take(pe, f"one.s{c}")
                for t in range(4):
                    i = 4 * c + t
                    ins = PE.matmul(v[:, t * SK:t * SK + SK], XT[:, tile(i)], one.KT[:, i // 2, :], start=True, stop=True)
                ins.then_inc(psum.filled(f"one.s{c}"), 1)
            for c in range(NC):
                pe.wait_ge(*psum.copied(f"one.s{c}"))
                v = psum.take(pe, f"one.pT{c}")
                for t in range(4):
                    ins = PE.transpose(v[0:64, tile(t)], one.PR[:, 4 * c + t, :], ident[:])
                ins.then_inc(psum.filled(f"one.pT{c}"), 1)
            for c in range(NC):
                pe.wait_ge(*psum.copied(f"one.pT{c}"))
                if c == 0:
                    pe.wait_ge(*psum.copied("one.v"))
                v = psum.take(pe, f"one.out{c}")
                for t in range(4):
                    i = 4 * c + t
                    ins = PE.matmul(v[:, tile(t)], one.PT[:, tile(i)], one.VV[:, i // 2, :], start=True, stop=True)
                ins.then_inc(psum.filled(f"one.out{c}"), 1)
            for c in range(NC):
                end_pe(pe, "one", c)

        def one_act(act):
            act.eng.wait_ge(*psum.made("one.k"))
            v = psum.view("one.k")
            A.copy(one.KT.rearrange("p b k -> p (b k)"), v[:, 0:NB * SK]).then_inc(act.read("one.k"), 1)
            act.eng.wait_ge(*psum.made("one.v"))
            v = psum.view("one.v")
            A.copy(one.VV.rearrange("p b k -> p (b k)"), v[0:64, 0:NB * D]).then_inc(act.read("one.v"), 1)
            for c in range(NC):
                act.eng.wait_ge(*psum.made(f"one.s{c}"))
                v = psum.view(f"one.s{c}")
                act.eng.wait_ge(sig("one.mx"), c + 1)
                for t in range(4):
                    i = 4 * c + t
                    ins = A.activation(one.PR[:, i], v[:, t * SK:t * SK + SK], ACT.Exp, bias=one.mx[:, i:i + 1],
                                       scale=D ** -0.5, accum_out=one.sm[:, i:i + 1])
                    if t < 3:
                        ins.then_inc(act.step(), 1)
                ins.then_inc(act.read(f"one.s{c}"), 1)
            for c in range(NC):
                act.eng.wait_ge(*psum.made(f"one.pT{c}"))
                v = psum.view(f"one.pT{c}")
                A.copy(one.PT[:, chunk(c)], v[0:64]).then_inc(act.read(f"one.pT{c}"), 1)
            for c in range(NC):
                end_act(act, "one", c)

        def one_dve(dve):
            for c in range(NC):
                dve.eng.wait_ge(*psum.made(f"one.s{c}"))
                v = psum.view(f"one.s{c}")[:, 0:4 * SK].rearrange("p (t k) -> p t k", t=4)
                mx = one.mx[:, ctiles(c)]
                V.tensor_reduce(mx, v, AX.X, ALU.max, negate=True).then_inc(dve.step(), 1)
                dve.eng.wait_ge(*dve.own())
                V.tensor_scalar(mx, mx, D ** -0.5, None, ALU.mult).then_inc(dve.flag("one.mx"), 1)
            for c in range(NC):
                dve.eng.wait_ge(*psum.copied(f"one.s{c}"))
                sm = one.sm[:, ctiles(c)]
                V.reciprocal(sm, sm).then_inc(dve.step(), 1)
                dve.eng.wait_ge(*dve.own())
                dve.eng.wait_ge(*psum.made(f"one.out{c}"))
                v = psum.view(f"one.out{c}")
                for t in range(4):
                    i = 4 * c + t
                    ins = V.scalar_tensor_tensor(R[:, i], v[:, tile(t)], one.sm[:, i:i + 1], X[:, i], ALU.mult, ALU.add)
                    if t < 3:
                        ins.then_inc(dve.step(), 1)
                ins.then_inc(dve.read(f"one.out{c}"), 1)
            end_dve(dve, "one")

        def one_pool(pool):
            end_pool(pool, "one")

        class spm:
            a = Carve(False)
            QT, KT = a(T), a(T)
            VV = a(NT, D)
            Z, SA, SB = a(NT, S), a(NT, S), a(NT, S)
            mx, sz, stp, cnt, rk, add_ = a(NT), a(NT), a(NT), a(NT), a(NT), a(NT)
            PT = a(2, 2, S)

        def sparse_pe(pe):
            pe.wait_ge(w_loaded[5], 16)
            for c in range(NC):
                x_t_ready(pe, "moe1", c)
                for n, w in (("q", "L2_attn_Wq"), ("k", "L2_attn_Wk")):
                    v = psum.take(pe, f"spm.{n}{c}")
                    PE.matmul(v, W(w), XT[:, chunk(c)], start=True, stop=True).then_inc(psum.filled(f"spm.{n}{c}"), 1)
                v = psum.take(pe, f"spm.v{c}")
                for t in range(4):
                    ins = PE.matmul(v[:, tile(t)], XT[:, tile(4 * c + t)], W("L2_attn_Wv"), start=True, stop=True)
                ins.then_inc(psum.filled(f"spm.v{c}"), 1)
            for c in range(NC):
                pe.wait_ge(*psum.copied(f"spm.q{c}"))
                pe.wait_ge(*psum.copied(f"spm.k{c}"))
                for b in (2 * c, 2 * c + 1):
                    v = psum.take(pe, f"spm.s{b}")
                    for t in range(2):
                        ins = PE.matmul(v[:, t * S:t * S + S], spm.QT[:, tile(2 * b + t)], spm.KT[:, b * S:b * S + S],
                                        start=True, stop=True)
                    ins.then_inc(psum.filled(f"spm.s{b}"), 1)
            for b in range(NB):
                turn_probs_pe(pe, "spm", spm.Z, b, lambda b: (sig("spm.probs"), b // 2 + 1))
                pe.wait_ge(*psum.copied(f"spm.pT{b}"))
                if b % 2 == 0:
                    v = psum.take(pe, f"spm.out{b // 2}")
                for t in range(2):
                    at = tile((b % 2) * 2 + t)
                    for kt in range(2):
                        ins = PE.matmul(v[:, at], spm.PT[:, b % 2, kt, tile(t)], spm.VV[:, 2 * b + kt, :],
                                        start=kt == 0, stop=kt == 1)
                if b % 2 == 0:
                    ins.then_inc(sig("spm.half"), 1)
                else:
                    ins.then_inc(psum.filled(f"spm.out{b // 2}"), 1)
            for c in range(NC):
                end_pe(pe, "spm", c)

        def sparse_act(act):
            for c in range(NC):
                move_act(act, f"spm.q{c}", spm.QT[:, chunk(c)])
                move_act(act, f"spm.k{c}", spm.KT[:, chunk(c)])
                move_act(act, f"spm.v{c}", spm.VV[:, ctiles(c)].rearrange("p t d -> p (t d)"))
            for b in range(NB):
                act.eng.wait_ge(*psum.made(f"spm.s{b}"))
                v = psum.view(f"spm.s{b}")
                act.eng.wait_ge(sig("spm.mx"), b + 1)
                for t in range(2):
                    i = 2 * b + t
                    ins = A.activation(spm.Z[:, i], v[:, t * S:t * S + S], ACT.Identity, bias=spm.mx[:, i:i + 1],
                                       scale=D ** -0.5, accum_out=spm.sz[:, i:i + 1])
                    if t == 0:
                        ins.then_inc(act.step(), 1)
                ins.then_inc(act.read(f"spm.s{b}"), 1)
            for b in range(NB):
                if b >= 2:
                    if b % 2:
                        k, _, n = psum.place[f"spm.out{b // 2 - 1}"]
                        act.eng.wait_ge(psum.full[k], n)
                    else:
                        act.eng.wait_ge(sig("spm.half"), b // 2)
                move_act(act, f"spm.pT{b}", spm.PT[:, b % 2].rearrange("p a q -> p (a q)"))
            for c in range(NC):
                end_act(act, "spm", c)

        def sort_descending(dve, src, bufs):
            rows_of = lambda a, w: a.rearrange("p t (n w) -> p (t n) w", w=w)
            cur, k = src, 2
            other = 0
            while k <= S:
                d = k // 2
                first = True
                while d >= 1:
                    nxt = bufs[other]
                    other ^= 1
                    w = k if first else 2 * d
                    i, o = rows_of(cur, w), rows_of(nxt, w)
                    lo = i[:, :, 0:d]
                    mirror = slice(k - 1, d - 1, -1) if first else slice(d, 2 * d)
                    hi, hi_o = i[:, :, mirror], o[:, :, mirror]
                    dve.eng.wait_ge(*dve.own())
                    V.tensor_tensor(o[:, :, 0:d], lo, hi, ALU.max).then_inc(dve.step(), 1)
                    V.tensor_tensor(hi_o, lo, hi, ALU.min).then_inc(dve.step(), 1)
                    cur, first = nxt, False
                    d //= 2
                k *= 2
            return cur

        def sparse_dve(dve):
            for b in range(NB):
                dve.eng.wait_ge(*psum.made(f"spm.s{b}"))
                v = psum.view(f"spm.s{b}").rearrange("p (t k) -> p t k", t=2)
                mx = spm.mx[:, 2 * b:2 * b + 2]
                V.tensor_reduce(mx, v, AX.X, ALU.max, negate=True).then_inc(dve.step(), 1)
                dve.eng.wait_ge(*dve.own())
                V.tensor_scalar(mx, mx, D ** -0.5, None, ALU.mult).then_inc(dve.flag("spm.mx"), 1)
            for c in range(NC):
                z = spm.Z[:, ctiles(c)]
                dve.eng.wait_ge(*psum.copied(f"spm.s{2 * c}"))
                dve.eng.wait_ge(*psum.copied(f"spm.s{2 * c + 1}"))
                stp, cnt, rk, ad = (a[:, ctiles(c)] for a in (spm.stp, spm.cnt, spm.rk, spm.add_))
                V.tensor_scalar(stp, spm.sz[:, ctiles(c)], 1.0, 1.0 / S, ALU.subtract, ALU.mult).then_inc(dve.step(), 1)
                dve.eng.wait_ge(*dve.own())
                for t in range(4 * c, 4 * c + 4):
                    V.tensor_scalar(spm.SA[:, t], spm.Z[:, t], spm.stp[:, t:t + 1], None, ALU.is_gt, ALU.add,
                                            accum_out=spm.cnt[:, t:t + 1]).then_inc(dve.step(), 1)
                dve.eng.wait_ge(*dve.own())
                V.reciprocal(rk, cnt).then_inc(dve.step(), 1)
                dve.eng.wait_ge(*dve.own())
                V.tensor_tensor(ad, stp, rk, ALU.add).then_inc(dve.step(), 1)
                cur = sort_descending(dve, z, (spm.SA[:, ctiles(c)], spm.SB[:, ctiles(c)]))
                oth = spm.SA[:, ctiles(c)]
                dve.eng.wait_ge(*dve.own())
                for t in range(4):
                    V.tensor_tensor_scan(oth[:, t], cur[:, t], zeros[:], 0.0, ALU.add, ALU.add).then_inc(dve.step(), 1)
                dve.eng.wait_ge(*dve.own())
                for t in range(4):
                    V.tensor_scalar(oth[:, t], oth[:, t], spm.rk[:, 4 * c + t:4 * c + t + 1],
                                            spm.add_[:, 4 * c + t:4 * c + t + 1], ALU.mult, ALU.subtract).then_inc(dve.step(), 1)
                dve.eng.wait_ge(*dve.own())
                V.tensor_tensor(z, z, oth, ALU.subtract).then_inc(dve.step(), 1)
                dve.eng.wait_ge(*dve.own())
                V.tensor_scalar(z, z, 0.0, None, ALU.max).then_inc(dve.flag("spm.probs"), 1)
            end_dve(dve, "spm", "spm.out", X)

        def sparse_pool(pool):
            end_pool(pool, "spm")

        class lora:
            a = Carve(True)
            LZ = a(NT, 138)
            ZT = a(T)
            M8, I8, IF = a(NT, 8), a(NT, 8, dt=U32), a(NT, 8)
            G, H2, EL = a(NT, 8), a(NT, 8), a(NT, 8)
            dn, zr = a(NT), a(NT)

        def lora_pe(pe):
            w0 = W_AT["L2_ffn_gate_w"][0]
            for c in range(NC):
                x_t_ready(pe, "x2", c)
                for half in range(2):
                    v = psum.take(pe, f"lora.lz{c}{half}")
                    for t in range(2):
                        ins = PE.matmul(v[:, t * 138:t * 138 + 138], XT[:, tile(4 * c + 2 * half + t)],
                                        WS[:, w0:w0 + 138], start=True, stop=True)
                    ins.then_inc(psum.filled(f"lora.lz{c}{half}"), 1)
            for c in range(NC):
                pe.wait_ge(sig("lora.z"), c + 1)
                turn_pe(pe, "lora.z", lora.LZ[:, :, 10:138], c)
            for c in range(NC):
                pe.wait_ge(*psum.copied(f"lora.zT{c}"))
                v = psum.take(pe, f"lora.out{c}")
                for t in range(4):
                    PE.matmul(v[:, tile(t)], XT[:, tile(4 * c + t)], W("L2_ffn_base_w"), start=True, stop=False)
                    ins = PE.matmul(v[:, tile(t)], lora.ZT[:, tile(4 * c + t)], W("L2_ffn_lora_B"),
                                    start=False, stop=True)
                ins.then_inc(psum.filled(f"lora.out{c}"), 1)
            for c in range(NC):
                end_pe(pe, "lora", c)

        def lora_act(act):
            for c in range(NC):
                act.eng.wait_ge(sig("lora.shifted"), c + 1)
                A.activation(lora.EL[:, ctiles(c)], lora.EL[:, ctiles(c)], ACT.Exp).then_inc(act.flag("lora.exp"), 1)
            for c in range(NC):
                move_act(act, f"lora.zT{c}", lora.ZT[:, chunk(c)])
            for c in range(NC):
                end_act(act, "lora", c)

        def lora_dve(dve):
            for c in range(NC):
                for half in range(2):
                    dve.eng.wait_ge(*psum.made(f"lora.lz{c}{half}"))
                    v = psum.view(f"lora.lz{c}{half}")
                    t = 4 * c + 2 * half
                    V.tensor_copy(lora.LZ[:, t:t + 2], v[:, 0:276].rearrange("p (t n) -> p t n", t=2)).then_inc(dve.read(f"lora.lz{c}{half}"), 1)
                dve.eng.wait_ge(*dve.own())
                for t in range(4 * c, 4 * c + 4):
                    V.max(lora.M8[:, t], lora.LZ[:, t, 0:10]).then_inc(dve.step(), 1)
                dve.eng.wait_ge(*dve.own())
                for t in range(4 * c, 4 * c + 4):
                    V.max_index(lora.I8[:, t], lora.M8[:, t], lora.LZ[:, t, 0:10]).then_inc(dve.step(), 1)
                V.tensor_tensor(lora.EL[:, ctiles(c)], lora.LZ[:, ctiles(c), 0:8],
                                           bc(lora.M8[:, ctiles(c), 0], 2, 8), ALU.subtract).then_inc(dve.flag("lora.shifted"), 1)
                dve.eng.wait_ge(*dve.own())
                V.tensor_copy(lora.IF[:, ctiles(c)], lora.I8[:, ctiles(c)]).then_inc(dve.step(), 1)
            for c in range(NC):
                g, h2, ex = lora.G[:, ctiles(c)], lora.H2[:, ctiles(c)], bc(expert[:], 1, 4)
                dn, zr = lora.dn[:, ctiles(c)], lora.zr[:, ctiles(c)]
                dve.eng.wait_ge(*dve.own())
                V.tensor_tensor(g, ex, bc(lora.IF[:, ctiles(c), 0], 2, 8), ALU.is_equal).then_inc(dve.step(), 1)
                V.tensor_tensor(h2, ex, bc(lora.IF[:, ctiles(c), 1], 2, 8), ALU.is_equal).then_inc(dve.step(), 1)
                dve.eng.wait_ge(*dve.own())
                V.tensor_tensor(g, g, h2, ALU.add).then_inc(dve.step(), 1)
                dve.eng.wait_ge(*dve.own())
                dve.eng.wait_ge(sig("lora.exp"), c + 1)
                V.tensor_tensor(g, g, lora.EL[:, ctiles(c)], ALU.mult).then_inc(dve.step(), 1)
                dve.eng.wait_ge(*dve.own())
                V.tensor_reduce(dn, g, AX.X, ALU.add).then_inc(dve.step(), 1)
                dve.eng.wait_ge(*dve.own())
                V.tensor_scalar(zr, dn, 0.0, None, ALU.is_equal).then_inc(dve.step(), 1)
                dve.eng.wait_ge(*dve.own())
                V.tensor_tensor(dn, dn, zr, ALU.add).then_inc(dve.step(), 1)
                dve.eng.wait_ge(*dve.own())
                V.reciprocal(dn, dn).then_inc(dve.step(), 1)
                dve.eng.wait_ge(*dve.own())
                V.tensor_scalar(dn, dn, 32.0 / 16.0, None, ALU.mult).then_inc(dve.step(), 1)
                dve.eng.wait_ge(*dve.own())
                V.tensor_tensor(g, g, bc(dn, 2, 8), ALU.mult).then_inc(dve.step(), 1)
                dve.eng.wait_ge(*dve.own())
                for t in range(4 * c, 4 * c + 4):
                    z = lora.LZ[:, t, 10:138].rearrange("p (e r) -> p e r", e=8)
                    ins = V.tensor_tensor(z, z, bc(lora.G[:, t], 2, 16), ALU.mult)
                    if t % 4 < 3:
                        ins.then_inc(dve.step(), 1)
                ins.then_inc(dve.flag("lora.z"), 1)
            end_dve(dve, "lora", "lora.out", XB)

        def lora_pool(pool):
            add_bias_pool(pool, "lora", "x2", "L2_ffn_base_b")
            end_pool(pool, "lora")

        GROUPS = NB * 8

        class big:
            a = Carve(False)
            QT = a(3, S)
            KM = a(3, 4, S)
            Q16, K16 = a(2, S, dt=BF16), a(2, 4 * S, dt=BF16)
            VV = a(4, 2, P)
            mx = a(2, 4)
            HL = a(2, 2 * P, dt=BF16)
            E = a(2, 4, 2, S)
            ES = a(2, 4, S)
            rc = a(S)
            OT = a(2, 8, S)
            Y = XB

        def big_pe(pe):
            pe.wait_ge(w_loaded[6], 16)
            wq = W("L3_attn_w_qkv")

            def project(n):
                b, g = divmod(n, 8)
                if n % 16 == 0:
                    pe.wait_ge(*psum.copied(f"lora.xT{b // 2}"))
                v = psum.take(pe, f"big.qk{n}")
                PE.matmul(v[:, 0:S], wq[:, tile(g)], XT[:, b * S:b * S + S], start=True, stop=True)
                PE.matmul(v[:, S:2 * S], wq[:, 1024 + g * P:1024 + g * P + P], XT[:, b * S:b * S + S],
                          start=True, stop=True).then_inc(psum.filled(f"big.qk{n}"), 1)
                v = psum.take(pe, f"big.v{n}")
                for t in range(2):
                    ins = PE.matmul(v[:, tile(t)], XT[:, tile(2 * b + t)], wq[:, 2048 + g * P:2048 + g * P + P],
                                    start=True, stop=True)
                ins.then_inc(psum.filled(f"big.v{n}"), 1)

            def maxima(n):
                pe.wait_ge(sig("big.k16"), n + 1)
                for pair in range(2):
                    v = psum.take(pe, f"big.m{n}.{pair}", 2)
                    for t in range(2):
                        ins = PE.matmul(v[:, t], big.Q16[:, n % 2, tile(t)],
                                        big.K16[:, n % 2, 2 * pair * S:2 * (pair + 1) * S], start=True, stop=True)
                    ins.then_inc(psum.filled(f"big.m{n}.{pair}"), 1)

            def shifts(n):
                pe.wait_ge(sig("big.shift"), n + 1)
                v = psum.take(pe, f"big.hT{n}")
                for t in range(2):
                    ins = PE.transpose(v.bitcast(BF16)[:, tile(t)],
                                       shift_parts[:, n % 2, t].rearrange("p h w -> p (h w)"), ident16[:])
                ins.then_inc(psum.filled(f"big.hT{n}"), 1)

            def scores(n):
                pe.wait_ge(*psum.copied(f"big.hT{n}"))
                for pair in range(2):
                    v = psum.take(pe, f"big.e{n}.{pair}", 2)
                    for hh in range(2):
                        h = 2 * pair + hh
                        PE.matmul(v[:, hh].rearrange("p (a q) -> p a q", a=2), pick[:, h, :],
                                  bc(big.HL[:, n % 2], 1, 2), start=True, stop=True)
                        for kt in range(2):
                            ins = PE.matmul(v[:, hh, kt * S:kt * S + S], big.KM[:, n % 3, h, tile(kt)],
                                            big.QT[:, n % 3, :], start=False, stop=True, skip_group_check=True)
                    ins.then_inc(psum.filled(f"big.e{n}.{pair}"), 1)

            def values(n):
                pe.wait_ge(sig("big.sums"), n + 1)
                pe.wait_ge(*psum.copied(f"big.v{n}"))
                v = psum.take(pe, f"big.o{n}")
                for kt in range(2):
                    for h in range(4):
                        PE.matmul(v[32 * h:32 * h + 32, 0:S], big.VV[:, n % 4, kt, 32 * h:32 * h + 32],
                                  big.E[:, n % 2, h, kt, :], start=kt == 0, stop=kt == 1)
                for h in range(4):
                    ins = PE.matmul(v[32 * h:32 * h + 32, S:2 * S], ones32[:], big.ES[:, n % 2, h, :],
                                    start=True, stop=True)
                ins.then_inc(psum.filled(f"big.o{n}"), 1)

            def output(b):
                pe.wait_ge(*psum.copied(f"big.o{8 * b + 7}"))
                v = psum.take(pe, f"big.out{b}")
                for t in range(2):
                    for g in range(8):
                        ins = PE.matmul(v[:, tile(t)], big.OT[:, b % 2, g, tile(t)], W("L3_attn_w_out")[:, tile(g)],
                                        start=g == 0, stop=g == 7)
                ins.then_inc(psum.filled(f"big.out{b}"), 1)

            project(0)
            project(1)
            maxima(0)
            shifts(0)
            for n in range(GROUPS + 1):
                if n + 2 < GROUPS:
                    project(n + 2)
                if n + 1 < GROUPS:
                    maxima(n + 1)
                if n < GROUPS:
                    scores(n)
                if n + 1 < GROUPS:
                    shifts(n + 1)
                if n >= 1:
                    values(n - 1)
                if n >= 9 and n % 8 == 1:
                    output(n // 8 - 1)
            output(NB - 1)
            for c in range(NC):
                end_pe(pe, "big", c)

        def big_act(act):
            def copies(n):
                if n >= 3:
                    act.eng.wait_ge(*psum.made(f"big.e{n - 3}.1"))
                act.eng.wait_ge(*psum.made(f"big.qk{n}"))
                v = psum.view(f"big.qk{n}")
                A.copy(big.QT[:, n % 3], v[:, 0:S]).then_inc(act.step(), 1)
                for h in range(4):
                    ins = A.activation(big.KM[:, n % 3, h], v[:, S:2 * S], ACT.Copy, scale=head_of4[:, h:h + 1])
                    if h < 3:
                        ins.then_inc(act.step(), 1)
                ins.then_inc(act.read(f"big.qk{n}"), 1)
                if n >= 4:
                    act.eng.wait_ge(*psum.made(f"big.o{n - 4}"))
                act.eng.wait_ge(*psum.made(f"big.v{n}"))
                A.copy(big.VV[:, n % 4].rearrange("p a d -> p (a d)"),
                       psum.view(f"big.v{n}")[:, 0:2 * P]).then_inc(act.read(f"big.v{n}"), 1)

            def shift_copy(n):
                if n >= 2:
                    act.eng.wait_ge(*psum.made(f"big.e{n - 2}.1"))
                act.eng.wait_ge(*psum.made(f"big.hT{n}"))
                A.copy(big.HL[:, n % 2], psum.view(f"big.hT{n}").bitcast(BF16)[:, 0:2 * P])\
                    .then_inc(act.read(f"big.hT{n}"), 1)

            copies(0)
            copies(1)
            shift_copy(0)
            for n in range(GROUPS):
                if n + 2 < GROUPS:
                    copies(n + 2)
                for pair in range(2):
                    if n >= 2:
                        act.eng.wait_ge(*psum.made(f"big.o{n - 2}"))
                    act.eng.wait_ge(*psum.made(f"big.e{n}.{pair}"))
                    A.activation(big.E[:, n % 2, 2 * pair:2 * pair + 2].rearrange("p a b q -> p a (b q)"),
                                 psum.view(f"big.e{n}.{pair}"), ACT.Exp,
                                 scale=32 ** -0.5).then_inc(act.read(f"big.e{n}.{pair}"), 1)
                if n + 1 < GROUPS:
                    shift_copy(n + 1)
            for c in range(NC):
                end_act(act, "big", c)

        def big_dve(dve):
            def halves(n):
                if n >= 2:
                    dve.eng.wait_ge(*psum.made(f"big.m{n - 2}.1"))
                dve.eng.wait_ge(*psum.copied(f"big.qk{n}"))
                V.tensor_copy(big.Q16[:, n % 2], big.QT[:, n % 3]).then_inc(dve.step(), 1)
                V.tensor_copy(big.K16[:, n % 2], big.KM[:, n % 3].rearrange("p h k -> p (h k)")).then_inc(dve.flag("big.k16"), 1)

            def maxima(n):
                dve.eng.wait_ge(*dve.own())
                for pair in range(2):
                    dve.eng.wait_ge(*psum.made(f"big.m{n}.{pair}"))
                    v = psum.view(f"big.m{n}.{pair}").rearrange("p t (h k) -> p t h k", h=2)
                    V.tensor_reduce(big.mx[:, :, 2 * pair:2 * pair + 2], v, AX.X, ALU.max,
                                    negate=True).then_inc(dve.read(f"big.m{n}.{pair}"), 1)
                if n >= 2:
                    dve.eng.wait_ge(*psum.made(f"big.hT{n - 2}"))
                dve.eng.wait_ge(*dve.own())
                V.tensor_copy(shift_parts[:, n % 2, :, :, 0], big.mx).then_inc(dve.step(), 1)
                dve.eng.wait_ge(*dve.own())
                V.tensor_tensor(shift_parts[:, n % 2, :, :, 1], big.mx, shift_parts[:, n % 2, :, :, 0],
                                ALU.subtract).then_inc(dve.flag("big.shift"), 1)

            def divide(n):
                b, g = divmod(n, 8)
                dve.eng.wait_ge(*dve.own())
                dve.eng.wait_ge(*psum.made(f"big.o{n}"))
                v = psum.view(f"big.o{n}")
                V.reciprocal(big.rc, v[:, S:2 * S]).then_inc(dve.step(), 1)
                dve.eng.wait_ge(*dve.own())
                V.tensor_tensor(big.OT[:, b % 2, g], v[:, 0:S], big.rc, ALU.mult).then_inc(dve.read(f"big.o{n}"), 1)

            def biased(b):
                dve.eng.wait_ge(*psum.made(f"big.out{b}"))
                v = psum.view(f"big.out{b}")[:, 0:2 * P].rearrange("p (t d) -> p t d", t=2)
                V.tensor_tensor(R[:, 2 * b:2 * b + 2], v, bc(row("L3_attn_b_out"), 1, 2),
                                ALU.add).then_inc(dve.read(f"big.out{b}"), 1)

            halves(0)
            halves(1)
            maxima(0)
            for n in range(GROUPS + 1):
                if n >= 10 and n % 8 == 2:
                    biased(n // 8 - 1)
                if n + 1 < GROUPS:
                    maxima(n + 1)
                if n + 2 < GROUPS:
                    halves(n + 2)
                if n >= 1:
                    divide(n - 1)
            biased(NB - 1)
            for c in range(NC):
                norm_stats(dve, c, R[:, ctiles(c)], "bign", 1e-6)
            for c in range(NC):
                y, r = big.Y[:, ctiles(c)], R[:, ctiles(c)]
                norm_apply(dve, c, r, y, "bign")
                dve.eng.wait_ge(*dve.own())
                V.tensor_tensor(y, y, bc(row("L3_attn_ln_gamma"), 1, 4), ALU.mult).then_inc(dve.step(), 1)
                dve.eng.wait_ge(*dve.own())
                V.tensor_tensor(y, y, bc(row("L3_attn_ln_beta"), 1, 4), ALU.add).then_inc(dve.step(), 1)
                dve.eng.wait_ge(*dve.own())
                V.tensor_tensor(r, y, X[:, ctiles(c)], ALU.add).then_inc(dve.step(), 1)
            end_dve(dve, "big")

        def big_pool(pool):
            for n in range(GROUPS):
                if n >= 2:
                    pool.eng.wait_ge(*psum.made(f"big.o{n - 2}"))
                pool.eng.wait_ge(*psum.copied(f"big.e{n}.1"))
                G.tensor_tensor(big.ES[:, n % 2], big.E[:, n % 2, :, 0], big.E[:, n % 2, :, 1],
                                ALU.add).then_inc(pool.flag("big.sums"), 1)
            for c in range(NC):
                norm_rstd(pool, c, "bign")
            end_pool(pool, "big")

        def absmax_dve(dve):
            for c in range(NC):
                norm_stats(dve, c, X[:, ctiles(c)], "fin", EPS)
            for c in range(NC):
                y = R[:, ctiles(c)]
                normed_dve(dve, c, X[:, ctiles(c)], y, "fin")
                dve.eng.wait_ge(*dve.own())
                V.tensor_reduce(ABSMAX[:, bass.ds(step * NT + 4 * c, 4)], y, AX.X, ALU.max,
                                        apply_absolute_value=True).then_inc(dve.step(), 1)
                V.tensor_copy(XALL[:, bass.ds(step * NT + 4 * c, 4), :], X[:, ctiles(c)]).then_inc(dve.step(), 1)

        def normed_dve(dve, c, src, y, name):
            norm_apply(dve, c, src, y, name)
            dve.eng.wait_ge(*dve.own())
            V.tensor_tensor(y, y, bc(row("L3_ffn_gamma"), 1, 4), ALU.mult).then_inc(dve.step(), 1)
            dve.eng.wait_ge(*dve.own())
            V.tensor_tensor(y, y, bc(row("L3_ffn_beta"), 1, 4), ALU.add).then_inc(dve.step(), 1)

        def absmax_pool(pool):
            for c in range(NC):
                norm_rstd(pool, c, "fin")


        NCH = B // 2

        class last:
            a = Carve(False)
            amax, scale, inv, f = a(1), a(1), a(1), a(1)
            wsum, wtot, delta, ndelta = a(1), a(1), a(1), a(1)
            tern, neg, aw = a(D), a(D), a(D)
            sums, tots = a(2), a(2)
            tern16 = a(D, dt=BF16)
            Q = a(2, 4, D)
            Q16 = a(NCH, 4, D, dt=BF16)
            QT = a(NCH, 4 * P, dt=BF16)
            RR = a(NCH, 4, D)
            OUT = a(NCH, 4, D)

        def last_ffn():
            ROUND = 1.5 * 2.0 ** 23
            RMAX, RADD = bass.bass_isa.ReduceOp.max, bass.bass_isa.ReduceOp.add
            psum.reset()
            with nc.Block(no_gpsimd_drain=True) as block:
                @block.tensor
                def _(pe):
                    for c in range(NCH):
                        pe.wait_ge(sig("last.q"), c + 1)
                        v = psum.take(pe, f"last.qT{c}").bitcast(BF16)
                        for t in range(4):
                            ins = PE.transpose(v[:, tile(t)], last.Q16[:, c, t], ident16[:])
                        ins.then_inc(psum.filled(f"last.qT{c}"), 1)
                    pe.wait_ge(sig("last.tern16"), 1)
                    for c in range(NCH):
                        pe.wait_ge(*psum.copied(f"last.qT{c}"))
                        v = psum.take(pe, f"last.y{c}")
                        for t in range(4):
                            ins = PE.matmul(v[:, tile(t)], last.QT[:, c, tile(t)], last.tern16, start=True, stop=True)
                        ins.then_inc(psum.filled(f"last.y{c}"), 1)

                @block.gpsimd
                def _(eng):
                    pool = Own(eng, pool_step, psum, sig)
                    eng.wait_ge(sig("last.rowmax"), 1)
                    G.partition_all_reduce(last.scale, last.amax, P, RMAX).then_inc(pool.flag("last.max"), 1)
                    eng.wait_ge(sig("last.wrows"), 1)
                    G.partition_all_reduce(last.wtot, last.wsum, P, RADD).then_inc(pool.flag("last.wsum"), 1)
                    eng.wait_ge(sig("last.sums"), 1)
                    G.partition_all_reduce(last.tots, last.sums, P, RADD).then_inc(pool.flag("last.tots"), 1)
                    for c in range(NCH):
                        norm_rstd(pool, c, "fin")
                    for c in range(NCH):
                        norm_rstd(pool, c, "last")

                @block.vector
                def _(eng):
                    dve = Own(eng, dve_step, psum, sig)
                    w = W("L3_ffn_weight")
                    V.tensor_reduce(last.amax, ABSMAX[:], AX.X, ALU.max).then_inc(dve.flag("last.rowmax"), 1)
                    V.tensor_reduce(last.wsum, w, AX.X, ALU.add, apply_absolute_value=True).then_inc(dve.flag("last.wrows"), 1)
                    eng.wait_ge(sig("last.wsum"), 1)
                    V.tensor_scalar(last.delta, last.wtot, 1.0 / (D * D), 0.7, ALU.mult, ALU.mult).then_inc(dve.step(), 1)
                    dve.eng.wait_ge(*dve.own())
                    V.tensor_scalar(last.ndelta, last.delta, -1.0, None, ALU.mult).then_inc(dve.step(), 1)
                    V.tensor_scalar(last.tern, w, last.delta, None, ALU.is_gt).then_inc(dve.step(), 1)
                    dve.eng.wait_ge(*dve.own())
                    V.tensor_scalar(last.neg, w, last.ndelta, None, ALU.is_lt).then_inc(dve.step(), 1)
                    dve.eng.wait_ge(*dve.own())
                    V.tensor_tensor(last.tern, last.tern, last.neg, ALU.subtract).then_inc(dve.step(), 1)
                    dve.eng.wait_ge(*dve.own())
                    V.tensor_copy(last.tern16, last.tern).then_inc(dve.flag("last.tern16"), 1)
                    V.tensor_tensor(last.aw, last.tern, w, ALU.mult).then_inc(dve.step(), 1)
                    V.tensor_reduce(last.sums[:, 1:2], last.tern, AX.X, ALU.add, apply_absolute_value=True).then_inc(dve.step(), 1)
                    dve.eng.wait_ge(*dve.own())
                    V.tensor_reduce(last.sums[:, 0:1], last.aw, AX.X, ALU.add).then_inc(dve.flag("last.sums"), 1)
                    eng.wait_ge(sig("last.tots"), 1)
                    V.tensor_scalar(last.tots[:, 1:2], last.tots[:, 1:2], 1.0, None, ALU.max).then_inc(dve.step(), 1)
                    eng.wait_ge(sig("last.max"), 1)
                    V.tensor_scalar(last.scale, last.scale, 1e-8, 1.0 / 127, ALU.max, ALU.mult).then_inc(dve.step(), 1)
                    dve.eng.wait_ge(*dve.own())
                    V.reciprocal(last.inv, last.scale).then_inc(dve.step(), 1)
                    V.reciprocal(last.f, last.tots[:, 1:2]).then_inc(dve.step(), 1)
                    dve.eng.wait_ge(*dve.own())
                    V.tensor_tensor(last.f, last.f, last.tots[:, 0:1], ALU.mult).then_inc(dve.step(), 1)
                    dve.eng.wait_ge(*dve.own())
                    V.tensor_tensor(last.f, last.f, last.scale, ALU.mult).then_inc(dve.step(), 1)
                    for c in range(NCH):
                        norm_stats(dve, c, XALL[:, ctiles(c)], "fin", EPS)
                    for c in range(NCH):
                        q = last.Q[:, c % 2]
                        normed_dve(dve, c, XALL[:, ctiles(c)], q, "fin")
                        dve.eng.wait_ge(*dve.own())
                        V.tensor_scalar(q, q, last.inv, 127.0, ALU.mult, ALU.min).then_inc(dve.step(), 1)
                        dve.eng.wait_ge(*dve.own())
                        V.tensor_scalar(q, q, -127.0, ROUND, ALU.max, ALU.add).then_inc(dve.step(), 1)
                        dve.eng.wait_ge(*dve.own())
                        V.tensor_scalar(last.Q16[:, c], q, ROUND, None, ALU.subtract).then_inc(dve.flag("last.q"), 1)
                    for c in range(NCH):
                        eng.wait_ge(*psum.made(f"last.y{c}"))
                        v = psum.view(f"last.y{c}")
                        V.scalar_tensor_tensor(last.RR[:, c].rearrange("p t d -> p (t d)"), v, last.f,
                                                         XALL[:, ctiles(c)].rearrange("p t d -> p (t d)"),
                                                         ALU.mult, ALU.add).then_inc(dve.read(f"last.y{c}"), 1)
                        norm_stats(dve, c, last.RR[:, c], "last", EPS)
                    for c in range(NCH):
                        norm_apply(dve, c, last.RR[:, c], last.OUT[:, c], "last", "last.out")

                @block.scalar
                def _(eng):
                    act = Own(eng, act_step, psum, sig)
                    for c in range(NCH):
                        eng.wait_ge(*psum.made(f"last.qT{c}"))
                        v = psum.view(f"last.qT{c}").bitcast(BF16)
                        A.copy(last.QT[:, c], v[:, 0:4 * P]).then_inc(act.read(f"last.qT{c}"), 1)

                @block.sync
                def _(sp):
                    for c in range(NCH):
                        sp.wait_ge(sig("last.out"), c + 1)
                        sp.dma_start(out[:, ctiles(c), :], last.OUT[:, c]).then_inc(x_stored, 16)
                    sp.wait_ge(x_stored, 16 * NCH)

        LOADS = 6

        def clear_counts():
            counts = sorted(s.num for s in bank_full + bank_read + [pe_step, dve_step, act_step, pool_step, loaded]
                            + list(signals.values()))
            assert counts == list(range(counts[0], counts[-1] + 1))
            nc.sync.sem_clear(range(counts[0], counts[-1] + 1))
            nc.all_engine_barrier(sem_only=True)

        x0 = Cross("x0", "L0_xattn", "ret", True, 0, KEEP0, 0)
        moe0 = Moe("moe0", "L0_ffn", "x0", False, 1, 2, 4, 0, True)
        moe1 = Moe("moe1", "L1_ffn", "one", True, 4, 4, 2, 1, False)
        x2 = Cross("x2", "L2_xattn", "spm", True, 5, None, 0)
        x3 = Cross("x3", "L3_xattn", "big", True, 6, KEEP3, 1)

        with nc.Fori(0, STEPS) as step:
            with nc.Block(no_gpsimd_drain=True) as block:
                @block.sync
                def _(sp):
                    sp.dma_start(X[:], x[:, bass.ds(step * NT, NT), :]).then_inc(loaded, 16)
                    sp.dma_start(XT[:], x_t[:, bass.ds(step * T, T)]).then_inc(loaded, 16)
                    sp.dma_start(CT[:], ctx_t[:, bass.ds(step * NB, NB), :]).then_inc(loaded, 16)
                    sp.dma_start(CD[:], ctx_d[:, bass.ds(step * NB, NB), :]).then_inc(loaded, 16)
                    sp.dma_start(KEEP0[:], keep0[bass.ds(step * NB, NB), :].partition_broadcast(P)).then_inc(loaded, 16)
                    sp.dma_start(KEEP3[:], keep3[bass.ds(step * NB, NB), :].partition_broadcast(P)).then_inc(loaded, 16)

                @block.tensor
                def _(eng):
                    retention_pe(eng)
                    x0.pe(eng)
                    moe0.pe(eng)
                    cosine_pe(eng)
                    one_pe(eng)
                    moe1.pe(eng)
                    sparse_pe(eng)
                    x2.pe(eng)
                    lora_pe(eng)
                    big_pe(eng)
                    x3.pe(eng)

                @block.scalar
                def _(eng):
                    act = Own(eng, act_step, psum, sig)
                    retention_act(act)
                    x0.act(act)
                    moe0.act(act)
                    cosine_act(act)
                    one_act(act)
                    moe1.act(act)
                    sparse_act(act)
                    x2.act(act)
                    lora_act(act)
                    big_act(act)
                    x3.act(act)

                @block.vector
                def _(eng):
                    eng.wait_ge(loaded, LOADS * 16)
                    dve = Own(eng, dve_step, psum, sig)
                    retention_dve(dve)
                    x0.dve(dve)
                    moe0.dve(dve)
                    cosine_dve(dve)
                    one_dve(dve)
                    moe1.dve(dve)
                    sparse_dve(dve)
                    x2.dve(dve)
                    lora_dve(dve)
                    big_dve(dve)
                    x3.dve(dve)
                    absmax_dve(dve)

                @block.gpsimd
                def _(eng):
                    pool = Own(eng, pool_step, psum, sig)
                    retention_pool(pool)
                    x0.pool(pool)
                    moe0.pool(pool)
                    cosine_pool(pool)
                    one_pool(pool)
                    moe1.pool(pool)
                    sparse_pool(pool)
                    x2.pool(pool)
                    lora_pool(pool)
                    big_pool(pool)
                    x3.pool(pool)
                    absmax_pool(pool)
            clear_counts()

        last_ffn()


def kernel(**inputs):
    import numpy as _np
    import concourse.bacc as _bacc
    from concourse import mybir as _mybir
    from concourse.bass_utils import run_bass_kernel_spmd as _run

    i = {n: _np.asarray(a) for n, a in inputs.items()}
    blocks = lambda w, j: w.reshape(j, 128, -1).transpose(1, 0, 2).reshape(128, -1)
    experts_in = lambda w: w.transpose(1, 0, 2).reshape(128, -1)
    experts_out = lambda w: blocks(w.reshape(-1, 128), w.shape[0] * w.shape[1] // 128)
    turned = {"L0_xattn_Wq", "L0_xattn_Wk", "L0_xattn_Wv", "L0_xattn_Wo", "L1_attn_Wq", "L1_attn_Wk", "L1_attn_Wv",
              "L1_attn_W1", "L1_attn_W2", "L2_attn_Wq", "L2_attn_Wk", "L2_attn_Wv", "L2_ffn_gate_w", "L2_ffn_base_w",
              "L3_xattn_Wq", "L3_xattn_Wk", "L3_xattn_Wv", "L3_xattn_Wo", "L3_ffn_weight"}

    def laid(n):
        w = i[n]
        if n in turned:
            return w.T
        if n in ("L0_ffn_W1", "L1_ffn_W1"):
            return experts_in(w)
        if n in ("L0_ffn_W2", "L1_ffn_W2"):
            return experts_out(w)
        if n == "L1_attn_W3":
            return blocks(w.T, 4)
        if n == "L3_attn_w_out":
            return blocks(w, 8)
        if n == "L2_ffn_lora_A":
            return w.reshape(128, 128).T
        if n == "L2_ffn_lora_B":
            return w.transpose(0, 2, 1).reshape(128, 128)
        return w

    weights = _np.concatenate([laid(n) for cols in W_COLS for n, _ in cols], axis=1)
    bcols = _np.concatenate([i[n].reshape(-1, 128).T for n, _ in B_COLS], axis=1)
    rows = _np.concatenate([i[n].reshape(-1) for n, _ in ROWS])
    ctx_t = i["ctx_1024"].transpose(2, 0, 1)
    arrays = {
        "x": i["x"].reshape(B * S // 128, 128, D).transpose(1, 0, 2),
        "x_t": i["x"].reshape(B * S, D).T,
        "ctx_t": ctx_t,
        "ctx_d": _np.concatenate([ctx_t, ctx_t], axis=2),
        "keep0": i["mask_BxS2_ik0"],
        "keep3": i["mask_BxS2_bf1"].view(_np.uint8),
        "weights": weights, "bcols": bcols, "rows": rows,
        "b2s": _np.stack([i["L0_ffn_b2"], i["L1_ffn_b2"]]),
    }
    nc = _bacc.Bacc("TRN2", target_bir_lowering=False, num_devices=1)
    args = []
    for name in arrays:
        arrays[name] = _np.ascontiguousarray(arrays[name])
        a = arrays[name]
        args.append(nc.dram_tensor(f"in_{name}", a.shape, _mybir.dt.from_np(a.dtype), kind="ExternalInput").ap())
    args.append(nc.dram_tensor("out_0_dram", (P, B * S // P, D), F32, kind="ExternalOutput").ap())
    decoder(nc, *args)
    r = _run(nc, [{f"in_{n}": a for n, a in arrays.items()}], core_ids=[0])
    return r.results[0]["out_0_dram"].transpose(1, 0, 2).reshape(B, S, D)
```

```python
import numpy as np
import concourse.bass as bass
from concourse import mybir
from contextlib import ExitStack

ALU = mybir.AluOpType
ACT = mybir.ActivationFunctionType
AX = mybir.AxisListType
F32 = mybir.dt.float32
BF16 = mybir.dt.bfloat16
I32 = mybir.dt.int32
U32 = mybir.dt.uint32
U8 = mybir.dt.uint8

B, S, D, SK = 8, 256, 128, 64
P = 128
BATCHES_PER_STEP = 4
NB = BATCHES_PER_STEP
STEPS = B // NB
NC = NB // 2
T = NB * S
NT = T // P
CH = 512
LOADS = 4
EPS = 1e-5

W_COLS = [
    [("L0_attn_Wq", 128), ("L0_attn_Wk", 128), ("L0_attn_Wv", 128), ("L0_attn_W_G", 128), ("L0_attn_W_O", 128),
     ("L0_xattn_Wq", 128), ("L0_xattn_Wk", 128), ("L0_xattn_Wv", 128), ("L0_xattn_Wo", 128), ("L0_ffn_Wr", 8)],
    [("L0_ffn_W1", 8 * 512)],
    [("L0_ffn_W2", 32 * 128)],
    [("L1_attn_Wq", 128), ("L1_attn_Wk", 128), ("L1_attn_Wv", 128), ("L1_attn_W1", 128), ("L1_attn_W2", 512),
     ("L1_attn_W3", 512), ("L1_xattn_key_matrix", 128), ("L1_xattn_value_matrix", 128), ("L1_ffn_Wr", 8)],
    [("L1_ffn_W1", 8 * 256), ("L1_ffn_W2", 16 * 128)],
    [("L2_attn_Wq", 128), ("L2_attn_Wk", 128), ("L2_attn_Wv", 128),
     ("L2_xattn_Wq", 128), ("L2_xattn_Wk", 128), ("L2_xattn_Wv", 128), ("L2_xattn_Wo", 128),
     ("L2_ffn_gate_w", 10), ("L2_ffn_lora_A", 128), ("L2_ffn_lora_B", 128), ("L2_ffn_base_w", 128)],
    [("L3_attn_w_qkv", 3072), ("L3_attn_w_out", 1024),
     ("L3_xattn_Wq", 128), ("L3_xattn_Wk", 128), ("L3_xattn_Wv", 128), ("L3_xattn_Wo", 128),
     ("L3_ffn_weight", 128)],
]
W_AT, W_GROUP, _at = {}, {}, 0
GROUP_AT = []
for _g, _cols in enumerate(W_COLS):
    GROUP_AT.append(_at)
    for _n, _w in _cols:
        W_AT[_n], W_GROUP[_n] = (_at, _w), _g
        _at += _w
GROUP_AT.append(_at)
W_TOTAL = _at
B_COLS = [("L0_xattn_bq", 1), ("L0_xattn_bk", 1), ("L0_ffn_b1", 32), ("L1_attn_b1", 1), ("L1_attn_b2", 4),
          ("L1_ffn_b1", 16), ("L2_xattn_bq", 1), ("L2_xattn_bk", 1), ("L3_xattn_bq", 1), ("L3_xattn_bk", 1)]
ROWS = [("L0_xattn_bv", 128), ("L0_xattn_bo", 128), ("L0_ffn_br", 8), ("L1_attn_bq", 128), ("L1_attn_bk", 128),
        ("L1_attn_bv", 128), ("L1_attn_b3", 128), ("L1_ffn_br", 8), ("L2_xattn_bv", 128), ("L2_xattn_bo", 128),
        ("L2_ffn_base_b", 128), ("L3_attn_b_out", 128), ("L3_attn_ln_gamma", 128), ("L3_attn_ln_beta", 128),
        ("L3_xattn_bv", 128), ("L3_xattn_bo", 128), ("L3_ffn_gamma", 128), ("L3_ffn_beta", 128)]


def spots(cols):
    at, out = 0, {}
    for n, w in cols:
        out[n] = (at, w)
        at += w
    return out, at


B_AT, B_TOTAL = spots(B_COLS)
R_AT, R_TOTAL = spots(ROWS)

GAMMA = [1.0 - 2.0 ** (-5.0 - h) for h in range(8)]


def bf16_parts(value):
    parts = []
    for _ in range(3):
        part = (np.array(value, np.float32).view(np.uint32) & np.uint32(0xFFFF0000)).view(np.float32)
        parts.append(float(part))
        value = value - float(part)
    assert value == 0
    return parts


class Psum:

    def __init__(self, banks, full, read):
        self.banks, self.full, self.read_ = banks, full, read
        self.reset()

    def reset(self):
        self.next, self.place, self.uses, self.last, self.open = 0, {}, [0] * 8, [None] * 8, set()

    def take(self, pe, name, n=1):
        k = self.next
        while k + n > 8 or any(self.last[j] in self.open for j in range(k, k + n)):
            k = 0 if k + n > 8 else k + 1
        self.next = (k + n) % 8
        for old in {self.last[j] for j in range(k, k + n)} - {None}:
            first, count = self.place[old][0], self.place[old][2]
            pe.wait_ge(self.read_[first], count)
        self.uses[k] += 1
        self.place[name] = (k, n, self.uses[k])
        self.open.add(name)
        for j in range(k, k + n):
            self.last[j] = name
        return self.view(name)

    def view(self, name):
        k, n, _ = self.place[name]
        return self.banks[:, k] if n == 1 else self.banks[:, k:k + n]

    def filled(self, name):
        self.open.discard(name)
        return self.full[self.place[name][0]]

    def made(self, name):
        k, _, count = self.place[name]
        return self.full[k], count

    def copied(self, name):
        k, _, count = self.place[name]
        return self.read_[k], count


class Own:

    def __init__(self, eng, step_sem, psum, sig):
        self.eng, self.step_sem, self.psum, self.sig = eng, step_sem, psum, sig
        self.count, self.last = {}, (step_sem, 0)

    def _next(self, sem, name):
        self.count[name] = self.count.get(name, 0) + 1
        self.last = (sem, self.count[name])
        return sem

    def step(self):
        return self._next(self.step_sem, "step")

    def flag(self, name):
        return self._next(self.sig(name), name)

    def read(self, product):
        self.last = self.psum.copied(product)
        return self.last[0]

    def own(self):
        return self.last


def decoder(nc, x, ctx_t, ctx_d, keep0, keep3, weights, bcols, rows, b2s, out):
    ctx = ExitStack()
    with ctx:
        sb = lambda n, s, d=F32: ctx.enter_context(nc.sbuf_tensor(n, s, d))
        sem = lambda n: ctx.enter_context(nc.semaphore(n))

        x_loaded = sem("x_loaded")
        w_loaded = [sem(f"w_loaded{g}") for g in range(len(W_COLS))]
        small_loaded, consts_made, x_stored = sem("small_loaded"), sem("consts_made"), sem("x_stored")
        setup_step, heads_made = sem("setup_step"), sem("heads_made")
        bank_full = [sem(f"bank_full{k}") for k in range(8)]
        bank_read = [sem(f"bank_read{k}") for k in range(8)]
        pe_step, dve_step, act_step, pool_step = (sem(n) for n in ("pe_step", "dve_step", "act_step", "pool_step"))
        loaded = sem("loaded")
        signals = {}

        def sig(name):
            if name not in signals:
                signals[name] = sem(name)
            return signals[name]

        psum = Psum(ctx.enter_context(nc.psum_tensor("banks", [P, 8, CH], F32)), bank_full, bank_read)

        WS = sb("WS", [P, W_TOTAL])
        W = lambda n: WS[:, W_AT[n][0]:W_AT[n][0] + W_AT[n][1]]
        BC = sb("BC", [P, B_TOTAL])
        bcol = lambda n, j=0: BC[:, B_AT[n][0] + j:B_AT[n][0] + j + 1]
        RW = sb("RW", [P, R_TOTAL])
        row = lambda n: RW[:, R_AT[n][0]:R_AT[n][0] + R_AT[n][1]]
        B2 = sb("B2", [8, 2, D])
        ident = sb("ident", [P, P])
        ident16 = sb("ident16", [P, P], BF16)
        ones16 = sb("ones16", [P, P], BF16)
        ones32 = sb("ones32", [P, 32])
        decay = sb("decay", [P, 8, S])
        head_of8 = sb("head_of8", [P, 16])
        head_of16 = sb("head_of16", [P, 8])
        shift_parts = sb("shift_parts", [P, 2, 2, 4, 32], BF16)
        head_of4 = sb("head_of4", [P, 4])
        pick = sb("pick", [P, 4, P], BF16)
        fills = sb("fills", [3, 2])
        expert = sb("expert", [P, 8])
        minus_half = sb("minus_half", [P, 32])
        zeros = sb("zeros", [P, S])
        XALL = sb("XALL", [P, B * S // P, D])
        ABSMAX = sb("ABSMAX", [P, B * S // P])

        X = sb("X", [P, NT, D])
        R = sb("R", [P, NT, D])
        XB = sb("XB", [P, NT, D])
        XT = sb("XT", [P, T])
        CT = sb("CT", [P, NB, SK])
        CD = sb("CD", [P, NB, 2 * SK])
        KEEP0 = sb("KEEP0", [P, NB, SK], I32)
        KEEP3 = sb("KEEP3", [P, NB, SK], U8)
        st = sb("st", [P, 16, 6])
        mv = sb("mv", [P, 16, 2])
        var = sb("var", [P, 16])
        rstd = sb("rstd", [P, 16])
        ARENA = (nc.sbuf_bytes_remaining - 64) // 4
        arena = sb("arena", [P, ARENA])

        class Carve:

            def __init__(self, top):
                self.top, self.at = top, ARENA if top else 0

            def __call__(self, *shape, dt=F32, parts=P):
                n = int(np.prod(shape))
                words = n if dt in (F32, I32, U32) else (n + 1) // 2
                if self.top:
                    self.at -= words
                a = arena[0:parts, self.at:self.at + words]
                if not self.top:
                    self.at += words
                assert 0 <= self.at <= ARENA, (self.at, shape)
                if dt not in (F32,):
                    a = a.bitcast(dt)
                if len(shape) > 1:
                    names = "abcd"[:len(shape)]
                    a = a.rearrange(f"p ({' '.join(names)}) -> p {' '.join(names)}", **dict(zip(names, shape)))
                return a

        def bc(ap, axis, n):
            a = ap.unsqueeze(axis)
            shape = list(a.shape)
            shape[axis] = n
            return a.broadcast_to(shape)

        tile = lambda t: slice(t * P, (t + 1) * P)
        chunk = lambda c: slice(c * CH, (c + 1) * CH)
        ctiles = lambda c: slice(4 * c, 4 * c + 4)

        with nc.Block(no_gpsimd_drain=True) as block:
            @block.sync
            def _(sp):
                sp.dma_start(RW[:], rows.partition_broadcast(P)).then_inc(small_loaded, 16)
                sp.dma_start(BC[:], bcols).then_inc(small_loaded, 16)
                sp.dma_start(B2[:], b2s.rearrange("l e d -> e l d")).then_inc(small_loaded, 16)
                sp.dma_start(XALL[:], x).then_inc(x_loaded, 16)
                for g in range(len(W_COLS)):
                    a, b = GROUP_AT[g], GROUP_AT[g + 1]
                    sp.dma_start(WS[:, a:b], weights[:, a:b]).then_inc(w_loaded[g], 16)

            @block.gpsimd
            def _(pool):
                pool.memset(ident[:], 0.0).then_inc(setup_step, 1)
                pool.memset(head_of8[:], 1.0).then_inc(setup_step, 1)
                pool.memset(head_of16[:], 0.0).then_inc(setup_step, 1)
                pool.memset(shift_parts[:], 0.0).then_inc(setup_step, 1)
                pool.memset(ones32[:], 1.0).then_inc(setup_step, 1)
                pool.memset(minus_half[:], -0.5).then_inc(setup_step, 1)
                pool.memset(zeros[:], 0.0).then_inc(setup_step, 1)
                pool.iota(expert[:], [[1, 8]], base=0, channel_multiplier=0,
                          allow_small_or_imprecise_dtypes=True).then_inc(setup_step, 1)
                for h in range(8):
                    pool.iota(decay[:, h, :], [[1, S]], base=0, channel_multiplier=-1,
                              allow_small_or_imprecise_dtypes=True).then_inc(setup_step, 1)
                pool.memset(fills[:], 0.0).then_inc(setup_step, 1)
                pool.memset(ones16[:], 1.0).then_inc(setup_step, 1)
                pool.wait_ge(setup_step, 18)
                pool.affine_select(ident[:], ident[:], pattern=[[-1, P]], compare_op=ALU.not_equal, fill=1.0,
                                   base=0, channel_multiplier=1).then_inc(setup_step, 1)
                pool.wait_ge(setup_step, 19)
                pool.affine_select(head_of8[:], head_of8[:], pattern=[[-8, 16]], compare_op=ALU.is_ge, fill=0.0,
                                   base=0, channel_multiplier=1).then_inc(setup_step, 1)
                pool.wait_ge(setup_step, 20)
                pool.affine_select(head_of8[:], head_of8[:], pattern=[[8, 16]], compare_op=ALU.is_ge, fill=0.0,
                                   base=7, channel_multiplier=-1).then_inc(setup_step, 1)
                pool.tensor_copy(ident16[:], ident[:]).then_inc(setup_step, 1)
                for col, value in enumerate((1e9, 1e8)):
                    for j, part in enumerate(bf16_parts(value)):
                        pool.wait_ge(setup_step, 22 + 3 * col + j)
                        pool.affine_select(fills[:, col:col + 1], fills[:, col:col + 1], pattern=[[0, 1]],
                                           compare_op=ALU.not_equal, fill=part, base=-j,
                                           channel_multiplier=1).then_inc(setup_step, 1)
                pool.wait_ge(consts_made, 8)
                for h in range(8):
                    pool.affine_select(decay[:, h, :], decay[:, h, :], pattern=[[1, S]], compare_op=ALU.is_ge,
                                       fill=0.0, base=0, channel_multiplier=-1).then_inc(setup_step, 1)
                pool.wait_ge(setup_step, 36)

            @block.scalar
            def _(act):
                act.wait_ge(setup_step, 17)
                for h in range(8):
                    nc.scalar.activation(decay[:, h, :], decay[:, h, :], ACT.Exp,
                                         scale=float(np.log(GAMMA[h]))).then_inc(consts_made, 1)

            @block.vector
            def _(dve):
                dve.wait_ge(setup_step, 22)
                nc.vector.tensor_reduce(head_of16[:], head_of8[:].rearrange("p (h b) -> p h b", b=2), AX.X,
                                        ALU.add).then_inc(heads_made, 1)
                nc.vector.tensor_reduce(head_of4[:], head_of8[:].rearrange("p (h b) -> p h b", b=4), AX.X,
                                        ALU.add).then_inc(heads_made, 1)
                dve.wait_ge(heads_made, 2)
                nc.vector.tensor_copy(pick[:], bc(head_of4[:], 2, P)).then_inc(heads_made, 1)
                dve.wait_ge(small_loaded, 48)

        V, A, G, PE = nc.vector, nc.scalar, nc.gpsimd, nc.tensor


        def norm_stats(dve, c, src, name, eps):
            dve.eng.wait_ge(*dve.own())
            for t in range(4):
                V.bn_stats(st[:, 4 * c + t, :], src[:, t, :]).then_inc(dve.step(), 1)
            dve.eng.wait_ge(*dve.own())
            for t in range(4):
                V.bn_aggr(mv[:, 4 * c + t, :], st[:, 4 * c + t, :]).then_inc(dve.step(), 1)
            dve.eng.wait_ge(*dve.own())
            V.tensor_scalar(var[:, ctiles(c)], mv[:, ctiles(c), 1], eps, None, ALU.add).then_inc(dve.flag(name + ".var"), 1)

        def norm_rstd(pool, c, name):
            pool.eng.wait_ge(sig(name + ".var"), c + 1)
            G.tensor_tensor(rstd[:, ctiles(c)], var[:, ctiles(c)], minus_half[:, 0:4], ALU.pow).then_inc(pool.flag(name + ".rstd"), 1)

        def norm_apply(dve, c, src, dst, name, ready=None):
            dve.eng.wait_ge(sig(name + ".rstd"), c + 1)
            for t in range(4):
                i = 4 * c + t
                ins = V.tensor_scalar(dst[:, t, :], src[:, t, :], mv[:, i, 0:1], rstd[:, i:i + 1],
                                      ALU.subtract, ALU.mult)
                if t == 3 and ready:
                    ins.then_inc(dve.flag(ready), 1)
                else:
                    ins.then_inc(dve.step(), 1)

        def end_sum_dve(dve, L, c, product=None, base=None):
            if product:
                if base is XB:
                    dve.eng.wait_ge(sig(L + ".xb"), c + 1)
                dve.eng.wait_ge(*psum.made(f"{product}{c}"))
                ps = psum.view(f"{product}{c}")
                V.tensor_tensor(R[:, ctiles(c)], ps.rearrange("p (t d) -> p t d", t=4),
                                base[:, ctiles(c)], ALU.add).then_inc(dve.read(f"{product}{c}"), 1)
            norm_stats(dve, c, R[:, ctiles(c)], L, EPS)

        def end_norm_dve(dve, L, c):
            norm_apply(dve, c, R[:, ctiles(c)], X[:, ctiles(c)], L, L + ".x")

        def end_dve(dve, L, product=None, base=None):
            for c in range(NC):
                end_sum_dve(dve, L, c, product, base)
            for c in range(NC):
                end_norm_dve(dve, L, c)

        def end_pool(pool, L):
            for c in range(NC):
                norm_rstd(pool, c, L)

        def end_pe(pe, L, c):
            pe.wait_ge(sig(L + ".x"), c + 1)
            v = psum.take(pe, f"{L}.xT{c}")
            for t in range(4):
                ins = PE.transpose(v[:, tile(t)], X[:, 4 * c + t, :], ident[:])
            ins.then_inc(psum.filled(f"{L}.xT{c}"), 1)

        def end_act(act, L, c):
            act.eng.wait_ge(*psum.made(f"{L}.xT{c}"))
            A.copy(XT[:, chunk(c)], psum.view(f"{L}.xT{c}")).then_inc(act.read(f"{L}.xT{c}"), 1)

        def add_bias_pool(pool, L, before, bias, chunks=range(NC)):
            for c in chunks:
                pool.eng.wait_ge(sig(before + ".x"), c + 1)
                G.tensor_tensor(XB[:, ctiles(c)], X[:, ctiles(c)], bc(row(bias), 1, 4), ALU.add).then_inc(pool.flag(L + ".xb"), 1)

        def x_t_ready(pe, before, c):
            pe.wait_ge(*psum.copied(f"{before}.xT{c}"))

        def project_out_pe(pe, name, src_t, w, c):
            pe.wait_ge(*psum.copied(f"{name}T{c}"))
            v = psum.take(pe, f"{name}.out{c}")
            for t in range(4):
                ins = PE.matmul(v[:, tile(t)], src_t[:, tile(4 * c + t)], w, start=True, stop=True)
            ins.then_inc(psum.filled(f"{name}.out{c}"), 1)

        def turn_pe(pe, name, src, c):
            v = psum.take(pe, f"{name}T{c}")
            for t in range(4):
                ins = PE.transpose(v[:, tile(t)], src[:, 4 * c + t, :], ident[:])
            ins.then_inc(psum.filled(f"{name}T{c}"), 1)

        def move_act(act, product, dst):
            act.eng.wait_ge(*psum.made(product))
            v = psum.view(product)
            A.copy(dst, v).then_inc(act.read(product), 1)

        def tokens_dve(eng, dve):
            eng.wait_ge(x_loaded, 16)
            for c in range(NC):
                V.tensor_copy(X[:, ctiles(c)], XALL[:, bass.ds(step * NT + 4 * c, 4), :]).then_inc(dve.flag("in.x"), 1)

        PAIRS = 4 * NB

        class ret:
            a = Carve(False)
            QT, KT = a(T), a(T)
            KM = a(4, 2, S)
            VG = a(NT, 2 * D)
            SG = a(NT, D)
            SD = a(4, 2, 384)
            PV = a(2, S)
            SQ = a(16, 16)
            m, v = a(NC, 32), a(NC, 32)
            rs = a(NC, 32)
            Y = R
            YT = QT

        def retention_pe(pe):
            for c in range(NC):
                end_pe(pe, "in", c)
            pe.wait_ge(w_loaded[0], 16)
            for c in range(NC):
                x_t_ready(pe, "in", c)
                for n, w in (("q", "L0_attn_Wq"), ("k", "L0_attn_Wk")):
                    v = psum.take(pe, f"ret.{n}{c}")
                    PE.matmul(v, W(w), XT[:, chunk(c)], start=True, stop=True).then_inc(psum.filled(f"ret.{n}{c}"), 1)
                w0 = W_AT["L0_attn_Wv"][0]
                for half in range(2):
                    v = psum.take(pe, f"ret.vg{c}{half}")
                    for t in range(2):
                        ins = PE.matmul(v[:, t * 256:t * 256 + 256], XT[:, tile(4 * c + 2 * half + t)],
                                        WS[:, w0:w0 + 256], start=True, stop=True)
                    ins.then_inc(psum.filled(f"ret.vg{c}{half}"), 1)

            def scores(k):
                b = k // 4
                if b % 2 == 0 and k % 4 == 0:
                    pe.wait_ge(*psum.copied(f"ret.q{b // 2}"))
                pe.wait_ge(sig("ret.km"), k + 1)
                v = psum.take(pe, f"ret.s{k}", 2)
                for hh in range(2):
                    key = ret.KM[:, k % 4, hh]
                    PE.matmul(v[:, hh, 0:256], key[:, 0:128], ret.QT[:, b * S:b * S + S], start=True, stop=True)
                    ins = PE.matmul(v[:, hh, 256:384], key[:, 128:256], ret.QT[:, b * S + 128:b * S + S],
                                    start=True, stop=True)
                ins.then_inc(psum.filled(f"ret.s{k}"), 1)

            def values(m):
                b, half = divmod(m, 2)
                if half == 0:
                    psum.take(pe, f"ret.pv{b}")
                    pe.wait_ge(*psum.copied(f"ret.vg{b // 2}{b % 2}"))
                v = psum.view(f"ret.pv{b}")
                pe.wait_ge(*psum.copied(f"ret.s{2 * m + 1}"))
                for key_block in range(2):
                    for h in range(4):
                        at = 16 * (4 * half + h)
                        sd = ret.SD[:, (2 * m + h // 2) % 4, h % 2]
                        values = ret.VG[:, 2 * b + key_block, at:at + 32]
                        if key_block == 0:
                            PE.matmul(v[32 * h:32 * h + 32, half * S:half * S + S], values, sd[:, 0:256],
                                      start=True, stop=True)
                        else:
                            ins = PE.matmul(v[32 * h:32 * h + 32, half * S + 128:half * S + S], values, sd[:, 256:384],
                                            start=False, stop=True, skip_group_check=True)
                if half == 0:
                    ins.then_inc(sig("ret.half"), 1)
                else:
                    ins.then_inc(psum.filled(f"ret.pv{b}"), 1)

            def turn_values(b):
                pe.wait_ge(*psum.copied(f"ret.pv{b}"))
                v = psum.take(pe, f"ret.o{b}")
                for t in range(2):
                    for half in range(2):
                        ins = PE.transpose(v[:, tile(2 * t + half)], ret.PV[:, half, tile(t)], ident[:])
                ins.then_inc(psum.filled(f"ret.o{b}"), 1)

            for k in range(PAIRS + 4):
                if k < PAIRS:
                    scores(k)
                if k % 2 and 3 <= k <= PAIRS + 1:
                    values((k - 3) // 2)
                if k % 4 == 3 and k >= 7:
                    turn_values((k - 7) // 4)
                if k == PAIRS + 1:
                    pe.wait_ge(sig("ret.y"), 1)
                    turn_pe(pe, "ret.y", ret.Y, 0)
                if k == PAIRS + 2:
                    project_out_pe(pe, "ret.y", ret.YT, W("L0_attn_W_O"), 0)
            end_pe(pe, "ret", 0)

        def retention_last_out_pe(pe):
            pe.wait_ge(sig("ret.y"), 2)
            turn_pe(pe, "ret.y", ret.Y, 1)
            project_out_pe(pe, "ret.y", ret.YT, W("L0_attn_W_O"), 1)

        def retention_act(act):
            for c in range(NC):
                end_act(act, "in", c)
            for c in range(NC):
                move_act(act, f"ret.q{c}", ret.QT[:, chunk(c)])
                move_act(act, f"ret.k{c}", ret.KT[:, chunk(c)])
                for half in range(2):
                    t = 4 * c + 2 * half
                    move_act(act, f"ret.vg{c}{half}", ret.VG[:, t:t + 2].rearrange("p t d -> p (t d)"))
                act.eng.wait_ge(*act.own())
                A.activation(ret.SG[:, ctiles(c)], ret.VG[:, ctiles(c), D:2 * D], ACT.Exp, scale=-1.0)\
                    .then_inc(act.flag("ret.gexp"), 1)
            for b in range(NB):
                if b:
                    act.eng.wait_ge(*psum.made(f"ret.o{b - 1}"))
                move_act(act, f"ret.pv{b}", ret.PV.rearrange("p a q -> p (a q)"))
            move_act(act, "ret.yT0", ret.YT[:, chunk(0)])
            end_act(act, "ret", 0)
            move_act(act, "ret.yT1", ret.YT[:, chunk(1)])

        def retention_dve(dve):
            for k in range(PAIRS):
                if k in (9, 13):
                    retention_center_dve(dve, k // 4 - 2)
                if k in (0, 5):
                    c = k // 5
                    g = ret.SG[:, ctiles(c)]
                    dve.eng.wait_ge(sig("ret.gexp"), c + 1)
                    V.tensor_scalar(g, g, 1.0, None, ALU.add).then_inc(dve.step(), 1)
                    dve.eng.wait_ge(*dve.own())
                    V.reciprocal(g, g).then_inc(dve.flag("ret.gate"), 1)
                dve.eng.wait_ge(*psum.made(f"ret.s{k}"))
                v = psum.view(f"ret.s{k}")
                if k >= 4:
                    m = k // 2 - 2
                    dve.eng.wait_ge(*((sig("ret.half"), m // 2 + 1) if m % 2 == 0 else psum.made(f"ret.pv{m // 2}")))
                d = decay[:, 2 * (k % 4):2 * (k % 4) + 2, :]
                V.tensor_tensor(ret.SD[:, k % 4, :, 0:256], v[:, :, 0:256], d, ALU.mult).then_inc(dve.step(), 1)
                V.tensor_tensor(ret.SD[:, k % 4, :, 256:384], v[:, :, 256:384], d[:, :, 0:128],
                                ALU.mult).then_inc(dve.read(f"ret.s{k}"), 1)
            retention_center_dve(dve, 2)
            retention_gate_dve(dve, 0)
            retention_center_dve(dve, 3)
            end_sum_dve(dve, "ret", 0, "ret.y.out", X)
            retention_gate_dve(dve, 1)
            end_norm_dve(dve, "ret", 0)

        def retention_center_dve(dve, b):
            v = psum.view(f"ret.o{b}").rearrange("p (g w) -> p g w", w=32)[:, :, 0:16]
            y = ret.Y[:, 2 * b:2 * b + 2].rearrange("p t (h w) -> p (t h) w", w=16)
            m = ret.m[:, b // 2, 16 * (b % 2):16 * (b % 2) + 16]
            dve.eng.wait_ge(*dve.own())
            dve.eng.wait_ge(*psum.made(f"ret.o{b}"))
            V.tensor_reduce(m, v, AX.X, ALU.add).then_inc(dve.step(), 1)
            dve.eng.wait_ge(*dve.own())
            V.tensor_scalar(m, m, 1.0 / 16, None, ALU.mult).then_inc(dve.step(), 1)
            dve.eng.wait_ge(*dve.own())
            V.tensor_tensor(y, v, bc(m, 2, 16), ALU.subtract).then_inc(dve.read(f"ret.o{b}"), 1)

            dve.eng.wait_ge(*dve.own())
            V.tensor_tensor(ret.SQ, y, y, ALU.mult).then_inc(dve.step(), 1)
            dve.eng.wait_ge(*dve.own())
            v = ret.v[:, b // 2, 16 * (b % 2):16 * (b % 2) + 16]
            V.tensor_reduce(v, ret.SQ, AX.X, ALU.add).then_inc(dve.step(), 1)
            dve.eng.wait_ge(*dve.own())
            V.tensor_scalar(v, v, 1.0 / 16, 1e-6, ALU.mult, ALU.add).then_inc(dve.flag("ret.hvar"), 1)

        def retention_gate_dve(dve, c):
            y = ret.Y[:, ctiles(c)].rearrange("p t (h w) -> p (t h) w", w=16)
            dve.eng.wait_ge(sig("ret.hrstd"), 2 * c + 2)
            V.tensor_tensor(y, y, bc(ret.rs[:, c], 2, 16), ALU.mult).then_inc(dve.step(), 1)
            dve.eng.wait_ge(*dve.own())
            dve.eng.wait_ge(sig("ret.silu"), c + 1)
            V.tensor_tensor(ret.Y[:, ctiles(c)], ret.Y[:, ctiles(c)], ret.SG[:, ctiles(c)], ALU.mult)\
                .then_inc(dve.flag("ret.y"), 1)

        def retention_pool(pool):
            def head_rstd(b):
                pool.eng.wait_ge(sig("ret.hvar"), b + 1)
                part = slice(16 * (b % 2), 16 * (b % 2) + 16)
                G.tensor_tensor(ret.rs[:, b // 2, part], ret.v[:, b // 2, part], minus_half[:, 0:16],
                                ALU.pow).then_inc(pool.flag("ret.hrstd"), 1)

            def silu(c):
                pool.eng.wait_ge(sig("ret.gate"), c + 1)
                G.tensor_tensor(ret.SG[:, ctiles(c)], ret.VG[:, ctiles(c), D:2 * D], ret.SG[:, ctiles(c)],
                                ALU.mult).then_inc(pool.flag("ret.silu"), 1)

            for k in range(PAIRS):
                b, hp = divmod(k, 4)
                if k in (8, 12):
                    silu(k // 12)
                if k % 8 == 0:
                    pool.eng.wait_ge(*psum.copied(f"ret.k{k // 8}"))
                if k >= 4:
                    pool.eng.wait_ge(*psum.made(f"ret.s{k - 4}"))
                G.tensor_tensor(ret.KM[:, k % 4], bc(ret.KT[:, b * S:b * S + S], 1, 2),
                                bc(head_of16[:, 2 * hp:2 * hp + 2], 2, S), ALU.mult).then_inc(pool.flag("ret.km"), 1)
            for b in range(NB):
                head_rstd(b)
            norm_rstd(pool, 0, "ret")

        class Cross:
            def __init__(self, L, prefix, before, top, group, keep, fill, ends_in_next=False, last=False):
                self.L, self.p, self.before, self.group = L, prefix, before, group
                self.keep, self.fill = keep, fill
                self.ends_in_next, self.last = ends_in_next, last
                a = Carve(top)
                self.QT = a(T)
                self.KT = a(NB, SK)
                self.KM = a(2, 16, SK)
                self.VB = a(2, 8, 32)
                self.SS = a(3, 16, SK)
                self.ET = a(2, 8, 2, P)
                self.PV = a(2, S)
                self.O = R
                self.OT = self.QT
                self.mx = a(2, 16)
                self.rc = a(2, 2, 16)
                self.keepf = a(NB, SK)
                self.fillr = a(NB, SK, dt=BF16)

            def w(self, n):
                return W(f"{self.p}_{n}")

            def pe(self, pe, out_before=None):
                self.start_pe(pe)
                self.queries_pe(pe, 0)
                self.rounds_pe(pe, 0, NT, out_before)

            def start_pe(self, pe):
                L = self.L
                pe.wait_ge(loaded, LOADS * 16)
                pe.wait_ge(w_loaded[self.group], 16)
                v = psum.take(pe, f"{L}.k")
                PE.matmul(v[:, 0:NB * SK], self.w("Wk"), CT[:].rearrange("p b k -> p (b k)"),
                          start=True, stop=True).then_inc(psum.filled(f"{L}.k"), 1)
                self.values_pe(pe, 0)

            def queries_pe(self, pe, c):
                x_t_ready(pe, self.before, c)
                v = psum.take(pe, f"{self.L}.q{c}")
                PE.matmul(v, self.w("Wq"), XT[:, chunk(c)], start=True, stop=True)\
                    .then_inc(psum.filled(f"{self.L}.q{c}"), 1)

            def chunk_pe(self, pe, c):
                self.queries_pe(pe, c)
                self.rounds_pe(pe, 4 * c, 4 * c + 4)

            def rounds_pe(self, pe, first, last, out_before=None):
                L = self.L
                self.scores_pe(pe, first)
                self.scores_pe(pe, first + 1)
                if out_before:
                    out_before(pe)
                for t in range(first, last + 2):
                    if t == 0:
                        self.values_pe(pe, 1)
                    if t + 2 < last:
                        self.scores_pe(pe, t + 2)
                    if t < last:
                        self.turn_pe(pe, t)
                    if t % 2 == 0 and t > first:
                        self.probs_pe(pe, t // 2 - 1)
                    if t % 2 == 1 and t > first + 1:
                        self.turn_probs_pe(pe, (t - 3) // 2)
                    if t % 2 == 1 and 3 <= t < 2 * NB - 1 and first == 0:
                        self.values_pe(pe, (t + 1) // 2)
                    if t == 1 and last == NT:
                        end_pe(pe, self.before, 1)
                        self.queries_pe(pe, 1)
                    if t == NT - 1:
                        self.turn_out_pe(pe, 0)
                    if t == NT:
                        project_out_pe(pe, f"{L}.o", self.OT, self.w("Wo"), 0)
                if last == NT:
                    self.turn_out_pe(pe, 1)
                    if not self.last:
                        end_pe(pe, L, 0)
                    project_out_pe(pe, f"{L}.o", self.OT, self.w("Wo"), 1)
                    if not self.ends_in_next and not self.last:
                        end_pe(pe, L, 1)

            def values_pe(self, pe, b):
                v = psum.take(pe, f"{self.L}.v{b}")
                PE.matmul(v[:, 0:D], CD[:, b, :], self.w("Wv"), start=True, stop=True)\
                    .then_inc(psum.filled(f"{self.L}.v{b}"), 1)

            def scores_pe(self, pe, t):
                L, b = self.L, t // 2
                if t % 4 == 0:
                    pe.wait_ge(*psum.copied(f"{L}.q{t // 4}"))
                if t % 2 == 0:
                    pe.wait_ge(sig(L + ".km"), b + 1)
                    if self.keep is not None and t == 0:
                        pe.wait_ge(sig(L + ".fill"), 1)
                v = psum.take(pe, f"{L}.s{t}", 2)
                for half in range(2):
                    km = self.KM[:, b % 2, 8 * half:8 * half + 8, :].rearrange("p h k -> p (h k)")
                    ins = PE.matmul(v[:, half], self.QT[:, tile(t)], km, start=True, stop=self.keep is None)
                    if self.keep is not None:
                        ins = PE.matmul(v[:, half].rearrange("p (h k) -> p h k", h=8), ones16[0:3, :],
                                        bc(self.fillr[0:3, b, :], 1, 8), start=False, stop=True)
                ins.then_inc(psum.filled(f"{L}.s{t}"), 1)

            def turn_pe(self, pe, t):
                L = self.L
                pe.wait_ge(sig(L + ".exp"), t + 1)
                v = psum.take(pe, f"{L}.eT{t}", 2)
                e = self.SS[:, t % 3].rearrange("p (a h) k -> p a (h k)", a=8)
                for pair in range(8):
                    ins = PE.transpose(v[:, pair // 4, tile(pair % 4)], e[:, pair, :], ident[:])
                ins.then_inc(psum.filled(f"{L}.eT{t}"), 1)

            def probs_pe(self, pe, b):
                L = self.L
                pe.wait_ge(*psum.copied(f"{L}.v{b}"))
                pe.wait_ge(*psum.copied(f"{L}.eT{2 * b}"))
                pe.wait_ge(*psum.copied(f"{L}.eT{2 * b + 1}"))
                v = psum.take(pe, f"{L}.pv{b}")
                for half in range(2):
                    for j in range(4):
                        pair = 4 * half + j
                        ins = PE.matmul(v[32 * j:32 * j + 32, half * S:half * S + S], self.VB[:, b % 2, pair, :],
                                        self.ET[:, b % 2, pair].rearrange("p t q -> p (t q)"), start=True, stop=True)
                ins.then_inc(psum.filled(f"{L}.pv{b}"), 1)

            def turn_probs_pe(self, pe, b):
                L = self.L
                pe.wait_ge(*psum.copied(f"{L}.pv{b}"))
                v = psum.take(pe, f"{L}.pn{b}")
                for t in range(2):
                    for half in range(2):
                        ins = PE.transpose(v[:, tile(2 * t + half)], self.PV[:, half, tile(t)], ident[:])
                ins.then_inc(psum.filled(f"{L}.pn{b}"), 1)

            def turn_out_pe(self, pe, c):
                pe.wait_ge(*psum.copied(f"{self.L}.pn{2 * c + 1}"))
                turn_pe(pe, f"{self.L}.o", self.O, c)

            def act(self, act):
                self.rounds_act(act, 0, NT)

            def chunk_act(self, act, c):
                self.rounds_act(act, 4 * c, 4 * c + 4)

            def rounds_act(self, act, first, last):
                L = self.L
                self.exp_act(act, first)
                for t in range(first, last):
                    if t + 1 < last:
                        self.exp_act(act, t + 1)
                    act.eng.wait_ge(*psum.made(f"{L}.eT{t}"))
                    v = psum.view(f"{L}.eT{t}").rearrange("p a (j q) -> p (a j) q", j=4)
                    if t >= 4:
                        act.eng.wait_ge(*psum.made(f"{L}.pv{t // 2 - 2}"))
                    A.copy(self.ET[:, (t // 2) % 2, :, t % 2], v).then_inc(act.read(f"{L}.eT{t}"), 1)
                    if t == 1 and last == NT:
                        end_act(act, self.before, 1)
                    if t % 2 == 0 and t > first:
                        self.copy_act(act, t // 2 - 1)
                if last == NT:
                    move_act(act, f"{L}.oT0", self.OT[:, chunk(0)])
                self.copy_act(act, last // 2 - 1)
                if last == NT:
                    move_act(act, f"{L}.oT1", self.OT[:, chunk(1)])
                    if not self.last:
                        end_act(act, L, 0)
                    if not self.ends_in_next and not self.last:
                        end_act(act, L, 1)

            def copy_act(self, act, b):
                if b >= 1:
                    act.eng.wait_ge(*psum.made(f"{self.L}.pn{b - 1}"))
                move_act(act, f"{self.L}.pv{b}", self.PV.rearrange("p a q -> p (a q)"))

            def exp_act(self, act, t):
                act.eng.wait_ge(*psum.copied(f"{self.L}.s{t}"))
                e = self.SS[:, t % 3]
                A.activation(e, e, ACT.Exp).then_inc(act.flag(self.L + ".exp"), 1)

            def dve(self, dve, sum_before, norm_before):
                L = self.L
                self.start_dve(dve)
                self.queries_dve(dve, 0)
                for t in range(NT):
                    if t >= 5 and t % 2 == 1:
                        self.out_dve(dve, (t - 5) // 2)
                    self.shift_dve(dve, t)
                    if t == 0:
                        sum_before()
                    if t == 1:
                        norm_before()
                        self.values_dve(dve, 1)
                    if t == 2:
                        self.queries_dve(dve, 1)
                    if t >= 4 and t % 2 == 0:
                        self.values_dve(dve, t // 2)
                self.end_dve(dve)

            def chunk_dve(self, dve, c, between=lambda t: None):
                self.queries_dve(dve, c)
                for t in range(4 * c, 4 * c + 4):
                    self.shift_dve(dve, t)
                    if t == 1:
                        self.values_dve(dve, 1)
                    between(t)
                if c == 0:
                    self.out_dve(dve, 0)
                    self.values_dve(dve, 2)
                    between(4)
                    self.out_dve(dve, 1)
                    self.values_dve(dve, 3)
                else:
                    self.end_dve(dve)

            def end_dve(self, dve):
                L = self.L
                self.out_dve(dve, NB - 2)
                end_sum_dve(dve, L, 0, f"{L}.o.out", XB)
                self.out_dve(dve, NB - 1)
                end_norm_dve(dve, L, 0)
                if not self.ends_in_next:
                    if self.last:
                        absmax_dve(dve, 0)
                    end_sum_dve(dve, L, 1, f"{L}.o.out", XB)
                    end_norm_dve(dve, L, 1)
                    if self.last:
                        absmax_dve(dve, 1)

            def start_dve(self, dve):
                L = self.L
                dve.eng.wait_ge(*dve.own())
                if self.keep is not None:
                    dve.eng.wait_ge(loaded, LOADS * 16)
                    V.tensor_scalar(self.keepf, self.keep[:], 0.0, None, ALU.not_equal).then_inc(dve.step(), 1)
                    dve.eng.wait_ge(*dve.own())
                    V.tensor_scalar(self.fillr[0:3], self.keepf[0:3], 1.0, fills[:, self.fill:self.fill + 1],
                                    ALU.subtract, ALU.mult).then_inc(dve.flag(L + ".fill"), 1)
                dve.eng.wait_ge(*psum.made(f"{L}.k"))
                v = psum.view(f"{L}.k")
                kt = self.KT.rearrange("p b k -> p (b k)")
                if self.keep is not None:
                    V.scalar_tensor_tensor(kt, v[:, 0:NB * SK], bcol(self.p + "_bk"),
                                           self.keepf.rearrange("p b k -> p (b k)"), ALU.add, ALU.mult)\
                        .then_inc(dve.read(f"{L}.k"), 1)
                else:
                    V.tensor_scalar(kt, v[:, 0:NB * SK], bcol(self.p + "_bk"), None, ALU.add)\
                        .then_inc(dve.read(f"{L}.k"), 1)
                for j in range(2):
                    V.memset(self.VB[:, j], 0.0).then_inc(dve.step(), 1)
                dve.eng.wait_ge(*dve.own())
                for j in range(2):
                    V.memset(self.VB[0:64, j, :, 16], 1.0).then_inc(dve.step(), 1)
                    V.memset(self.VB[64:128, j, :, 17], 1.0).then_inc(dve.step(), 1)
                self.values_dve(dve, 0)

            def queries_dve(self, dve, c):
                L = self.L
                dve.eng.wait_ge(*psum.made(f"{L}.q{c}"))
                V.tensor_scalar(self.QT[:, chunk(c)], psum.view(f"{L}.q{c}"), bcol(self.p + "_bq"), 8 ** -0.5,
                                ALU.add, ALU.mult).then_inc(dve.read(f"{L}.q{c}"), 1)

            def shift_dve(self, dve, t):
                L = self.L
                dve.eng.wait_ge(*psum.made(f"{L}.s{t}"))
                v = psum.view(f"{L}.s{t}").rearrange("p a (h k) -> p (a h) k", h=8)
                V.tensor_reduce(self.mx[:, t % 2], v, AX.X, ALU.max).then_inc(dve.step(), 1)
                dve.eng.wait_ge(*dve.own())
                if t >= 3:
                    dve.eng.wait_ge(*psum.made(f"{L}.eT{t - 3}"))
                V.tensor_tensor(self.SS[:, t % 3], v, bc(self.mx[:, t % 2], 2, SK), ALU.subtract)\
                    .then_inc(dve.read(f"{L}.s{t}"), 1)

            def values_dve(self, dve, b):
                L = self.L
                dve.eng.wait_ge(*psum.made(f"{L}.v{b}"))
                if b >= 2:
                    dve.eng.wait_ge(*psum.made(f"{L}.pv{b - 2}"))
                v = psum.view(f"{L}.v{b}")[:, 0:D].rearrange("p (a j w) -> p a j w", j=2, w=8)
                bias = row(self.p + "_bv").rearrange("p (a j w) -> p a j w", j=2, w=8)
                dve.eng.wait_ge(*dve.own())
                V.tensor_tensor(self.VB[0:64, b % 2, :, 0:8], v[0:64, :, 0], bias[0:64, :, 0], ALU.add)\
                    .then_inc(dve.step(), 1)
                V.tensor_tensor(self.VB[64:128, b % 2, :, 8:16], v[64:128, :, 1], bias[64:128, :, 1],
                                ALU.add).then_inc(dve.read(f"{L}.v{b}"), 1)

            def out_dve(self, dve, b):
                L = self.L
                dve.eng.wait_ge(*psum.made(f"{L}.pn{b}"))
                v = psum.view(f"{L}.pn{b}").rearrange("p (a x) -> p a x", x=32)
                rc = self.rc[:, b % 2].rearrange("p a (b j) -> p (a b) j", j=2)
                dve.eng.wait_ge(*dve.own())
                V.reciprocal(rc, v[:, :, 16:18]).then_inc(dve.step(), 1)
                dve.eng.wait_ge(*dve.own())
                o = self.O[:, 2 * b:2 * b + 2].rearrange("p t (a j w) -> p (t a) j w", j=2, w=8)
                V.tensor_tensor(o, v[:, :, 0:16].rearrange("p a (j w) -> p a j w", j=2), bc(rc, 3, 8),
                                ALU.mult).then_inc(dve.read(f"{L}.pn{b}"), 1)

            def pool(self, pool, norms_before):
                for b in range(NB):
                    if b == 2:
                        for name in norms_before:
                            norm_rstd(pool, 1, name)
                        add_bias_pool(pool, self.L, self.before, self.p + "_bo")
                    self.spread_pool(pool, b)
                norm_rstd(pool, 0, self.L)
                if self.last:
                    norm_rstd(pool, 0, "fin")
                if not self.ends_in_next:
                    norm_rstd(pool, 1, self.L)
                if self.last:
                    norm_rstd(pool, 1, "fin")

            def spread_pool(self, pool, b):
                L = self.L
                if b == 0:
                    pool.eng.wait_ge(*psum.copied(f"{L}.k"))
                if b >= 2:
                    pool.eng.wait_ge(*psum.made(f"{L}.s{2 * b - 3}"))
                G.tensor_tensor(self.KM[:, b % 2], bc(self.KT[:, b, :], 1, 16), bc(head_of8[:], 2, SK),
                                ALU.mult).then_inc(pool.flag(L + ".km"), 1)


        MAIN_ROUNDS = 11

        def nothing(i):
            pass

        class Moe:
            def __init__(self, L, prefix, before, top, group1, group2, J, b2, top2, skip=0):
                self.L, self.p, self.before, self.g1, self.g2, self.J, self.b2, self.top2 = \
                    L, prefix, before, group1, group2, J, b2, top2
                a = Carve(top)
                a(max(skip, 1))
                self.HT = a(2, J, CH)
                self.LG, self.EL, self.GW = a(NT, 8), a(NT, 8), a(NT, 8)
                self.M8, self.I8, self.IF = a(NT, 8), a(NT, 8, dt=U32), a(NT, 8)
                self.H2 = a(NT, 8)
                self.dn = a(NT)
                self.GT = a(T, parts=8)
                self.WORDS = a.at
                self.W1 = W(prefix + "_W1").rearrange("p (e j h) -> p e j h", e=8, j=J)
                self.W2 = W(prefix + "_W2").rearrange("p (e j d) -> p e j d", e=8, j=J)

            def pe(self, pe):
                L = self.L
                self.logits_pe(pe, 0)
                pe.wait_ge(w_loaded[self.g1], 16)
                self.hidden_pe(pe, 0)
                end_pe(pe, self.before, 1)
                self.gates_pe(pe, 0)
                pe.wait_ge(w_loaded[self.g2], 16)
                for i in range(MAIN_ROUNDS):
                    if i + 1 < 8 * NC:
                        self.hidden_pe(pe, i + 1)
                    self.sum_pe(pe, i)
                    if i == 0:
                        self.logits_pe(pe, 1)
                    if i == 4:
                        self.gates_pe(pe, 1)
                    if i == 9:
                        end_pe(pe, L, 0)

            def late_round_pe(self, pe, i):
                if i + 1 < 8 * NC:
                    self.hidden_pe(pe, i + 1)
                self.sum_pe(pe, i)

            def sum_pe(self, pe, i):
                L = self.L
                c, e = divmod(i, 8)
                if e == 0:
                    pe.wait_ge(*psum.copied(f"{L}.gT{c}"))
                    v = psum.take(pe, f"{L}.b2{c}")
                    for t in range(4):
                        ins = PE.matmul(v[:, tile(t)], self.GT[:, tile(4 * c + t)], B2[:, self.b2, :],
                                        start=True, stop=True)
                    ins.then_inc(psum.filled(f"{L}.b2{c}"), 1)
                for j in range(self.J):
                    pe.wait_ge(*psum.copied(f"{L}.h{i}.{j}"))
                v = psum.take(pe, f"{L}.y{i}")
                for t in range(4):
                    for j in range(self.J):
                        ins = PE.matmul(v[:, tile(t)], self.HT[:, i % 2, j, tile(t)], self.W2[:, e, j],
                                        start=j == 0, stop=j == self.J - 1)
                ins.then_inc(psum.filled(f"{L}.y{i}"), 1)

            def start_chunk_pe(self, pe, c):
                self.logits_pe(pe, c)
                pe.wait_ge(w_loaded[self.g1], 16)
                self.hidden_pe(pe, 8 * c)
                self.gates_pe(pe, c)
                pe.wait_ge(w_loaded[self.g2], 16)

            def round_pe(self, pe, i):
                if i % 8 < 7:
                    self.hidden_pe(pe, i + 1)
                self.sum_pe(pe, i)

            def logits_pe(self, pe, c):
                x_t_ready(pe, self.before, c)
                v = psum.take(pe, f"{self.L}.lg{c}")
                for t in range(4):
                    ins = PE.matmul(v[:, 8 * t:8 * t + 8], XT[:, tile(4 * c + t)], W(self.p + "_Wr"),
                                    start=True, stop=True)
                ins.then_inc(psum.filled(f"{self.L}.lg{c}"), 1)

            def gates_pe(self, pe, c):
                pe.wait_ge(sig(self.L + ".gates"), c + 1)
                v = psum.take(pe, f"{self.L}.gT{c}")
                for t in range(4):
                    ins = PE.transpose(v[0:8, tile(t)], self.GW[:, 4 * c + t, :], ident[:])
                ins.then_inc(psum.filled(f"{self.L}.gT{c}"), 1)

            def hidden_pe(self, pe, i):
                c, e = divmod(i, 8)
                for j in range(self.J):
                    v = psum.take(pe, f"{self.L}.h{i}.{j}")
                    PE.matmul(v, self.W1[:, e, j], XT[:, chunk(c)], start=True, stop=True)\
                        .then_inc(psum.filled(f"{self.L}.h{i}.{j}"), 1)

            def hidden_free(self, eng, i):
                if i >= 2:
                    eng.wait_ge(*psum.made(f"{self.L}.y{i - 2}"))

            def act_share(self, j):
                return j % 4 != 3

            def act(self, act):
                L = self.L
                self.exp_act(act, 0)
                self.hidden_act(act, 0)
                end_act(act, self.before, 1)
                self.gates_act(act, 0)
                for i in range(MAIN_ROUNDS):
                    if i + 1 < 8 * NC:
                        self.hidden_act(act, i + 1)
                    if i == 2:
                        self.exp_act(act, 1)
                    if i == 5:
                        self.gates_act(act, 1)
                end_act(act, L, 0)

            def late_round_act(self, act, i):
                if i + 1 < 8 * NC:
                    self.hidden_act(act, i + 1)

            def start_chunk_act(self, act, c):
                self.exp_act(act, c)
                self.hidden_act(act, 8 * c)
                self.gates_act(act, c)

            def round_act(self, act, i):
                if i % 8 < 7:
                    self.hidden_act(act, i + 1)

            def exp_act(self, act, c):
                act.eng.wait_ge(sig(self.L + ".shifted"), c + 1)
                A.activation(self.EL[:, ctiles(c)], self.EL[:, ctiles(c)], ACT.Exp).then_inc(act.flag(self.L + ".exp"), 1)

            def gates_act(self, act, c):
                act.eng.wait_ge(*psum.made(f"{self.L}.gT{c}"))
                v = psum.view(f"{self.L}.gT{c}")
                A.copy(self.GT[:, chunk(c)], v[0:8]).then_inc(act.read(f"{self.L}.gT{c}"), 1)

            def hidden_act(self, act, i):
                for j in range(self.J):
                    if self.act_share(j):
                        act.eng.wait_ge(*psum.made(f"{self.L}.h{i}.{j}"))
                        v = psum.view(f"{self.L}.h{i}.{j}")
                        self.hidden_free(act.eng, i)
                        A.activation(self.HT[:, i % 2, j], v, ACT.Relu,
                                     bias=bcol(self.p + "_b1", (i % 8) * self.J + j))\
                            .then_inc(act.read(f"{self.L}.h{i}.{j}"), 1)

            def hidden_dve(self, dve, i):
                for j in range(self.J):
                    if not self.act_share(j):
                        dve.eng.wait_ge(*psum.made(f"{self.L}.h{i}.{j}"))
                        v = psum.view(f"{self.L}.h{i}.{j}")
                        self.hidden_free(dve.eng, i)
                        V.tensor_scalar(self.HT[:, i % 2, j], v, bcol(self.p + "_b1", (i % 8) * self.J + j), 0.0,
                                        ALU.add, ALU.max).then_inc(dve.read(f"{self.L}.h{i}.{j}"), 1)

            def dve(self, dve, sum_before, norm_before):
                L = self.L
                self.logits_dve(dve, 0)
                sum_before()
                norm_before()
                self.hidden_dve(dve, 0)
                self.gates_dve(dve, 0)
                for i in range(MAIN_ROUNDS):
                    if i + 1 < 8 * NC:
                        self.hidden_dve(dve, i + 1)
                    self.sum_dve(dve, i)
                    if i == 1:
                        self.logits_dve(dve, 1)
                    if i == 3:
                        self.gates_dve(dve, 1)
                    if i == 7:
                        end_sum_dve(dve, L, 0)
                    if i == 8:
                        end_norm_dve(dve, L, 0)

            def late_round_dve(self, dve, i):
                if i + 1 < 8 * NC:
                    self.hidden_dve(dve, i + 1)
                self.sum_dve(dve, i)

            def start_chunk_dve(self, dve, c):
                self.logits_dve(dve, c)
                self.hidden_dve(dve, 8 * c)
                self.gates_dve(dve, c)

            def round_dve(self, dve, i):
                if i % 8 < 7:
                    self.hidden_dve(dve, i + 1)
                self.sum_dve(dve, i)

            def sum_dve(self, dve, i):
                L = self.L
                c, e = divmod(i, 8)
                r = R[:, ctiles(c)]
                if e == 0:
                    dve.eng.wait_ge(*psum.made(f"{L}.b2{c}"))
                    v = psum.view(f"{L}.b2{c}")
                    V.tensor_tensor(r, v.rearrange("p (t d) -> p t d", t=4), X[:, ctiles(c)],
                                    ALU.add).then_inc(dve.read(f"{L}.b2{c}"), 1)
                dve.eng.wait_ge(*psum.made(f"{L}.y{i}"))
                v = psum.view(f"{L}.y{i}")
                dve.eng.wait_ge(*dve.own())
                for t in range(4):
                    ins = V.scalar_tensor_tensor(r[:, t], v[:, tile(t)], self.GW[:, 4 * c + t, e:e + 1],
                                                 r[:, t], ALU.mult, ALU.add)
                    if t < 3:
                        ins.then_inc(dve.step(), 1)
                ins.then_inc(dve.read(f"{L}.y{i}"), 1)

            def logits_dve(self, dve, c):
                L = self.L
                dve.eng.wait_ge(*psum.made(f"{L}.lg{c}"))
                v = psum.view(f"{L}.lg{c}")
                lg = self.LG[:, ctiles(c)]
                V.tensor_tensor(lg, v[:, 0:32].rearrange("p (t e) -> p t e", t=4),
                                bc(row(self.p + "_br"), 1, 4), ALU.add).then_inc(dve.read(f"{L}.lg{c}"), 1)
                dve.eng.wait_ge(*dve.own())
                for t in range(4 * c, 4 * c + 4):
                    V.max(self.M8[:, t], self.LG[:, t]).then_inc(dve.step(), 1)
                dve.eng.wait_ge(*dve.own())
                V.tensor_tensor(self.EL[:, ctiles(c)], lg, bc(self.M8[:, ctiles(c), 0], 2, 8),
                                ALU.subtract).then_inc(dve.flag(L + ".shifted"), 1)
                for t in range(4 * c, 4 * c + 4):
                    V.max_index(self.I8[:, t], self.M8[:, t], self.LG[:, t]).then_inc(dve.step(), 1)
                dve.eng.wait_ge(*dve.own())
                V.tensor_copy(self.IF[:, ctiles(c)], self.I8[:, ctiles(c)]).then_inc(dve.step(), 1)

            def gates_dve(self, dve, c):
                L = self.L
                g, h2, dn = self.GW[:, ctiles(c)], self.H2[:, ctiles(c)], self.dn[:, ctiles(c)]
                ex = bc(expert[:], 1, 4)
                dve.eng.wait_ge(*dve.own())
                V.tensor_tensor(g, ex, bc(self.IF[:, ctiles(c), 0], 2, 8), ALU.is_equal).then_inc(dve.step(), 1)
                dve.eng.wait_ge(sig(L + ".exp"), c + 1)
                if self.top2:
                    V.tensor_tensor(h2, ex, bc(self.IF[:, ctiles(c), 1], 2, 8), ALU.is_equal).then_inc(dve.step(), 1)
                    dve.eng.wait_ge(*dve.own())
                    V.tensor_tensor(g, g, h2, ALU.add).then_inc(dve.step(), 1)
                    dve.eng.wait_ge(*dve.own())
                    V.tensor_tensor(g, g, self.EL[:, ctiles(c)], ALU.mult).then_inc(dve.step(), 1)
                    dve.eng.wait_ge(*dve.own())
                    V.tensor_reduce(dn, g, AX.X, ALU.add).then_inc(dve.step(), 1)
                else:
                    V.tensor_reduce(dn, self.EL[:, ctiles(c)], AX.X, ALU.add).then_inc(dve.step(), 1)
                dve.eng.wait_ge(*dve.own())
                V.reciprocal(dn, dn).then_inc(dve.step(), 1)
                dve.eng.wait_ge(*dve.own())
                V.tensor_tensor(g, g, bc(dn, 2, 8), ALU.mult).then_inc(dve.flag(L + ".gates"), 1)

            def pool(self, pool):
                norm_rstd(pool, 1, self.before)
                norm_rstd(pool, 0, self.L)

        SPARSE_WORDS = 3 * T + NT * S + 2 * 4 * S + 6 * NT

        moe0 = Moe("moe0", "L0_ffn", "x0", False, 1, 2, 4, 0, True)

        class cos:
            a = Carve(True)
            QKV = a(4, 3 * D)
            QT, KT = a(CH), a(CH)
            PR = a(4, S)
            PT = a(2, 2, S)
            OT, H1 = a(CH), a(CH)
            H2 = a(4, CH)
            sq = a(D)
            ssq, rn = a(4, 2), a(4, 2)
            mx, nb, sm = a(4), a(4), a(4)
            WORDS = ARENA - a.at

        def cosine_pe(pe, c, between=nothing):
            pe.wait_ge(w_loaded[3], 16)
            w0 = W_AT["L1_attn_Wq"][0]
            x_t_ready(pe, "moe0", c)
            for t in range(4 * c, 4 * c + 4):
                v = psum.take(pe, f"cos.qkv{t}")
                PE.matmul(v[:, 0:384], XT[:, tile(t)], WS[:, w0:w0 + 384], start=True, stop=True)\
                    .then_inc(psum.filled(f"cos.qkv{t}"), 1)
            between(0)
            for name, cols in (("q", slice(0, D)), ("k", slice(D, 2 * D))):
                if name == "q":
                    pe.wait_ge(*psum.copied(f"cos.qkv{4 * c + 3}"))
                else:
                    pe.wait_ge(sig("cos.khat"), c + 1)
                v = psum.take(pe, f"cos.{name}T{c}")
                for t in range(4):
                    ins = PE.transpose(v[:, tile(t)], cos.QKV[:, t, cols], ident[:])
                ins.then_inc(psum.filled(f"cos.{name}T{c}"), 1)
            between(1)
            pe.wait_ge(*psum.copied(f"cos.qT{c}"))
            pe.wait_ge(*psum.copied(f"cos.kT{c}"))
            for b in range(2):
                v = psum.take(pe, f"cos.s{2 * c + b}")
                for t in range(2):
                    ins = PE.matmul(v[:, t * S:t * S + S], cos.QT[:, tile(2 * b + t)], cos.KT[:, b * S:b * S + S],
                                    start=True, stop=True)
                ins.then_inc(psum.filled(f"cos.s{2 * c + b}"), 1)
            between(2)
            for b in range(2):
                turn_probs_pe(pe, "cos", cos.PR, b, 2 * c + b, "cos.probs", 2 * c + b + 1)
            v = psum.take(pe, f"cos.oT{c}")
            for b in range(2):
                pe.wait_ge(*psum.copied(f"cos.pT{2 * c + b}"))
                for kt in range(2):
                    ins = PE.matmul(v[:, b * S:b * S + S], cos.QKV[:, 2 * b + kt, 2 * D:3 * D],
                                    cos.PT[:, b, kt, :], start=kt == 0, stop=kt == 1)
            ins.then_inc(psum.filled(f"cos.oT{c}"), 1)
            between(3)
            pe.wait_ge(*psum.copied(f"cos.oT{c}"))
            v = psum.take(pe, f"cos.h1{c}")
            PE.matmul(v, W("L1_attn_W1"), cos.OT, start=True, stop=True).then_inc(psum.filled(f"cos.h1{c}"), 1)
            between(4)
            pe.wait_ge(*psum.copied(f"cos.h1{c}"))
            for j in range(4):
                v = psum.take(pe, f"cos.h2{c}.{j}")
                PE.matmul(v, W("L1_attn_W2")[:, tile(j)], cos.H1, start=True, stop=True)\
                    .then_inc(psum.filled(f"cos.h2{c}.{j}"), 1)
            for j in range(4):
                pe.wait_ge(*psum.copied(f"cos.h2{c}.{j}"))
            v = psum.take(pe, f"cos.out{c}")
            for t in range(4):
                for j in range(4):
                    ins = PE.matmul(v[:, tile(t)], cos.H2[:, j, tile(t)], W("L1_attn_W3")[:, tile(j)],
                                    start=j == 0, stop=j == 3)
            ins.then_inc(psum.filled(f"cos.out{c}"), 1)
            between(5)
            end_pe(pe, "cos", c)

        def turn_probs_pe(pe, name, src, local, b, ready, count):
            pe.wait_ge(sig(ready), count)
            v = psum.take(pe, f"{name}.pT{b}")
            for kt in range(2):
                for t in range(2):
                    ins = PE.transpose(v[:, kt * S + t * P:kt * S + t * P + P], src[:, 2 * local + t, tile(kt)], ident[:])
            ins.then_inc(psum.filled(f"{name}.pT{b}"), 1)

        def cosine_act(act, c, between=nothing):
            for t in range(4):
                act.eng.wait_ge(*psum.copied(f"cos.qkv{4 * c + t}"))
                for j in range(2):
                    act.eng.wait_ge(*act.own())
                    ins = A.activation(cos.sq, cos.QKV[:, t, j * D:j * D + D], ACT.Square,
                                       accum_out=cos.ssq[:, t, j:j + 1])
                    if t == 3 and j == 1:
                        ins.then_inc(act.flag("cos.ssq"), 1)
                    else:
                        ins.then_inc(act.step(), 1)
            between(0)
            move_act(act, f"cos.qT{c}", cos.QT)
            move_act(act, f"cos.kT{c}", cos.KT)
            between(1)
            for b in range(2):
                act.eng.wait_ge(*psum.made(f"cos.s{2 * c + b}"))
                v = psum.view(f"cos.s{2 * c + b}")
                act.eng.wait_ge(sig("cos.nb"), 2 * c + b + 1)
                for t in range(2):
                    i = 2 * b + t
                    ins = A.activation(cos.PR[:, i], v[:, t * S:t * S + S], ACT.Exp, bias=cos.nb[:, i:i + 1],
                                       scale=cos.rn[:, i, 0:1], accum_out=cos.sm[:, i:i + 1])
                    if t == 0:
                        ins.then_inc(act.step(), 1)
                ins.then_inc(act.read(f"cos.s{2 * c + b}"), 1)
            between(2)
            for b in range(2):
                move_act(act, f"cos.pT{2 * c + b}", cos.PT[:, b].rearrange("p a q -> p (a q)"))
            move_act(act, f"cos.oT{c}", cos.OT)
            between(3)
            act.eng.wait_ge(*psum.made(f"cos.h1{c}"))
            A.activation(cos.H1, psum.view(f"cos.h1{c}"), ACT.Relu, bias=bcol("L1_attn_b1"))\
                .then_inc(act.read(f"cos.h1{c}"), 1)
            between(4)
            for j in range(0, 4, 2):
                act.eng.wait_ge(*psum.made(f"cos.h2{c}.{j}"))
                A.activation(cos.H2[:, j], psum.view(f"cos.h2{c}.{j}"), ACT.Relu, bias=bcol("L1_attn_b2", j))\
                    .then_inc(act.read(f"cos.h2{c}.{j}"), 1)
            between(5)
            end_act(act, "cos", c)

        def cosine_dve(dve, c, between=nothing):
            bias = RW[:, R_AT["L1_attn_bq"][0]:R_AT["L1_attn_bq"][0] + 384]
            dve.eng.wait_ge(*dve.own())
            for t in range(4):
                dve.eng.wait_ge(*psum.made(f"cos.qkv{4 * c + t}"))
                V.tensor_tensor(cos.QKV[:, t], psum.view(f"cos.qkv{4 * c + t}")[:, 0:384], bias, ALU.add)\
                    .then_inc(dve.read(f"cos.qkv{4 * c + t}"), 1)
            between(0)
            dve.eng.wait_ge(sig("cos.pow"), c + 1)
            V.tensor_scalar(cos.rn, cos.rn, 1e12, None, ALU.min).then_inc(dve.step(), 1)
            dve.eng.wait_ge(*dve.own())
            for t in range(4):
                k = cos.QKV[:, t, D:2 * D]
                ins = V.tensor_scalar(k, k, cos.rn[:, t, 1:2], None, ALU.mult)
                if t < 3:
                    ins.then_inc(dve.step(), 1)
            ins.then_inc(dve.flag("cos.khat"), 1)
            between(1)
            for b in range(2):
                dve.eng.wait_ge(*psum.made(f"cos.s{2 * c + b}"))
                v = psum.view(f"cos.s{2 * c + b}").rearrange("p (t k) -> p t k", t=2)
                mx = cos.mx[:, 2 * b:2 * b + 2]
                V.tensor_reduce(mx, v, AX.X, ALU.max, negate=True).then_inc(dve.step(), 1)
                dve.eng.wait_ge(*dve.own())
                V.tensor_tensor(cos.nb[:, 2 * b:2 * b + 2], mx, cos.rn[:, 2 * b:2 * b + 2, 0], ALU.mult)\
                    .then_inc(dve.flag("cos.nb"), 1)
            between(2)
            for b in range(2):
                dve.eng.wait_ge(*psum.copied(f"cos.s{2 * c + b}"))
                sm = cos.sm[:, 2 * b:2 * b + 2]
                V.reciprocal(sm, sm).then_inc(dve.step(), 1)
                dve.eng.wait_ge(*dve.own())
                for t in (2 * b, 2 * b + 1):
                    ins = V.tensor_scalar(cos.PR[:, t], cos.PR[:, t], cos.sm[:, t:t + 1], None, ALU.mult)
                    if t % 2 == 0:
                        ins.then_inc(dve.step(), 1)
                ins.then_inc(dve.flag("cos.probs"), 1)
            between(3)
            between(4)
            for j in (1, 3):
                dve.eng.wait_ge(*psum.made(f"cos.h2{c}.{j}"))
                V.tensor_scalar(cos.H2[:, j], psum.view(f"cos.h2{c}.{j}"), bcol("L1_attn_b2", j), 0.0,
                                ALU.add, ALU.max).then_inc(dve.read(f"cos.h2{c}.{j}"), 1)
            end_sum_dve(dve, "cos", c, "cos.out", XB)
            end_norm_dve(dve, "cos", c)
            between(5)

        def cosine_pool(pool, c):
            pool.eng.wait_ge(sig("cos.ssq"), c + 1)
            G.tensor_tensor(cos.rn.rearrange("p t j -> p (t j)"), cos.ssq.rearrange("p t j -> p (t j)"),
                            minus_half[:, 0:8], ALU.pow).then_inc(pool.flag("cos.pow"), 1)
            add_bias_pool(pool, "cos", "moe0", "L1_attn_b3", (c,))
            norm_rstd(pool, c, "cos")

        class one:
            a = Carve(False)
            a(moe0.WORDS)
            KT = a(NB, SK)
            VV = a(NB, D, parts=64)
            PR = a(4, SK)
            PT = a(CH, parts=64)
            mx, sm = a(4), a(4)

        def one_start_pe(pe):
            v = psum.take(pe, "one.k")
            PE.matmul(v[:, 0:NB * SK], W("L1_xattn_key_matrix"), CT[:].rearrange("p b k -> p (b k)"),
                      start=True, stop=True).then_inc(psum.filled("one.k"), 1)
            v = psum.take(pe, "one.v")
            for b in range(NB):
                ins = PE.matmul(v[0:64, b * D:b * D + D], CT[:, b, :], W("L1_xattn_value_matrix"), start=True, stop=True)
            ins.then_inc(psum.filled("one.v"), 1)

        def one_pe(pe, c, between=nothing):
            if c == 0:
                pe.wait_ge(*psum.copied("one.k"))
            x_t_ready(pe, "cos", c)
            v = psum.take(pe, f"one.s{c}")
            for t in range(4):
                i = 4 * c + t
                ins = PE.matmul(v[:, t * SK:t * SK + SK], XT[:, tile(i)], one.KT[:, i // 2, :], start=True, stop=True)
            ins.then_inc(psum.filled(f"one.s{c}"), 1)
            between(6)
            pe.wait_ge(*psum.copied(f"one.s{c}"))
            v = psum.take(pe, f"one.pT{c}")
            for t in range(4):
                ins = PE.transpose(v[0:64, tile(t)], one.PR[:, t, :], ident[:])
            ins.then_inc(psum.filled(f"one.pT{c}"), 1)
            between(7)
            pe.wait_ge(*psum.copied(f"one.pT{c}"))
            if c == 0:
                pe.wait_ge(*psum.copied("one.v"))
            v = psum.take(pe, f"one.out{c}")
            for t in range(4):
                ins = PE.matmul(v[:, tile(t)], one.PT[:, tile(t)], one.VV[:, (4 * c + t) // 2, :], start=True, stop=True)
            ins.then_inc(psum.filled(f"one.out{c}"), 1)

        def one_start_act(act):
            act.eng.wait_ge(*psum.made("one.k"))
            v = psum.view("one.k")
            A.copy(one.KT.rearrange("p b k -> p (b k)"), v[:, 0:NB * SK]).then_inc(act.read("one.k"), 1)
            act.eng.wait_ge(*psum.made("one.v"))
            v = psum.view("one.v")
            A.copy(one.VV.rearrange("p b k -> p (b k)"), v[0:64, 0:NB * D]).then_inc(act.read("one.v"), 1)

        def one_act(act, c, between=nothing):
            act.eng.wait_ge(*psum.made(f"one.s{c}"))
            v = psum.view(f"one.s{c}")
            act.eng.wait_ge(sig("one.mx"), c + 1)
            for t in range(4):
                ins = A.activation(one.PR[:, t], v[:, t * SK:t * SK + SK], ACT.Exp, bias=one.mx[:, t:t + 1],
                                   scale=D ** -0.5, accum_out=one.sm[:, t:t + 1])
                if t < 3:
                    ins.then_inc(act.step(), 1)
            ins.then_inc(act.read(f"one.s{c}"), 1)
            between(6)
            act.eng.wait_ge(*psum.made(f"one.pT{c}"))
            v = psum.view(f"one.pT{c}")
            A.copy(one.PT, v[0:64]).then_inc(act.read(f"one.pT{c}"), 1)
            between(7)

        def one_dve(dve, c, between=nothing):
            dve.eng.wait_ge(*dve.own())
            dve.eng.wait_ge(*psum.made(f"one.s{c}"))
            v = psum.view(f"one.s{c}")[:, 0:4 * SK].rearrange("p (t k) -> p t k", t=4)
            V.tensor_reduce(one.mx, v, AX.X, ALU.max, negate=True).then_inc(dve.step(), 1)
            dve.eng.wait_ge(*dve.own())
            V.tensor_scalar(one.mx, one.mx, D ** -0.5, None, ALU.mult).then_inc(dve.flag("one.mx"), 1)
            between(6)
            dve.eng.wait_ge(*psum.copied(f"one.s{c}"))
            V.reciprocal(one.sm, one.sm).then_inc(dve.step(), 1)
            between(7)
            dve.eng.wait_ge(*dve.own())
            dve.eng.wait_ge(*psum.made(f"one.out{c}"))
            v = psum.view(f"one.out{c}")
            for t in range(4):
                i = 4 * c + t
                ins = V.scalar_tensor_tensor(R[:, i], v[:, tile(t)], one.sm[:, t:t + 1], X[:, i], ALU.mult, ALU.add)
                if t < 3:
                    ins.then_inc(dve.step(), 1)
            ins.then_inc(dve.read(f"one.out{c}"), 1)
            end_sum_dve(dve, "one", c)
            end_norm_dve(dve, "one", c)

        SORT_STEPS = [(k, d) for k in (2 ** j for j in range(1, S.bit_length())) for d in
                      (k // 2 ** j for j in range(1, k.bit_length()))]

        class spm:
            a = Carve(False)
            QT, KT = a(T), a(T)
            PT = QT.rearrange("p (b k q) -> p b k q", b=2, k=2)
            VV = a(NT, D)
            Z = a(NT, S)
            SA, SB = a(4, S), a(4, S)
            mx, sz, stp, cnt, rk, add_ = a(NT), a(NT), a(NT), a(NT), a(NT), a(NT)
            assert a.at == SPARSE_WORDS

        def sparse_project_pe(pe, c):
            pe.wait_ge(w_loaded[5], 16)
            x_t_ready(pe, "moe1", c)
            for n, w in (("q", "L2_attn_Wq"), ("k", "L2_attn_Wk")):
                v = psum.take(pe, f"spm.{n}{c}")
                PE.matmul(v, W(w), XT[:, chunk(c)], start=True, stop=True).then_inc(psum.filled(f"spm.{n}{c}"), 1)
            v = psum.take(pe, f"spm.v{c}")
            for t in range(4):
                ins = PE.matmul(v[:, tile(t)], XT[:, tile(4 * c + t)], W("L2_attn_Wv"), start=True, stop=True)
            ins.then_inc(psum.filled(f"spm.v{c}"), 1)

        def sparse_scores_pe(pe, c):
            pe.wait_ge(*psum.copied(f"spm.q{c}"))
            pe.wait_ge(*psum.copied(f"spm.k{c}"))
            for b in (2 * c, 2 * c + 1):
                v = psum.take(pe, f"spm.s{b}")
                for t in range(2):
                    ins = PE.matmul(v[:, t * S:t * S + S], spm.QT[:, tile(2 * b + t)], spm.KT[:, b * S:b * S + S],
                                    start=True, stop=True)
                ins.then_inc(psum.filled(f"spm.s{b}"), 1)

        def sparse_values_pe(pe, c):
            for b in (2 * c, 2 * c + 1):
                turn_probs_pe(pe, "spm", spm.Z, b, b, "spm.probs", c + 1)
            v = psum.take(pe, f"spm.out{c}")
            for b in (2 * c, 2 * c + 1):
                pe.wait_ge(*psum.copied(f"spm.pT{b}"))
                for t in range(2):
                    at = tile((b % 2) * 2 + t)
                    for kt in range(2):
                        ins = PE.matmul(v[:, at], spm.PT[:, b % 2, kt, tile(t)], spm.VV[:, 2 * b + kt, :],
                                        start=kt == 0, stop=kt == 1)
            ins.then_inc(psum.filled(f"spm.out{c}"), 1)

        def sparse_project_act(act, c):
            move_act(act, f"spm.q{c}", spm.QT[:, chunk(c)])
            move_act(act, f"spm.k{c}", spm.KT[:, chunk(c)])
            move_act(act, f"spm.v{c}", spm.VV[:, ctiles(c)].rearrange("p t d -> p (t d)"))

        def sparse_shift_act(act, c):
            for b in (2 * c, 2 * c + 1):
                act.eng.wait_ge(*psum.made(f"spm.s{b}"))
                v = psum.view(f"spm.s{b}")
                act.eng.wait_ge(sig("spm.mx"), b + 1)
                for t in range(2):
                    i = 2 * b + t
                    ins = A.activation(spm.Z[:, i], v[:, t * S:t * S + S], ACT.Identity, bias=spm.mx[:, i:i + 1],
                                       scale=D ** -0.5, accum_out=spm.sz[:, i:i + 1])
                    if t == 0:
                        ins.then_inc(act.step(), 1)
                ins.then_inc(act.read(f"spm.s{b}"), 1)

        def sparse_values_act(act, c):
            if c:
                act.eng.wait_ge(*psum.made(f"spm.out{c - 1}"))
            for b in (2 * c, 2 * c + 1):
                move_act(act, f"spm.pT{b}", spm.PT[:, b % 2].rearrange("p a q -> p (a q)"))

        def sparse_max_dve(dve, c):
            for b in (2 * c, 2 * c + 1):
                dve.eng.wait_ge(*psum.made(f"spm.s{b}"))
                v = psum.view(f"spm.s{b}").rearrange("p (t k) -> p t k", t=2)
                mx = spm.mx[:, 2 * b:2 * b + 2]
                V.tensor_reduce(mx, v, AX.X, ALU.max, negate=True).then_inc(dve.step(), 1)
                dve.eng.wait_ge(*dve.own())
                V.tensor_scalar(mx, mx, D ** -0.5, None, ALU.mult).then_inc(dve.flag("spm.mx"), 1)

        def sparse_count_dve(dve, c):
            dve.eng.wait_ge(*psum.copied(f"spm.s{2 * c}"))
            dve.eng.wait_ge(*psum.copied(f"spm.s{2 * c + 1}"))
            stp, cnt, rk, ad = (a[:, ctiles(c)] for a in (spm.stp, spm.cnt, spm.rk, spm.add_))
            V.tensor_scalar(stp, spm.sz[:, ctiles(c)], 1.0, 1.0 / S, ALU.subtract, ALU.mult).then_inc(dve.step(), 1)
            dve.eng.wait_ge(*dve.own())
            for t in range(4 * c, 4 * c + 4):
                V.tensor_scalar(spm.SA[:, t % 4], spm.Z[:, t], spm.stp[:, t:t + 1], None, ALU.is_gt, ALU.add,
                                accum_out=spm.cnt[:, t:t + 1]).then_inc(dve.step(), 1)
            dve.eng.wait_ge(*dve.own())
            V.reciprocal(rk, cnt).then_inc(dve.step(), 1)
            dve.eng.wait_ge(*dve.own())
            V.tensor_tensor(ad, stp, rk, ALU.add).then_inc(dve.step(), 1)

        def sort_dve(dve, c, first, last):
            rows_of = lambda a, w: a.rearrange("p t (n w) -> p (t n) w", w=w)
            for j in range(first, last):
                k, d = SORT_STEPS[j]
                src = (spm.SA, spm.SB)[(j - 1) % 2] if j else spm.Z[:, ctiles(c)]
                mirrored = d == k // 2
                w = k if mirrored else 2 * d
                i, o = rows_of(src, w), rows_of((spm.SA, spm.SB)[j % 2], w)
                partner = slice(k - 1, d - 1, -1) if mirrored else slice(d, 2 * d)
                lo, hi = i[:, :, 0:d], i[:, :, partner]
                dve.eng.wait_ge(*dve.own())
                V.tensor_tensor(o[:, :, 0:d], lo, hi, ALU.max).then_inc(dve.step(), 1)
                V.tensor_tensor(o[:, :, partner], lo, hi, ALU.min).then_inc(dve.step(), 1)

        def sparse_probs_dve(dve, c):
            z, cur, oth = spm.Z[:, ctiles(c)], spm.SB, spm.SA
            assert len(SORT_STEPS) % 2 == 0
            dve.eng.wait_ge(*dve.own())
            for t in range(4):
                V.tensor_tensor_scan(oth[:, t], cur[:, t], zeros[:], 0.0, ALU.add, ALU.add).then_inc(dve.step(), 1)
            dve.eng.wait_ge(*dve.own())
            for t in range(4):
                V.tensor_scalar(oth[:, t], oth[:, t], spm.rk[:, 4 * c + t:4 * c + t + 1],
                                spm.add_[:, 4 * c + t:4 * c + t + 1], ALU.mult, ALU.subtract).then_inc(dve.step(), 1)
            dve.eng.wait_ge(*dve.own())
            V.tensor_tensor(z, z, oth, ALU.subtract).then_inc(dve.step(), 1)
            dve.eng.wait_ge(*dve.own())
            V.tensor_scalar(z, z, 0.0, None, ALU.max).then_inc(dve.flag("spm.probs"), 1)

        EXPERTS_AFTER = {0: (0,), 1: (1,), 2: (2, 3), 3: (4,), 4: (5,), 5: (6, 7)}

        def middle_pe(pe):
            one_start_pe(pe)
            def experts(j):
                if j < 5:
                    moe0.late_round_pe(pe, MAIN_ROUNDS + j)
                if j == 6:
                    end_pe(pe, "moe0", 1)

            cosine_pe(pe, 0, experts)
            one_pe(pe, 0, experts)
            end_pe(pe, "one", 0)
            def experts1(j):
                for e in EXPERTS_AFTER.get(j, ()):
                    moe1.round_pe(pe, e)
                if j == 6:
                    end_pe(pe, "moe1", 0)
                if j == 7:
                    sparse_project_pe(pe, 0)

            moe1.start_chunk_pe(pe, 0)
            cosine_pe(pe, 1, experts1)
            one_pe(pe, 1, experts1)
            sparse_scores_pe(pe, 0)
            end_pe(pe, "one", 1)
            moe1.start_chunk_pe(pe, 1)
            for i in range(8, 16):
                moe1.round_pe(pe, i)
            end_pe(pe, "moe1", 1)
            sparse_project_pe(pe, 1)
            sparse_scores_pe(pe, 1)
            sparse_values_pe(pe, 0)
            end_pe(pe, "spm", 0)
            x2.start_pe(pe)
            x2.chunk_pe(pe, 0)
            sparse_values_pe(pe, 1)
            end_pe(pe, "spm", 1)
            x2.chunk_pe(pe, 1)

        def middle_act(act):
            one_start_act(act)
            def experts(j):
                if j < 5:
                    moe0.late_round_act(act, MAIN_ROUNDS + j)
                if j == 6:
                    end_act(act, "moe0", 1)

            cosine_act(act, 0, experts)
            one_act(act, 0, experts)
            end_act(act, "one", 0)
            def experts1(j):
                for e in EXPERTS_AFTER.get(j, ()):
                    moe1.round_act(act, e)
                if j == 6:
                    end_act(act, "moe1", 0)
                if j == 7:
                    sparse_project_act(act, 0)

            moe1.start_chunk_act(act, 0)
            cosine_act(act, 1, experts1)
            one_act(act, 1, experts1)
            sparse_shift_act(act, 0)
            end_act(act, "one", 1)
            moe1.start_chunk_act(act, 1)
            for i in range(8, 16):
                moe1.round_act(act, i)
            end_act(act, "moe1", 1)
            sparse_project_act(act, 1)
            sparse_shift_act(act, 1)
            sparse_values_act(act, 0)
            end_act(act, "spm", 0)
            x2.chunk_act(act, 0)
            sparse_values_act(act, 1)
            end_act(act, "spm", 1)
            x2.chunk_act(act, 1)

        def middle_dve(dve):
            def experts(j):
                if j < 5:
                    moe0.late_round_dve(dve, MAIN_ROUNDS + j)
                if j == 5:
                    end_sum_dve(dve, "moe0", 1)
                    end_norm_dve(dve, "moe0", 1)

            cosine_dve(dve, 0, experts)
            one_dve(dve, 0, experts)
            def experts1(j):
                for e in EXPERTS_AFTER.get(j, ()):
                    moe1.round_dve(dve, e)
                if j == 5:
                    end_sum_dve(dve, "moe1", 0)
                    end_norm_dve(dve, "moe1", 0)

            moe1.start_chunk_dve(dve, 0)
            cosine_dve(dve, 1, experts1)
            one_dve(dve, 1, experts1)
            sparse_max_dve(dve, 0)
            moe1.start_chunk_dve(dve, 1)
            sparse_count_dve(dve, 0)
            for e in range(8):
                sort_dve(dve, 0, 4 * e, 4 * e + 4)
                moe1.round_dve(dve, 8 + e)
            end_sum_dve(dve, "moe1", 1)
            end_norm_dve(dve, "moe1", 1)
            sort_dve(dve, 0, 32, 36)
            sparse_max_dve(dve, 1)
            sparse_probs_dve(dve, 0)
            sparse_count_dve(dve, 1)
            sort_dve(dve, 1, 0, 5)
            end_sum_dve(dve, "spm", 0, "spm.out", X)
            sort_dve(dve, 1, 5, 7)
            end_norm_dve(dve, "spm", 0)
            sort_dve(dve, 1, 7, 9)
            x2.start_dve(dve)
            x2.chunk_dve(dve, 0, lambda t: sort_dve(dve, 1, 9 + 5 * t, 14 + 5 * t))
            sort_dve(dve, 1, 34, 36)
            sparse_probs_dve(dve, 1)
            end_sum_dve(dve, "spm", 1, "spm.out", X)
            end_norm_dve(dve, "spm", 1)
            x2.chunk_dve(dve, 1)

        def middle_pool(pool):
            cosine_pool(pool, 0)
            norm_rstd(pool, 1, "moe0")
            norm_rstd(pool, 0, "one")
            cosine_pool(pool, 1)
            norm_rstd(pool, 0, "moe1")
            norm_rstd(pool, 1, "one")
            norm_rstd(pool, 1, "moe1")
            norm_rstd(pool, 0, "spm")
            x2.spread_pool(pool, 0)
            x2.spread_pool(pool, 1)
            add_bias_pool(pool, "x2", "spm", "L2_xattn_bo", (0,))
            norm_rstd(pool, 1, "spm")
            add_bias_pool(pool, "x2", "spm", "L2_xattn_bo", (1,))
            x2.spread_pool(pool, 2)
            x2.spread_pool(pool, 3)
            end_pool(pool, "x2")

        class lora:
            a = Carve(True)
            LZ = a(NT, 138)
            ZT = a(T)
            M8, I8, IF = a(NT, 8), a(NT, 8, dt=U32), a(NT, 8)
            G, H2, EL = a(NT, 8), a(NT, 8), a(NT, 8)
            dn, zr = a(NT), a(NT)

        def lora_pe(pe):
            w0 = W_AT["L2_ffn_gate_w"][0]
            for c in range(NC):
                x_t_ready(pe, "x2", c)
                for half in range(2):
                    v = psum.take(pe, f"lora.lz{c}{half}")
                    for t in range(2):
                        ins = PE.matmul(v[:, t * 138:t * 138 + 138], XT[:, tile(4 * c + 2 * half + t)],
                                        WS[:, w0:w0 + 138], start=True, stop=True)
                    ins.then_inc(psum.filled(f"lora.lz{c}{half}"), 1)
            for c in range(NC):
                pe.wait_ge(sig("lora.z"), c + 1)
                turn_pe(pe, "lora.z", lora.LZ[:, :, 10:138], c)
            for c in range(NC):
                pe.wait_ge(*psum.copied(f"lora.zT{c}"))
                v = psum.take(pe, f"lora.out{c}")
                for t in range(4):
                    PE.matmul(v[:, tile(t)], XT[:, tile(4 * c + t)], W("L2_ffn_base_w"), start=True, stop=False)
                    ins = PE.matmul(v[:, tile(t)], lora.ZT[:, tile(4 * c + t)], W("L2_ffn_lora_B"),
                                    start=False, stop=True)
                ins.then_inc(psum.filled(f"lora.out{c}"), 1)
            for c in range(NC):
                end_pe(pe, "lora", c)

        def lora_act(act):
            for c in range(NC):
                act.eng.wait_ge(sig("lora.shifted"), c + 1)
                A.activation(lora.EL[:, ctiles(c)], lora.EL[:, ctiles(c)], ACT.Exp).then_inc(act.flag("lora.exp"), 1)
            for c in range(NC):
                move_act(act, f"lora.zT{c}", lora.ZT[:, chunk(c)])
            for c in range(NC):
                end_act(act, "lora", c)

        def lora_dve(dve):
            for c in range(NC):
                for half in range(2):
                    dve.eng.wait_ge(*psum.made(f"lora.lz{c}{half}"))
                    v = psum.view(f"lora.lz{c}{half}")
                    t = 4 * c + 2 * half
                    V.tensor_copy(lora.LZ[:, t:t + 2], v[:, 0:276].rearrange("p (t n) -> p t n", t=2)).then_inc(dve.read(f"lora.lz{c}{half}"), 1)
                dve.eng.wait_ge(*dve.own())
                for t in range(4 * c, 4 * c + 4):
                    V.max(lora.M8[:, t], lora.LZ[:, t, 0:10]).then_inc(dve.step(), 1)
                dve.eng.wait_ge(*dve.own())
                for t in range(4 * c, 4 * c + 4):
                    V.max_index(lora.I8[:, t], lora.M8[:, t], lora.LZ[:, t, 0:10]).then_inc(dve.step(), 1)
                V.tensor_tensor(lora.EL[:, ctiles(c)], lora.LZ[:, ctiles(c), 0:8],
                                           bc(lora.M8[:, ctiles(c), 0], 2, 8), ALU.subtract).then_inc(dve.flag("lora.shifted"), 1)
                dve.eng.wait_ge(*dve.own())
                V.tensor_copy(lora.IF[:, ctiles(c)], lora.I8[:, ctiles(c)]).then_inc(dve.step(), 1)
            for c in range(NC):
                g, h2, ex = lora.G[:, ctiles(c)], lora.H2[:, ctiles(c)], bc(expert[:], 1, 4)
                dn, zr = lora.dn[:, ctiles(c)], lora.zr[:, ctiles(c)]
                dve.eng.wait_ge(*dve.own())
                V.tensor_tensor(g, ex, bc(lora.IF[:, ctiles(c), 0], 2, 8), ALU.is_equal).then_inc(dve.step(), 1)
                V.tensor_tensor(h2, ex, bc(lora.IF[:, ctiles(c), 1], 2, 8), ALU.is_equal).then_inc(dve.step(), 1)
                dve.eng.wait_ge(*dve.own())
                V.tensor_tensor(g, g, h2, ALU.add).then_inc(dve.step(), 1)
                dve.eng.wait_ge(*dve.own())
                dve.eng.wait_ge(sig("lora.exp"), c + 1)
                V.tensor_tensor(g, g, lora.EL[:, ctiles(c)], ALU.mult).then_inc(dve.step(), 1)
                dve.eng.wait_ge(*dve.own())
                V.tensor_reduce(dn, g, AX.X, ALU.add).then_inc(dve.step(), 1)
                dve.eng.wait_ge(*dve.own())
                V.tensor_scalar(zr, dn, 0.0, None, ALU.is_equal).then_inc(dve.step(), 1)
                dve.eng.wait_ge(*dve.own())
                V.tensor_tensor(dn, dn, zr, ALU.add).then_inc(dve.step(), 1)
                dve.eng.wait_ge(*dve.own())
                V.reciprocal(dn, dn).then_inc(dve.step(), 1)
                dve.eng.wait_ge(*dve.own())
                V.tensor_scalar(dn, dn, 32.0 / 16.0, None, ALU.mult).then_inc(dve.step(), 1)
                dve.eng.wait_ge(*dve.own())
                V.tensor_tensor(g, g, bc(dn, 2, 8), ALU.mult).then_inc(dve.step(), 1)
                dve.eng.wait_ge(*dve.own())
                for t in range(4 * c, 4 * c + 4):
                    z = lora.LZ[:, t, 10:138].rearrange("p (e r) -> p e r", e=8)
                    ins = V.tensor_tensor(z, z, bc(lora.G[:, t], 2, 16), ALU.mult)
                    if t % 4 < 3:
                        ins.then_inc(dve.step(), 1)
                ins.then_inc(dve.flag("lora.z"), 1)
            end_dve(dve, "lora", "lora.out", XB)

        def lora_pool(pool):
            add_bias_pool(pool, "lora", "x2", "L2_ffn_base_b")
            end_pool(pool, "lora")

        GROUPS = NB * 8

        class big:
            a = Carve(False)
            QT = a(3, S)
            KM = a(3, 4, S)
            Q16, K16 = a(2, S, dt=BF16), a(2, 4 * S, dt=BF16)
            VV = a(4, 2, P)
            mx = a(2, 4)
            HL = a(2, 2 * P, dt=BF16)
            E = a(2, 4, 2, S)
            ES = a(2, 4, S)
            rc = a(S)
            OT = a(2, 8, S)
            Y = XB

        def big_pe(pe):
            pe.wait_ge(w_loaded[6], 16)
            wq = W("L3_attn_w_qkv")

            def project(n):
                b, g = divmod(n, 8)
                if n % 16 == 0:
                    pe.wait_ge(*psum.copied(f"lora.xT{b // 2}"))
                v = psum.take(pe, f"big.qk{n}")
                PE.matmul(v[:, 0:S], wq[:, tile(g)], XT[:, b * S:b * S + S], start=True, stop=True)
                PE.matmul(v[:, S:2 * S], wq[:, 1024 + g * P:1024 + g * P + P], XT[:, b * S:b * S + S],
                          start=True, stop=True).then_inc(psum.filled(f"big.qk{n}"), 1)
                v = psum.take(pe, f"big.v{n}")
                for t in range(2):
                    ins = PE.matmul(v[:, tile(t)], XT[:, tile(2 * b + t)], wq[:, 2048 + g * P:2048 + g * P + P],
                                    start=True, stop=True)
                ins.then_inc(psum.filled(f"big.v{n}"), 1)

            def maxima(n):
                pe.wait_ge(sig("big.k16"), n + 1)
                for pair in range(2):
                    v = psum.take(pe, f"big.m{n}.{pair}", 2)
                    for t in range(2):
                        ins = PE.matmul(v[:, t], big.Q16[:, n % 2, tile(t)],
                                        big.K16[:, n % 2, 2 * pair * S:2 * (pair + 1) * S], start=True, stop=True)
                    ins.then_inc(psum.filled(f"big.m{n}.{pair}"), 1)

            def shifts(n):
                pe.wait_ge(sig("big.shift"), n + 1)
                v = psum.take(pe, f"big.hT{n}")
                for t in range(2):
                    ins = PE.transpose(v.bitcast(BF16)[:, tile(t)],
                                       shift_parts[:, n % 2, t].rearrange("p h w -> p (h w)"), ident16[:])
                ins.then_inc(psum.filled(f"big.hT{n}"), 1)

            def scores(n):
                pe.wait_ge(*psum.copied(f"big.hT{n}"))
                for pair in range(2):
                    v = psum.take(pe, f"big.e{n}.{pair}", 2)
                    for hh in range(2):
                        h = 2 * pair + hh
                        PE.matmul(v[:, hh].rearrange("p (a q) -> p a q", a=2), pick[:, h, :],
                                  bc(big.HL[:, n % 2], 1, 2), start=True, stop=True)
                        for kt in range(2):
                            ins = PE.matmul(v[:, hh, kt * S:kt * S + S], big.KM[:, n % 3, h, tile(kt)],
                                            big.QT[:, n % 3, :], start=False, stop=True, skip_group_check=True)
                    ins.then_inc(psum.filled(f"big.e{n}.{pair}"), 1)

            def values(n):
                pe.wait_ge(sig("big.sums"), n + 1)
                pe.wait_ge(*psum.copied(f"big.v{n}"))
                v = psum.take(pe, f"big.o{n}")
                for kt in range(2):
                    for h in range(4):
                        PE.matmul(v[32 * h:32 * h + 32, 0:S], big.VV[:, n % 4, kt, 32 * h:32 * h + 32],
                                  big.E[:, n % 2, h, kt, :], start=kt == 0, stop=kt == 1)
                for h in range(4):
                    ins = PE.matmul(v[32 * h:32 * h + 32, S:2 * S], ones32[:], big.ES[:, n % 2, h, :],
                                    start=True, stop=True)
                ins.then_inc(psum.filled(f"big.o{n}"), 1)

            project(0)
            project(1)
            maxima(0)
            shifts(0)
            for n in range(GROUPS + 1):
                if n + 2 < GROUPS:
                    project(n + 2)
                if n + 1 < GROUPS:
                    maxima(n + 1)
                if n < GROUPS:
                    scores(n)
                if n + 1 < GROUPS:
                    shifts(n + 1)
                if n >= 1:
                    values(n - 1)
                if n >= 9 and n % 8 == 1:
                    big_output_pe(pe, n // 8 - 1)
                if n == 25:
                    end_pe(pe, "big", 0)
            big_output_pe(pe, NB - 1)

        def big_output_pe(pe, b):
            pe.wait_ge(*psum.copied(f"big.o{8 * b + 7}"))
            v = psum.take(pe, f"big.out{b}")
            for t in range(2):
                for g in range(8):
                    ins = PE.matmul(v[:, tile(t)], big.OT[:, b % 2, g, tile(t)], W("L3_attn_w_out")[:, tile(g)],
                                    start=g == 0, stop=g == 7)
            ins.then_inc(psum.filled(f"big.out{b}"), 1)

        def big_act(act):
            def copies(n):
                if n >= 3:
                    act.eng.wait_ge(*psum.made(f"big.e{n - 3}.1"))
                act.eng.wait_ge(*psum.made(f"big.qk{n}"))
                v = psum.view(f"big.qk{n}")
                A.copy(big.QT[:, n % 3], v[:, 0:S]).then_inc(act.step(), 1)
                for h in range(4):
                    ins = A.activation(big.KM[:, n % 3, h], v[:, S:2 * S], ACT.Copy, scale=head_of4[:, h:h + 1])
                    if h < 3:
                        ins.then_inc(act.step(), 1)
                ins.then_inc(act.read(f"big.qk{n}"), 1)
                if n >= 4:
                    act.eng.wait_ge(*psum.made(f"big.o{n - 4}"))
                act.eng.wait_ge(*psum.made(f"big.v{n}"))
                A.copy(big.VV[:, n % 4].rearrange("p a d -> p (a d)"),
                       psum.view(f"big.v{n}")[:, 0:2 * P]).then_inc(act.read(f"big.v{n}"), 1)

            def shift_copy(n):
                if n >= 2:
                    act.eng.wait_ge(*psum.made(f"big.e{n - 2}.1"))
                act.eng.wait_ge(*psum.made(f"big.hT{n}"))
                A.copy(big.HL[:, n % 2], psum.view(f"big.hT{n}").bitcast(BF16)[:, 0:2 * P])\
                    .then_inc(act.read(f"big.hT{n}"), 1)

            copies(0)
            copies(1)
            shift_copy(0)
            for n in range(GROUPS):
                if n + 2 < GROUPS:
                    copies(n + 2)
                for pair in range(2):
                    if n >= 2:
                        act.eng.wait_ge(*psum.made(f"big.o{n - 2}"))
                    act.eng.wait_ge(*psum.made(f"big.e{n}.{pair}"))
                    A.activation(big.E[:, n % 2, 2 * pair:2 * pair + 2].rearrange("p a b q -> p a (b q)"),
                                 psum.view(f"big.e{n}.{pair}"), ACT.Exp,
                                 scale=32 ** -0.5).then_inc(act.read(f"big.e{n}.{pair}"), 1)
                if n + 1 < GROUPS:
                    shift_copy(n + 1)
                if n == 25:
                    end_act(act, "big", 0)

        def big_dve(dve):
            def halves(n):
                if n >= 2:
                    dve.eng.wait_ge(*psum.made(f"big.m{n - 2}.1"))
                dve.eng.wait_ge(*psum.copied(f"big.qk{n}"))
                V.tensor_copy(big.Q16[:, n % 2], big.QT[:, n % 3]).then_inc(dve.step(), 1)
                V.tensor_copy(big.K16[:, n % 2], big.KM[:, n % 3].rearrange("p h k -> p (h k)")).then_inc(dve.flag("big.k16"), 1)

            def maxima(n):
                dve.eng.wait_ge(*dve.own())
                for pair in range(2):
                    dve.eng.wait_ge(*psum.made(f"big.m{n}.{pair}"))
                    v = psum.view(f"big.m{n}.{pair}").rearrange("p t (h k) -> p t h k", h=2)
                    V.tensor_reduce(big.mx[:, :, 2 * pair:2 * pair + 2], v, AX.X, ALU.max,
                                    negate=True).then_inc(dve.read(f"big.m{n}.{pair}"), 1)
                if n >= 2:
                    dve.eng.wait_ge(*psum.made(f"big.hT{n - 2}"))
                dve.eng.wait_ge(*dve.own())
                V.tensor_copy(shift_parts[:, n % 2, :, :, 0], big.mx).then_inc(dve.step(), 1)
                dve.eng.wait_ge(*dve.own())
                V.tensor_tensor(shift_parts[:, n % 2, :, :, 1], big.mx, shift_parts[:, n % 2, :, :, 0],
                                ALU.subtract).then_inc(dve.flag("big.shift"), 1)

            def divide(n):
                b, g = divmod(n, 8)
                dve.eng.wait_ge(*dve.own())
                dve.eng.wait_ge(*psum.made(f"big.o{n}"))
                v = psum.view(f"big.o{n}")
                V.reciprocal(big.rc, v[:, S:2 * S]).then_inc(dve.step(), 1)
                dve.eng.wait_ge(*dve.own())
                V.tensor_tensor(big.OT[:, b % 2, g], v[:, 0:S], big.rc, ALU.mult).then_inc(dve.read(f"big.o{n}"), 1)

            halves(0)
            halves(1)
            maxima(0)
            for n in range(GROUPS + 1):
                if n >= 10 and n % 8 == 2:
                    big_bias_dve(dve, n // 8 - 1)
                if n in (19, 21, 23):
                    big_norm_dve(dve, 0, (n - 19) // 2)
                if n + 1 < GROUPS:
                    maxima(n + 1)
                if n + 2 < GROUPS:
                    halves(n + 2)
                if n >= 1:
                    divide(n - 1)

        def big_bias_dve(dve, b):
            dve.eng.wait_ge(*psum.made(f"big.out{b}"))
            v = psum.view(f"big.out{b}")[:, 0:2 * P].rearrange("p (t d) -> p t d", t=2)
            V.tensor_tensor(R[:, 2 * b:2 * b + 2], v, bc(row("L3_attn_b_out"), 1, 2),
                            ALU.add).then_inc(dve.read(f"big.out{b}"), 1)

        def big_norm_dve(dve, c, part):
            y, r = big.Y[:, ctiles(c)], R[:, ctiles(c)]
            if part == 0:
                norm_stats(dve, c, r, "bign", 1e-6)
            if part == 1:
                norm_apply(dve, c, r, y, "bign")
                dve.eng.wait_ge(*dve.own())
                V.tensor_tensor(y, y, bc(row("L3_attn_ln_gamma"), 1, 4), ALU.mult).then_inc(dve.step(), 1)
                dve.eng.wait_ge(*dve.own())
                V.tensor_tensor(y, y, bc(row("L3_attn_ln_beta"), 1, 4), ALU.add).then_inc(dve.step(), 1)
                dve.eng.wait_ge(*dve.own())
                V.tensor_tensor(r, y, X[:, ctiles(c)], ALU.add).then_inc(dve.step(), 1)
                end_sum_dve(dve, "big", c)
            if part == 2:
                end_norm_dve(dve, "big", c)

        def big_last_sum_dve(dve):
            big_bias_dve(dve, NB - 1)
            big_norm_dve(dve, 1, 0)

        def big_last_norm_dve(dve):
            big_norm_dve(dve, 1, 1)
            big_norm_dve(dve, 1, 2)

        def big_pool(pool):
            for n in range(GROUPS):
                if n >= 2:
                    pool.eng.wait_ge(*psum.made(f"big.o{n - 2}"))
                pool.eng.wait_ge(*psum.copied(f"big.e{n}.1"))
                G.tensor_tensor(big.ES[:, n % 2], big.E[:, n % 2, :, 0], big.E[:, n % 2, :, 1],
                                ALU.add).then_inc(pool.flag("big.sums"), 1)
                if n == 19:
                    norm_rstd(pool, 0, "bign")
                if n == 21:
                    norm_rstd(pool, 0, "big")

        def absmax_dve(dve, c):
            norm_stats(dve, c, X[:, ctiles(c)], "fin", EPS)
            V.tensor_copy(XALL[:, bass.ds(step * NT + 4 * c, 4), :], X[:, ctiles(c)]).then_inc(dve.step(), 1)
            y = R[:, ctiles(c)]
            normed_dve(dve, c, X[:, ctiles(c)], y, "fin")
            dve.eng.wait_ge(*dve.own())
            V.tensor_reduce(ABSMAX[:, bass.ds(step * NT + 4 * c, 4)], y, AX.X, ALU.max,
                            apply_absolute_value=True).then_inc(dve.step(), 1)

        def normed_dve(dve, c, src, y, name):
            norm_apply(dve, c, src, y, name)
            dve.eng.wait_ge(*dve.own())
            V.tensor_tensor(y, y, bc(row("L3_ffn_gamma"), 1, 4), ALU.mult).then_inc(dve.step(), 1)
            dve.eng.wait_ge(*dve.own())
            V.tensor_tensor(y, y, bc(row("L3_ffn_beta"), 1, 4), ALU.add).then_inc(dve.step(), 1)


        NCH = B // 2
        KEPT = NCH - NC

        class last:
            a = Carve(False)
            amax, scale, inv, f = a(1), a(1), a(1), a(1)
            wsum, wtot, delta, ndelta = a(1), a(1), a(1), a(1)
            tern, neg, aw = a(D), a(D), a(D)
            sums, tots = a(2), a(2)
            tern16 = a(D, dt=BF16)
            Q = a(2, 4, D)
            Q16 = a(NCH, 4, D, dt=BF16)
            QT = a(NCH, 4 * P, dt=BF16)
            RR = a(NCH, 4, D)
            OUT = a(NCH, 4, D)

        def last_ffn():
            ROUND = 1.5 * 2.0 ** 23
            RMAX, RADD = bass.bass_isa.ReduceOp.max, bass.bass_isa.ReduceOp.add
            psum.reset()
            with nc.Block(no_gpsimd_drain=True) as block:
                @block.tensor
                def _(pe):
                    for c in range(NCH):
                        pe.wait_ge(sig("last.q"), c + 1)
                        v = psum.take(pe, f"last.qT{c}").bitcast(BF16)
                        for t in range(4):
                            ins = PE.transpose(v[:, tile(t)], last.Q16[:, c, t], ident16[:])
                        ins.then_inc(psum.filled(f"last.qT{c}"), 1)
                    pe.wait_ge(sig("last.tern16"), 1)
                    for c in range(NCH):
                        pe.wait_ge(*psum.copied(f"last.qT{c}"))
                        v = psum.take(pe, f"last.y{c}")
                        for t in range(4):
                            ins = PE.matmul(v[:, tile(t)], last.QT[:, c, tile(t)], last.tern16, start=True, stop=True)
                        ins.then_inc(psum.filled(f"last.y{c}"), 1)

                @block.gpsimd
                def _(eng):
                    pool = Own(eng, pool_step, psum, sig)
                    eng.wait_ge(sig("last.rowmax"), 1)
                    G.partition_all_reduce(last.scale, last.amax, P, RMAX).then_inc(pool.flag("last.max"), 1)
                    eng.wait_ge(sig("last.wrows"), 1)
                    G.partition_all_reduce(last.wtot, last.wsum, P, RADD).then_inc(pool.flag("last.wsum"), 1)
                    eng.wait_ge(sig("last.sums"), 1)
                    G.partition_all_reduce(last.tots, last.sums, P, RADD).then_inc(pool.flag("last.tots"), 1)
                    for c in range(KEPT):
                        norm_rstd(pool, c, "fin")
                    for c in range(NCH):
                        norm_rstd(pool, c, "last")

                @block.vector
                def _(eng):
                    dve = Own(eng, dve_step, psum, sig)
                    w = W("L3_ffn_weight")
                    V.tensor_reduce(last.amax, ABSMAX[:], AX.X, ALU.max).then_inc(dve.flag("last.rowmax"), 1)
                    V.tensor_reduce(last.wsum, w, AX.X, ALU.add, apply_absolute_value=True).then_inc(dve.flag("last.wrows"), 1)
                    eng.wait_ge(sig("last.wsum"), 1)
                    V.tensor_scalar(last.delta, last.wtot, 1.0 / (D * D), 0.7, ALU.mult, ALU.mult).then_inc(dve.step(), 1)
                    dve.eng.wait_ge(*dve.own())
                    V.tensor_scalar(last.ndelta, last.delta, -1.0, None, ALU.mult).then_inc(dve.step(), 1)
                    V.tensor_scalar(last.tern, w, last.delta, None, ALU.is_gt).then_inc(dve.step(), 1)
                    dve.eng.wait_ge(*dve.own())
                    V.tensor_scalar(last.neg, w, last.ndelta, None, ALU.is_lt).then_inc(dve.step(), 1)
                    dve.eng.wait_ge(*dve.own())
                    V.tensor_tensor(last.tern, last.tern, last.neg, ALU.subtract).then_inc(dve.step(), 1)
                    dve.eng.wait_ge(*dve.own())
                    V.tensor_copy(last.tern16, last.tern).then_inc(dve.flag("last.tern16"), 1)
                    V.tensor_tensor(last.aw, last.tern, w, ALU.mult).then_inc(dve.step(), 1)
                    V.tensor_reduce(last.sums[:, 1:2], last.tern, AX.X, ALU.add, apply_absolute_value=True).then_inc(dve.step(), 1)
                    dve.eng.wait_ge(*dve.own())
                    V.tensor_reduce(last.sums[:, 0:1], last.aw, AX.X, ALU.add).then_inc(dve.flag("last.sums"), 1)
                    eng.wait_ge(sig("last.tots"), 1)
                    V.tensor_scalar(last.tots[:, 1:2], last.tots[:, 1:2], 1.0, None, ALU.max).then_inc(dve.step(), 1)
                    eng.wait_ge(sig("last.max"), 1)
                    V.tensor_scalar(last.scale, last.scale, 1e-8, 1.0 / 127, ALU.max, ALU.mult).then_inc(dve.step(), 1)
                    dve.eng.wait_ge(*dve.own())
                    V.reciprocal(last.inv, last.scale).then_inc(dve.step(), 1)
                    V.reciprocal(last.f, last.tots[:, 1:2]).then_inc(dve.step(), 1)
                    dve.eng.wait_ge(*dve.own())
                    V.tensor_tensor(last.f, last.f, last.tots[:, 0:1], ALU.mult).then_inc(dve.step(), 1)
                    dve.eng.wait_ge(*dve.own())
                    V.tensor_tensor(last.f, last.f, last.scale, ALU.mult).then_inc(dve.step(), 1)
                    for c in range(KEPT):
                        norm_stats(dve, c, XALL[:, ctiles(c)], "fin", EPS)
                    for c in range(NCH):
                        if c < KEPT:
                            q = last.Q[:, c % 2]
                            normed_dve(dve, c, XALL[:, ctiles(c)], q, "fin")
                        else:
                            q = R[:, ctiles(c - KEPT)]
                        dve.eng.wait_ge(*dve.own())
                        V.tensor_scalar(q, q, last.inv, 127.0, ALU.mult, ALU.min).then_inc(dve.step(), 1)
                        dve.eng.wait_ge(*dve.own())
                        V.tensor_scalar(q, q, -127.0, ROUND, ALU.max, ALU.add).then_inc(dve.step(), 1)
                        dve.eng.wait_ge(*dve.own())
                        V.tensor_scalar(last.Q16[:, c], q, ROUND, None, ALU.subtract).then_inc(dve.flag("last.q"), 1)
                    for c in range(NCH):
                        eng.wait_ge(*psum.made(f"last.y{c}"))
                        v = psum.view(f"last.y{c}")
                        V.scalar_tensor_tensor(last.RR[:, c].rearrange("p t d -> p (t d)"), v, last.f,
                                                         XALL[:, ctiles(c)].rearrange("p t d -> p (t d)"),
                                                         ALU.mult, ALU.add).then_inc(dve.read(f"last.y{c}"), 1)
                        norm_stats(dve, c, last.RR[:, c], "last", EPS)
                    for c in range(NCH):
                        norm_apply(dve, c, last.RR[:, c], last.OUT[:, c], "last", "last.out")

                @block.scalar
                def _(eng):
                    act = Own(eng, act_step, psum, sig)
                    for c in range(NCH):
                        eng.wait_ge(*psum.made(f"last.qT{c}"))
                        v = psum.view(f"last.qT{c}").bitcast(BF16)
                        A.copy(last.QT[:, c], v[:, 0:4 * P]).then_inc(act.read(f"last.qT{c}"), 1)

                @block.sync
                def _(sp):
                    for c in range(NCH):
                        sp.wait_ge(sig("last.out"), c + 1)
                        sp.dma_start(out[:, ctiles(c), :], last.OUT[:, c]).then_inc(x_stored, 16)
                    sp.wait_ge(x_stored, 16 * NCH)


        def clear_counts():
            counts = sorted(s.num for s in bank_full + bank_read + [pe_step, dve_step, act_step, pool_step, loaded]
                            + list(signals.values()))
            assert counts == list(range(counts[0], counts[-1] + 1))
            nc.sync.sem_clear(range(counts[0], counts[-1] + 1))
            nc.all_engine_barrier(sem_only=True)

        x0 = Cross("x0", "L0_xattn", "ret", True, 0, KEEP0, 0, ends_in_next=True)
        moe1 = Moe("moe1", "L1_ffn", "one", True, 4, 4, 2, 1, False, cos.WORDS)
        x2 = Cross("x2", "L2_xattn", "spm", True, 5, None, 0)
        x3 = Cross("x3", "L3_xattn", "big", True, 6, KEEP3, 1, last=True)

        with nc.Fori(0, STEPS) as step:
            with nc.Block(no_gpsimd_drain=True) as block:
                @block.sync
                def _(sp):
                    sp.dma_start(CT[:], ctx_t[:, bass.ds(step * NB, NB), :]).then_inc(loaded, 16)
                    sp.dma_start(CD[:], ctx_d[:, bass.ds(step * NB, NB), :]).then_inc(loaded, 16)
                    sp.dma_start(KEEP0[:], keep0[bass.ds(step * NB, NB), :].partition_broadcast(P)).then_inc(loaded, 16)
                    sp.dma_start(KEEP3[:], keep3[bass.ds(step * NB, NB), :].partition_broadcast(P)).then_inc(loaded, 16)

                @block.tensor
                def _(eng):
                    retention_pe(eng)
                    x0.pe(eng, retention_last_out_pe)
                    moe0.pe(eng)
                    middle_pe(eng)
                    lora_pe(eng)
                    big_pe(eng)
                    x3.pe(eng)

                @block.scalar
                def _(eng):
                    act = Own(eng, act_step, psum, sig)
                    retention_act(act)
                    x0.act(act)
                    moe0.act(act)
                    middle_act(act)
                    lora_act(act)
                    big_act(act)
                    x3.act(act)

                @block.vector
                def _(eng):
                    dve = Own(eng, dve_step, psum, sig)
                    tokens_dve(eng, dve)
                    retention_dve(dve)
                    x0.dve(dve, lambda: end_sum_dve(dve, "ret", 1, "ret.y.out", X), lambda: end_norm_dve(dve, "ret", 1))
                    moe0.dve(dve, lambda: end_sum_dve(dve, "x0", 1, "x0.o.out", XB), lambda: end_norm_dve(dve, "x0", 1))
                    middle_dve(dve)
                    lora_dve(dve)
                    big_dve(dve)
                    x3.dve(dve, lambda: big_last_sum_dve(dve), lambda: big_last_norm_dve(dve))

                @block.gpsimd
                def _(eng):
                    pool = Own(eng, pool_step, psum, sig)
                    retention_pool(pool)
                    x0.pool(pool, ("ret",))
                    moe0.pool(pool)
                    middle_pool(pool)
                    lora_pool(pool)
                    big_pool(pool)
                    x3.pool(pool, ("bign", "big"))
            clear_counts()

        last_ffn()


def kernel(**inputs):
    import numpy as _np
    import concourse.bacc as _bacc
    from concourse import mybir as _mybir
    from concourse.bass_utils import run_bass_kernel_spmd as _run

    i = {n: _np.asarray(a) for n, a in inputs.items()}
    blocks = lambda w, j: w.reshape(j, 128, -1).transpose(1, 0, 2).reshape(128, -1)
    experts_in = lambda w: w.transpose(1, 0, 2).reshape(128, -1)
    experts_out = lambda w: blocks(w.reshape(-1, 128), w.shape[0] * w.shape[1] // 128)
    turned = {"L0_xattn_Wq", "L0_xattn_Wk", "L0_xattn_Wv", "L0_xattn_Wo", "L1_attn_Wq", "L1_attn_Wk", "L1_attn_Wv",
              "L1_attn_W1", "L1_attn_W2", "L2_attn_Wq", "L2_attn_Wk", "L2_attn_Wv", "L2_ffn_gate_w", "L2_ffn_base_w",
              "L3_xattn_Wq", "L3_xattn_Wk", "L3_xattn_Wv", "L3_xattn_Wo", "L3_ffn_weight"}

    def laid(n):
        w = i[n]
        if n in turned:
            return w.T
        if n in ("L0_ffn_W1", "L1_ffn_W1"):
            return experts_in(w)
        if n in ("L0_ffn_W2", "L1_ffn_W2"):
            return experts_out(w)
        if n == "L1_attn_W3":
            return blocks(w.T, 4)
        if n == "L3_attn_w_out":
            return blocks(w, 8)
        if n == "L2_ffn_lora_A":
            return w.reshape(128, 128).T
        if n == "L2_ffn_lora_B":
            return w.transpose(0, 2, 1).reshape(128, 128)
        return w

    weights = _np.concatenate([laid(n) for cols in W_COLS for n, _ in cols], axis=1)
    bcols = _np.concatenate([i[n].reshape(-1, 128).T for n, _ in B_COLS], axis=1)
    rows = _np.concatenate([i[n].reshape(-1) for n, _ in ROWS])
    ctx_t = i["ctx_1024"].transpose(2, 0, 1)
    arrays = {
        "x": i["x"].reshape(B * S // 128, 128, D).transpose(1, 0, 2),
        "ctx_t": ctx_t,
        "ctx_d": _np.concatenate([ctx_t, ctx_t], axis=2),
        "keep0": i["mask_BxS2_ik0"],
        "keep3": i["mask_BxS2_bf1"].view(_np.uint8),
        "weights": weights, "bcols": bcols, "rows": rows,
        "b2s": _np.stack([i["L0_ffn_b2"], i["L1_ffn_b2"]]),
    }
    nc = _bacc.Bacc("TRN2", target_bir_lowering=False, num_devices=1)
    args = []
    for name in arrays:
        arrays[name] = _np.ascontiguousarray(arrays[name])
        a = arrays[name]
        args.append(nc.dram_tensor(f"in_{name}", a.shape, _mybir.dt.from_np(a.dtype), kind="ExternalInput").ap())
    args.append(nc.dram_tensor("out_0_dram", (P, B * S // P, D), F32, kind="ExternalOutput").ap())
    decoder(nc, *args)
    r = _run(nc, [{f"in_{n}": a for n, a in arrays.items()}], core_ids=[0])
    return r.results[0]["out_0_dram"].transpose(1, 0, 2).reshape(B, S, D)
```
